# Optimizing a Trainium2 kernel written in Bass

```python
import numpy as np
import jax
import jax.numpy as jnp

def _softmax(x, axis=-1):
    return jax.nn.softmax(x, axis=axis)

def _gelu(x):
    return jax.nn.gelu(x, approximate=True)

def _silu(x):
    return jax.nn.silu(x)

def _sigmoid(x):
    return jax.nn.sigmoid(x)

def _layernorm(x, axis=-1, eps=1e-05):
    m = jnp.mean(x, axis=axis, keepdims=True)
    v = jnp.var(x, axis=axis, keepdims=True)
    return (x - m) / jnp.sqrt(v + eps)

def _scatter_add(tgt, idx, src, axis=0):
    return tgt.at[idx].add(src)

def _segment_sum(src, seg, n):
    return jax.ops.segment_sum(src, seg, n)
kernel_name = 'mk_vit_tower_d2_tok_img512_r4_c8d353'

def setup_inputs(seed: int=0):
    np.random.seed(seed)
    _w = jnp.asarray

    def _rec_inputs():
        import jax
        import jax.numpy as jnp
        _rk = jax.random.key(seed)
        x = -0.000147625 + 0.999875 * jax.random.normal(jax.random.fold_in(_rk, 1), (128, 3, 224, 224), jnp.float32)
        return x
    x = _rec_inputs()

    def _L0_tok_setup():
        import jax, jax.numpy as jnp
        import numpy as np
        N_PATCHES = 8
        PATCH = 28
        C = 3
        IN_D = C * PATCH * PATCH
        HID = 128
        SEQ = N_PATCHES * N_PATCHES + 1

        def _positional_embedding(seq_len, dim):
            i = np.arange(seq_len)[:, None].astype(np.float32)
            j = np.arange(dim)[None, :].astype(np.float32)
            ang = i / np.power(100000.0, j / dim)
            pe = np.where(j % 2 == 0, np.sin(ang), np.cos(ang))
            return jnp.asarray(pe, dtype=jnp.float32)
        key = jax.random.key(seed)
        k1, k2, k3, k4 = jax.random.split(key, 4)
        B = 64
        X = jax.random.normal(k1, (B, C, 224, 224), dtype=jnp.float32)
        bound = 1.0 / np.sqrt(IN_D)
        W = jax.random.uniform(k2, (HID, IN_D), minval=-bound, maxval=bound, dtype=jnp.float32)
        b = jax.random.uniform(k3, (HID,), minval=-bound, maxval=bound, dtype=jnp.float32)
        class_token = jax.random.uniform(k4, (1, HID), dtype=jnp.float32)
        pos_embed = _positional_embedding(SEQ, HID)
        return {'X': X, 'W': W, 'b': b, 'class_token': class_token, 'pos_embed': pos_embed}
    _L0_tok_all = _L0_tok_setup()
    _L0_tok_in = {k: v for k, v in _L0_tok_all.items() if k in ('W', 'b', 'class_token', 'pos_embed')}
    del _L0_tok_all

    def _L0_attn_setup():
        import jax, jax.numpy as jnp
        import numpy as np
        B, T, C = (4, 1024, 128)

        def _rope_tables(T, C):
            pos = jnp.arange(T - 1, -1, -1, dtype=jnp.float32)
            dim = jnp.arange(C // 2, dtype=jnp.float32)
            angle = pos[:, None] * dim[None, :]
            return (jnp.cos(angle), jnp.sin(angle))

        def _rotate(z, cos, sin):
            Bz, Tz, Cz = z.shape
            zp = z.reshape(Bz, Tz, Cz // 2, 2)
            z0, z1 = (zp[..., 0], zp[..., 1])
            r0 = cos * z0 - sin * z1
            r1 = sin * z0 + cos * z1
            return jnp.stack([r0, r1], axis=-1).reshape(Bz, Tz, Cz)
        key = jax.random.key(seed)
        ks = jax.random.split(key, 9)
        s = 0.02
        inp = {'x': jax.random.normal(ks[0], (B, T, C), dtype=jnp.float32), 'Wk': jax.random.normal(ks[1], (C, C), dtype=jnp.float32) * s, 'bk': jax.random.normal(ks[2], (C,), dtype=jnp.float32) * s, 'Wq': jax.random.normal(ks[3], (C, C), dtype=jnp.float32) * s, 'bq': jax.random.normal(ks[4], (C,), dtype=jnp.float32) * s, 'Wv': jax.random.normal(ks[5], (C, C), dtype=jnp.float32) * s, 'bv': jax.random.normal(ks[6], (C,), dtype=jnp.float32) * s, 'Wp': jax.random.normal(ks[7], (C, C), dtype=jnp.float32) * s, 'bp': jax.random.normal(ks[8], (C,), dtype=jnp.float32) * s}
        return inp
    _L0_attn_all = _L0_attn_setup()
    _L0_attn_in = {k: v for k, v in _L0_attn_all.items() if k in ('Wk', 'bk', 'Wq', 'bq', 'Wv', 'bv', 'Wp', 'bp')}
    del _L0_attn_all

    def _L0_ffn_setup():
        import jax, jax.numpy as jnp
        import numpy as np
        D, H, E, B, S = (128, 512, 16, 8, 2048)
        MAX_GROUP_SIZE = 1024
        MIN_CAPACITY = 8
        CAPACITY_FACTOR = 1.0

        def _group_dims(num_tokens, num_experts):
            num_groups = -(-num_tokens // MAX_GROUP_SIZE)
            while num_tokens % num_groups != 0 or num_groups % num_experts != 0:
                num_groups += 1
            return (num_tokens // num_groups, num_groups)
        key = jax.random.key(seed)
        ks = jax.random.split(key, 6)
        s = 0.02
        return {'x': jax.random.normal(ks[0], (B, S, D), jnp.float32), 'gate_w': jax.random.normal(ks[1], (D, E), jnp.float32) * s, 'w1': jax.random.normal(ks[2], (E, D, H), jnp.float32) * s, 'b1': jnp.zeros((E, H), jnp.float32), 'w2': jax.random.normal(ks[3], (E, H, D), jnp.float32) * s, 'b2': jnp.zeros((E, D), jnp.float32), 'sw1': jax.random.normal(ks[4], (D, H), jnp.float32) * s, 'sb1': jnp.zeros((H,), jnp.float32), 'sw2': jax.random.normal(ks[5], (H, D), jnp.float32) * s, 'sb2': jnp.zeros((D,), jnp.float32)}
    _L0_ffn_all = _L0_ffn_setup()
    _L0_ffn_in = {k: v for k, v in _L0_ffn_all.items() if k in ('gate_w', 'w1', 'b1', 'w2', 'b2', 'sw1', 'sb1', 'sw2', 'sb2')}
    del _L0_ffn_all

    def _L1_attn_setup():
        import jax, jax.numpy as jnp
        import numpy as np
        B, T, D = (8, 512, 128)
        DK = 128
        FENETRES = (24, 168, 180)
        EPS = 1e-05
        key = jax.random.key(seed)
        ks = jax.random.split(key, 8)
        s = 0.02
        return {'x': jax.random.normal(ks[0], (B, T, D), dtype=jnp.float32), 'Wq': jax.random.normal(ks[1], (D, DK), dtype=jnp.float32) * s, 'bq': jnp.zeros((DK,), dtype=jnp.float32), 'Wk': jax.random.normal(ks[2], (D, DK), dtype=jnp.float32) * s, 'bk': jnp.zeros((DK,), dtype=jnp.float32), 'Wo': jax.random.normal(ks[3], (D, D), dtype=jnp.float32) * s, 'bo': jnp.zeros((D,), dtype=jnp.float32), 'gamma': jnp.ones((D,), dtype=jnp.float32), 'beta': jnp.zeros((D,), dtype=jnp.float32)}
    _L1_attn_all = _L1_attn_setup()
    _L1_attn_in = {k: v for k, v in _L1_attn_all.items() if k in ('Wq', 'bq', 'Wk', 'bk', 'Wo', 'bo', 'gamma', 'beta')}
    del _L1_attn_all

    def _L1_ffn_setup():
        import jax, jax.numpy as jnp
        import numpy as np
        B, S, D, O = (1, 512, 128, 128)
        H, QD, K, PK = (8, 64, 16, 64)
        N = PK * PK
        HALF = QD // 2

        def _l2norm(x):
            n = jnp.sqrt(jnp.sum(x * x, axis=-1, keepdims=True))
            return x / jnp.maximum(n, 1e-12)
        key = jax.random.key(seed)
        ks = jax.random.split(key, 9)
        return {'hidden_states': jax.random.normal(ks[0], (B, S, D), jnp.float32), 'Wq': jax.random.normal(ks[1], (H * QD, D), jnp.float32) * 0.02, 'bq': jnp.zeros((H * QD,), jnp.float32), 'ln_g': jnp.ones((QD,), jnp.float32), 'ln_b': jnp.zeros((QD,), jnp.float32), 'keys0': jax.random.normal(ks[2], (PK, HALF), jnp.float32) * 0.02, 'keys1': jax.random.normal(ks[3], (PK, HALF), jnp.float32) * 0.02, 'expert_down': jax.random.normal(ks[4], (N, D), jnp.float32) * 0.02, 'expert_up': jax.random.normal(ks[5], (N, O), jnp.float32) * 0.02}
    _L1_ffn_all = _L1_ffn_setup()
    _L1_ffn_in = {k: v for k, v in _L1_ffn_all.items() if k in ('Wq', 'bq', 'ln_g', 'ln_b', 'keys0', 'keys1', 'expert_down', 'expert_up')}
    del _L1_ffn_all
    return {'x': x, 'L0_tok_W': _L0_tok_in['W'], 'L0_tok_b': _L0_tok_in['b'], 'L0_tok_class_token': _L0_tok_in['class_token'], 'L0_tok_pos_embed': _L0_tok_in['pos_embed'], 'L0_attn_Wk': _L0_attn_in['Wk'], 'L0_attn_bk': _L0_attn_in['bk'], 'L0_attn_Wq': _L0_attn_in['Wq'], 'L0_attn_bq': _L0_attn_in['bq'], 'L0_attn_Wv': _L0_attn_in['Wv'], 'L0_attn_bv': _L0_attn_in['bv'], 'L0_attn_Wp': _L0_attn_in['Wp'], 'L0_attn_bp': _L0_attn_in['bp'], 'L0_ffn_gate_w': _L0_ffn_in['gate_w'], 'L0_ffn_w1': _L0_ffn_in['w1'], 'L0_ffn_b1': _L0_ffn_in['b1'], 'L0_ffn_w2': _L0_ffn_in['w2'], 'L0_ffn_b2': _L0_ffn_in['b2'], 'L0_ffn_sw1': _L0_ffn_in['sw1'], 'L0_ffn_sb1': _L0_ffn_in['sb1'], 'L0_ffn_sw2': _L0_ffn_in['sw2'], 'L0_ffn_sb2': _L0_ffn_in['sb2'], 'L1_attn_Wq': _L1_attn_in['Wq'], 'L1_attn_bq': _L1_attn_in['bq'], 'L1_attn_Wk': _L1_attn_in['Wk'], 'L1_attn_bk': _L1_attn_in['bk'], 'L1_attn_Wo': _L1_attn_in['Wo'], 'L1_attn_bo': _L1_attn_in['bo'], 'L1_attn_gamma': _L1_attn_in['gamma'], 'L1_attn_beta': _L1_attn_in['beta'], 'L1_ffn_Wq': _L1_ffn_in['Wq'], 'L1_ffn_bq': _L1_ffn_in['bq'], 'L1_ffn_ln_g': _L1_ffn_in['ln_g'], 'L1_ffn_ln_b': _L1_ffn_in['ln_b'], 'L1_ffn_keys0': _L1_ffn_in['keys0'], 'L1_ffn_keys1': _L1_ffn_in['keys1'], 'L1_ffn_expert_down': _L1_ffn_in['expert_down'], 'L1_ffn_expert_up': _L1_ffn_in['expert_up']}

def reference(x, L0_tok_W, L0_tok_b, L0_tok_class_token, L0_tok_pos_embed, L0_attn_Wk, L0_attn_bk, L0_attn_Wq, L0_attn_bq, L0_attn_Wv, L0_attn_bv, L0_attn_Wp, L0_attn_bp, L0_ffn_gate_w, L0_ffn_w1, L0_ffn_b1, L0_ffn_w2, L0_ffn_b2, L0_ffn_sw1, L0_ffn_sb1, L0_ffn_sw2, L0_ffn_sb2, L1_attn_Wq, L1_attn_bq, L1_attn_Wk, L1_attn_bk, L1_attn_Wo, L1_attn_bo, L1_attn_gamma, L1_attn_beta, L1_ffn_Wq, L1_ffn_bq, L1_ffn_ln_g, L1_ffn_ln_b, L1_ffn_keys0, L1_ffn_keys1, L1_ffn_expert_down, L1_ffn_expert_up):
    import jax
    import jax.numpy as jnp

    def _L0_tok_ref(X, W, b, class_token, pos_embed):
        import jax, jax.numpy as jnp
        import numpy as np
        N_PATCHES = 8
        PATCH = 28
        C = 3
        IN_D = C * PATCH * PATCH
        HID = 128
        SEQ = N_PATCHES * N_PATCHES + 1

        def _positional_embedding(seq_len, dim):
            i = np.arange(seq_len)[:, None].astype(np.float32)
            j = np.arange(dim)[None, :].astype(np.float32)
            ang = i / np.power(100000.0, j / dim)
            pe = np.where(j % 2 == 0, np.sin(ang), np.cos(ang))
            return jnp.asarray(pe, dtype=jnp.float32)
        B = X.shape[0]
        patches = X.reshape(B, C, N_PATCHES, PATCH, N_PATCHES, PATCH)
        patches = patches.transpose(0, 2, 4, 1, 3, 5).reshape(B, N_PATCHES * N_PATCHES, IN_D)
        tokens = jnp.einsum('bpi,hi->bph', patches, W) + b
        cls = jnp.broadcast_to(class_token[None, :, :], (B, 1, HID))
        tokens = jnp.concatenate([cls, tokens], axis=1)
        return tokens * pos_embed[None, :, :]

    def _L0_attn_ref(x, Wk, bk, Wq, bq, Wv, bv, Wp, bp):
        import jax, jax.numpy as jnp
        import numpy as np
        B, T, C = (4, 1024, 128)

        def _rope_tables(T, C):
            pos = jnp.arange(T - 1, -1, -1, dtype=jnp.float32)
            dim = jnp.arange(C // 2, dtype=jnp.float32)
            angle = pos[:, None] * dim[None, :]
            return (jnp.cos(angle), jnp.sin(angle))

        def _rotate(z, cos, sin):
            Bz, Tz, Cz = z.shape
            zp = z.reshape(Bz, Tz, Cz // 2, 2)
            z0, z1 = (zp[..., 0], zp[..., 1])
            r0 = cos * z0 - sin * z1
            r1 = sin * z0 + cos * z1
            return jnp.stack([r0, r1], axis=-1).reshape(Bz, Tz, Cz)
        Bx, Tx, Cx = x.shape
        k = x @ Wk + bk
        q = x @ Wq + bq
        v = x @ Wv + bv
        cos, sin = _rope_tables(Tx, Cx)
        k = _rotate(k, cos, sin)
        q = _rotate(q, cos, sin)
        wei = jnp.einsum('btc,bsc->bts', k, q) * Cx ** (-0.5)
        mask = jnp.tril(jnp.ones((Tx, Tx), dtype=bool))
        wei = jnp.where(mask, wei, -jnp.inf)
        wei = jax.nn.softplus(wei)
        out = wei @ v
        out = out @ Wp + bp
        return out

    def _L0_ffn_ref(x, gate_w, w1, b1, w2, b2, sw1, sb1, sw2, sb2):
        import jax, jax.numpy as jnp
        import numpy as np
        D, H, E, B, S = (128, 512, 16, 8, 2048)
        MAX_GROUP_SIZE = 1024
        MIN_CAPACITY = 8
        CAPACITY_FACTOR = 1.0

        def _group_dims(num_tokens, num_experts):
            num_groups = -(-num_tokens // MAX_GROUP_SIZE)
            while num_tokens % num_groups != 0 or num_groups % num_experts != 0:
                num_groups += 1
            return (num_tokens // num_groups, num_groups)
        Bn, Sn, Dn = x.shape
        En = gate_w.shape[1]
        T = Bn * Sn
        group_size, num_groups = _group_dims(T, En)
        cap = max(int(round(CAPACITY_FACTOR * group_size * num_groups / En)), MIN_CAPACITY)
        xg = x.reshape(num_groups, group_size, Dn)
        logits = jnp.einsum('gsd,de->gse', xg, gate_w)
        probs = jax.nn.softmax(logits, axis=-1)
        flat_probs = probs.transpose(2, 0, 1).reshape(En, T)
        scores, tok_idx = jax.lax.top_k(flat_probs, cap)
        xf = x.reshape(T, Dn)
        toks = xf[tok_idx]
        h = jax.nn.gelu(jnp.einsum('ecd,edh->ech', toks, w1) + b1[:, None, :])
        y = jnp.einsum('ech,ehd->ecd', h, w2) + b2[:, None, :]
        y = y * scores[..., None]
        routed = jnp.zeros_like(xf).at[tok_idx.reshape(-1)].add(y.reshape(-1, Dn))
        shared = jax.nn.gelu(xf @ sw1 + sb1) @ sw2 + sb2
        out = (routed + shared).reshape(Bn, Sn, Dn)
        return out

    def _L1_attn_ref(x, Wq, bq, Wk, bk, Wo, bo, gamma, beta):
        import jax, jax.numpy as jnp
        import numpy as np
        B, T, D = (8, 512, 128)
        DK = 128
        FENETRES = (24, 168, 180)
        EPS = 1e-05
        q = x @ Wq + bq
        k = x @ Wk + bk
        dk = q.shape[-1]
        scores = jnp.einsum('btd,bsd->bts', q, k) / jnp.sqrt(jnp.float32(dk))
        t = jnp.arange(x.shape[1])
        dist = jnp.abs(t[:, None] - t[None, :])
        acc = jnp.zeros_like(x)
        for w in FENETRES:
            band = dist <= w // 2
            s = jnp.where(band[None, :, :], scores, jnp.float32(-1000000000.0))
            attn = jax.nn.softmax(s, axis=-1)
            acc = acc + jnp.einsum('bts,bsd->btd', attn, x)
        acc = acc / jnp.float32(len(FENETRES))
        out = acc @ Wo + bo
        res = x + out
        mu = jnp.mean(res, axis=-1, keepdims=True)
        var = jnp.mean(jnp.square(res - mu), axis=-1, keepdims=True)
        return (res - mu) * jax.lax.rsqrt(var + EPS) * gamma + beta

    def _L1_ffn_ref(hidden_states, Wq, bq, ln_g, ln_b, keys0, keys1, expert_down, expert_up):
        import jax, jax.numpy as jnp
        import numpy as np
        B, S, D, O = (1, 512, 128, 128)
        H, QD, K, PK = (8, 64, 16, 64)
        N = PK * PK
        HALF = QD // 2

        def _l2norm(x):
            n = jnp.sqrt(jnp.sum(x * x, axis=-1, keepdims=True))
            return x / jnp.maximum(n, 1e-12)
        b, s, d = hidden_states.shape
        q = (hidden_states @ Wq.T + bq).reshape(b, s, H, QD)
        mu = jnp.mean(q, axis=-1, keepdims=True)
        var = jnp.mean((q - mu) ** 2, axis=-1, keepdims=True)
        q = (q - mu) / jnp.sqrt(var + 1e-05) * ln_g + ln_b
        q0, q1 = (q[..., :HALF], q[..., HALF:])
        s0 = jnp.einsum('bshq,eq->bshe', _l2norm(q0), _l2norm(keys0))
        s1 = jnp.einsum('bshq,eq->bshe', _l2norm(q1), _l2norm(keys1))
        sc0, ix0 = jax.lax.top_k(s0, K)
        sc1, ix1 = jax.lax.top_k(s1, K)
        cs = (sc0[..., :, None] + sc1[..., None, :]).reshape(b, s, H, K * K)
        ci = (ix0[..., :, None] + ix1[..., None, :]).reshape(b, s, H, K * K)
        fs, pos = jax.lax.top_k(cs, K)
        fi = jnp.take_along_axis(ci, pos, axis=-1)
        w = jax.nn.softmax(fs, axis=-1)
        down = expert_down[fi]
        up = expert_up[fi]
        inner = jnp.einsum('bsd,bshkd->bshk', hidden_states, down)
        act = jax.nn.gelu(inner, approximate=False)
        out = jnp.einsum('bshk,bshko->bso', act * w, up)
        return out
    h = _L0_tok_ref(x, L0_tok_W, L0_tok_b, L0_tok_class_token, L0_tok_pos_embed)
    h = h + _L0_attn_ref(_layernorm(h, axis=-1), L0_attn_Wk, L0_attn_bk, L0_attn_Wq, L0_attn_bq, L0_attn_Wv, L0_attn_bv, L0_attn_Wp, L0_attn_bp)
    h = h + _L0_ffn_ref(_layernorm(h, axis=-1), L0_ffn_gate_w, L0_ffn_w1, L0_ffn_b1, L0_ffn_w2, L0_ffn_b2, L0_ffn_sw1, L0_ffn_sb1, L0_ffn_sw2, L0_ffn_sb2)
    h = h + _L1_attn_ref(_layernorm(h, axis=-1), L1_attn_Wq, L1_attn_bq, L1_attn_Wk, L1_attn_bk, L1_attn_Wo, L1_attn_bo, L1_attn_gamma, L1_attn_beta)
    h = h + _L1_ffn_ref(_layernorm(h, axis=-1), L1_ffn_Wq, L1_ffn_bq, L1_ffn_ln_g, L1_ffn_ln_b, L1_ffn_keys0, L1_ffn_keys1, L1_ffn_expert_down, L1_ffn_expert_up)
    return h

_drawn_inputs = setup_inputs


def setup_inputs(seed=0):
    import zlib

    import numpy as np

    out = dict(_drawn_inputs(seed))
    spreads = {'L0_ffn_b1': (0.0, 0.8),
     'L0_ffn_b2': (0.0, 0.41),
     'L0_ffn_sb1': (0.0, 0.1),
     'L0_ffn_sb2': (0.0, 0.1),
     'L1_attn_bq': (0.0, 0.8),
     'L1_attn_bk': (0.0, 0.8),
     'L1_attn_bo': (0.0, 0.1),
     'L1_attn_gamma': (1.0, 0.2),
     'L1_attn_beta': (0.0, 0.1),
     'L1_ffn_bq': (0.0, 0.8),
     'L1_ffn_ln_g': (1.0, 0.6),
     'L1_ffn_ln_b': (0.0, 0.8)}
    factors = {'L0_attn_Wk': 3.724,
     'L0_attn_bk': 8.0,
     'L0_attn_Wq': 3.721,
     'L0_attn_bq': 8.0,
     'L0_ffn_w1': 5.463,
     'L0_ffn_w2': 4.955,
     'L1_attn_Wq': 8.0,
     'L1_attn_Wk': 8.0,
     'L1_ffn_Wq': 8.0,
     'L1_ffn_keys0': 8.0,
     'L1_ffn_keys1': 8.0,
     'L1_ffn_expert_down': 8.0,
     'L1_ffn_expert_up': 8.0}
    for name, (base, spread) in spreads.items():
        noise = np.random.default_rng([zlib.crc32(name.encode()), seed]).standard_normal(out[name].shape)
        drawn = base * np.exp(spread * noise) if base else spread * noise
        out[name] = jnp.asarray(drawn.astype(out[name].dtype))
    for name, factor in factors.items():
        out[name] = (out[name] * factor).astype(out[name].dtype)
    return out
```

```python
import numpy as np
import concourse.bass as bass
from concourse import mybir
from contextlib import ExitStack

F32 = mybir.dt.float32
BF16 = mybir.dt.bfloat16
I32 = mybir.dt.int32
U32 = mybir.dt.uint32
ALU = mybir.AluOpType
ACT = mybir.ActivationFunctionType
AX = mybir.AxisListType
D, B, T, P = 128, 128, 65, 128
N = B * T
GB = 4
STEPS = B // GB
W = GB * T
EPS = 1e-5


class Steps:

    def __init__(self, eng, sem, base=0):
        self.eng, self.sem, self.base, self.n = eng, sem, base, 0

    def mark(self, ins):
        self.n += 1
        ins.then_inc(self.sem, 1)

    def wait(self):
        self.eng.wait_ge(self.sem, self.base + self.n)

    def link(self, ins):
        self.mark(ins)
        self.wait()


def embed(nc, d, dst):
    NB = 8
    BLOCKS = B // NB
    TOK = T - 1
    KC, REST = 18, 48
    with ExitStack() as ctx:
        def sb(name, shape, dt=F32):
            return ctx.enter_context(nc.sbuf_tensor("em_" + name, shape, dt))

        def sem(name):
            return ctx.enter_context(nc.semaphore("em_" + name))
        w = sb("w", [P, KC, D])
        w_rest = sb("w_rest", [REST, D])
        bias = sb("bias", [D, 1])
        pos = sb("pos", [D, T])
        cls = sb("cls", [D, 1])
        ident = sb("ident", [P, P])
        x = sb("x", [P, 2, KC, 512])
        x_rest = sb("x_rest", [REST, 2, 512])
        tokT = sb("tokT", [D, NB, T])
        tok = sb("tok", [T, NB, D])
        ps = ctx.enter_context(nc.psum_tensor("em_ps", [P, 8, 512], F32))
        consts_in = sem("consts_in")
        x_in = [sem(f"x_in{k}") for k in range(2)]
        acc_done = sem("acc_done"); tokT_ready = sem("tokT_ready"); tok_T = sem("tok_T"); tok_ready = sem("tok_ready")
        cls_ready = sem("cls_ready"); stored = sem("stored")
        rows = dst.rearrange("(b t) c -> t b c", t=T)
        with nc.Block() as block:
            @block.sync
            def _(sp):
                for to, name in ((w, "w_tok"), (w_rest, "w_tok_rest"), (bias, "b_tok"), (pos, "pos_cols"), (cls, "cls_col"),
                                 (ident, "ident")):
                    sp.dma_start(to[:], d[name]).then_inc(consts_in, 16)
                with sp.Fori(0, BLOCKS // 2) as g:
                    for k in range(2):
                        sp.wait_ge(acc_done, 2 * g)
                        sp.dma_start(x[:, k], d["x_main"][bass.ds(2 * g + k, 1)].rearrange("g p k t -> (g p) k t")).then_inc(x_in[k], 16)
                        sp.dma_start(x_rest[:, k], d["x_rest"][bass.ds(2 * g + k, 1)].rearrange("g p t -> (g p) t")).then_inc(x_in[k], 16)

            @block.gpsimd
            def _(pool):
                with pool.Fori(0, BLOCKS) as g:
                    pool.wait_ge(tok_ready, g + 1)
                    pool.dma_start(rows[:, bass.ds(g * NB, NB), :], tok[:, :, :]).then_inc(stored, 16)
                pool.wait_ge(stored, 16 * BLOCKS)

            @block.tensor
            def _(pe):
                pe.wait_ge(consts_in, 96)
                with pe.Fori(0, BLOCKS // 2) as g:
                    for k in range(2):
                        pe.wait_ge(x_in[k], 32 * g + 32)
                        pe.wait_ge(tokT_ready, 2 * g + k)
                        for c in range(KC):
                            nc.tensor.matmul(ps[:, k, :], w[:, c, :], x[:, k, c, :], start=(c == 0), stop=False)
                        nc.tensor.matmul(ps[:, k, :], w_rest[:, :], x_rest[:, k, :], start=False, stop=True).then_inc(acc_done, 1)
                        pe.wait_ge(tokT_ready, 2 * g + k + 1)
                        pe.wait_ge(tok_ready, 2 * g + k)
                        for b in range(NB):
                            last = nc.tensor.transpose(ps[0:T, 2 + b // 4, (b % 4) * D:(b % 4 + 1) * D], tokT[:, b, :], ident[:, :])
                        last.then_inc(tok_T, 1)

            @block.scalar
            def _(a):
                with a.Fori(0, BLOCKS) as g:
                    a.wait_ge(tok_T, g + 1)
                    a.wait_ge(stored, 16 * g)
                    for k in range(2):
                        last = nc.scalar.activation(tok[:, 4 * k:4 * k + 4, :].rearrange("p w c -> p (w c)"),
                                                    ps[0:T, 2 + k, :], ACT.Copy)
                    last.then_inc(tok_ready, 1)

            @block.vector
            def _(v):
                v.wait_ge(consts_in, 96)
                nc.vector.tensor_scalar(tokT[:, :, 0:1], pos[:, 0:1].unsqueeze(1).to_broadcast([D, NB, 1]), cls[:, 0:1], None,
                                        ALU.mult).then_inc(cls_ready, 1)
                with v.Fori(0, BLOCKS // 2) as g:
                    for k in range(2):
                        v.wait_ge(acc_done, 2 * g + k + 1)
                        v.wait_ge(tok_T, 2 * g + k)
                        nc.vector.scalar_tensor_tensor(tokT[:, :, 1:T], ps[:, k, :].rearrange("p (b t) -> p b t", t=TOK), bias[:, 0:1],
                                                       pos[:, 1:T].unsqueeze(1).to_broadcast([D, NB, TOK]),
                                                       ALU.add, ALU.mult).then_inc(tokT_ready, 1)


def norm_stats(nc, v, st, gate, x, stats, mv, xn, var_ready):
    g = x.shape[1]
    st.mark(nc.vector.memset(gate, 0.0))
    for j in range(g):
        last = nc.vector.bn_stats(stats[:, j, :], x[:, j, :])
    st.link(last)
    st.mark(nc.vector.memset(gate, 0.0))
    for j in range(g):
        last = nc.vector.bn_aggr(mv[:, j, :], stats[:, j, :])
    st.link(last)
    nc.vector.tensor_scalar(mv[:, :, 1], mv[:, :, 1], EPS, None, ALU.add).then_inc(var_ready, 1)
    for j in range(g):
        last = nc.vector.tensor_scalar(xn[:, j, :], x[:, j, :], mv[:, j, 0:1], None, ALU.subtract)
    st.link(last)


def attend0(nc, d, src, dst, table, probs, xfT):
    E = 16
    with ExitStack() as ctx:
        def sb(name, shape, dt=F32):
            return ctx.enter_context(nc.sbuf_tensor("a0_" + name, shape, dt))

        def sem(name):
            return ctx.enter_context(nc.semaphore("a0_" + name))
        wkq = sb("wkq", [D, 4, D])
        bkq = sb("bkq", [D, 4])
        wvT = sb("wvT", [D, D]); wp = sb("wp", [D, D]); bv = sb("bv", [D, T]); bp = sb("bp", [T, D])
        wvp = sb("wvp", [D, D]); bvp = sb("bvp", [T, D])
        gate_w = sb("gate_w", [D, E])
        cos = sb("cos", [D, T]); sin = sb("sin", [D, T]); tri = sb("tri", [T, T])
        ident = sb("ident", [P, P])
        x = sb("x", [T, GB, D]); xn = sb("xn", [T, GB, D]); stats = sb("stats", [T, GB, 6]); mv = sb("mv", [T, GB, 2])
        ln = sb("ln", [T, GB]); rstd = sb("rstd", [T, GB]); gate = sb("gate", [T, 1])
        xT = sb("xT", [D, W])
        r1 = sb("r1", [D, W]); r2 = sb("r2", [D, W])
        kT = sb("kT", [D, W]); qT = sb("qT", [D, W]); vv = sb("vv", [T, GB, D])
        ab = sb("ab", [T, W]); pw = sb("pw", [T, W]); wei = sb("wei", [T, W])
        h = sb("h", [T, GB, D])
        xf = sb("xf", [T, GB, D + E]); xfTs = sb("xfTs", [D, W])
        lm = sb("lm", [T, GB]); le = sb("le", [T, GB, E])
        ps = ctx.enter_context(nc.psum_tensor("a0_ps", [P, 8, 512], F32))
        names = ("consts_in folded step x_in var rstd normed x_T x_Tc kq v kq_rot sc sp_abs sp_exp sp_ln wei_ready out h_ready "
                 "xf_ready xf_T xf_Tc logits l_sub l_exp table_ready stored act_step").split()
        s = {n: sem(n) for n in names}
        xr = src.rearrange("(b t) c -> t b c", t=T)
        hr = dst.rearrange("(b t) c -> t b c", t=T)
        tr = table.rearrange("(b t) c -> t b c", t=T)
        pr = probs.rearrange("(b t) c -> t b c", t=T)
        bat = lambda ap: ap.rearrange("p (g t) -> p g t", g=GB)
        with nc.Block() as block:
            @block.sync
            def _(sp):
                for to, name in ((wkq, "w_kq"), (bkq, "b_kq"), (wvT, "wvT"), (wp, "wp"), (bv, "bv_cols"), (bp, "bp_rows"),
                                 (gate_w, "gate_w"), (cos, "cos"), (sin, "sin"), (tri, "tri"), (ident, "ident")):
                    sp.dma_start(to[:], d[name]).then_inc(s["consts_in"], 16)
                with sp.Fori(0, STEPS) as i:
                    sp.wait_ge(s["h_ready"], i)
                    sp.dma_start(x[:, :, :], xr[:, bass.ds(i * GB, GB), :]).then_inc(s["x_in"], 16)
                    sp.wait_ge(s["h_ready"], i + 1)
                    sp.dma_start(hr[:, bass.ds(i * GB, GB), :], h[:, :, :]).then_inc(s["stored"], 16)
                    sp.wait_ge(s["xf_Tc"], i + 1)
                    sp.dma_start(xfT[:, bass.ds(i * W, W)], xfTs[:, :]).then_inc(s["stored"], 16)
                    sp.wait_ge(s["table_ready"], i + 1)
                    sp.dma_start(tr[:, bass.ds(i * GB, GB), :], xf[:, :, :]).then_inc(s["stored"], 16)
                    sp.dma_start(pr[:, bass.ds(i * GB, GB), :], xf[:, :, D:D + E]).then_inc(s["stored"], 16)
                sp.wait_ge(s["stored"], 64 * STEPS)

            @block.tensor
            def _(pe):
                pe.wait_ge(s["consts_in"], 176)
                nc.tensor.matmul(ps[:, 0, 0:D], wvT[:, :], wp[:, :], start=True, stop=True)
                nc.tensor.matmul(ps[0:T, 1, 0:D], bv[:, :], wp[:, :], start=True, stop=True).then_inc(s["folded"], 1)
                pe.wait_ge(s["act_step"], 2)
                with pe.Fori(0, STEPS) as i:
                    pe.wait_ge(s["normed"], i + 1)
                    for g in range(GB):
                        last = nc.tensor.transpose(ps[:, 0, g * T:(g + 1) * T], xn[:, g, :], ident[0:T, 0:T])
                    last.then_inc(s["x_T"], 1)
                    pe.wait_ge(s["x_Tc"], i + 1)
                    for j in range(4):
                        last = nc.tensor.matmul(ps[:, 1 + j, 0:W], wkq[:, j, :], xT[:, :], start=True, stop=True)
                    last.then_inc(s["kq"], 1)
                    for g in range(GB):
                        last = nc.tensor.matmul(ps[0:T, 5, g * D:(g + 1) * D], xT[:, g * T:(g + 1) * T], wvp[:, :],
                                                start=True, stop=True)
                    last.then_inc(s["v"], 1)
                    pe.wait_ge(s["kq_rot"], i + 1)
                    for g in range(GB):
                        c = slice(g * T, (g + 1) * T)
                        last = nc.tensor.matmul(ps[0:T, 6, c], qT[:, c], kT[:, c], start=True, stop=True)
                    last.then_inc(s["sc"], 1)
                    pe.wait_ge(s["wei_ready"], i + 1)
                    for g in range(GB):
                        last = nc.tensor.matmul(ps[0:T, 7, g * D:(g + 1) * D], wei[:, g * T:(g + 1) * T], vv[:, g, :],
                                                start=True, stop=True)
                    last.then_inc(s["out"], 1)
                    pe.wait_ge(s["xf_ready"], i + 1)
                    for g in range(GB):
                        last = nc.tensor.transpose(ps[:, 0, g * T:(g + 1) * T], xf[:, g, 0:D], ident[0:T, 0:T])
                    last.then_inc(s["xf_T"], 1)
                    pe.wait_ge(s["xf_Tc"], i + 1)
                    for g in range(GB):
                        last = nc.tensor.matmul(ps[0:T, 6, g * E:(g + 1) * E], xfTs[:, g * T:(g + 1) * T], gate_w[:, :],
                                                start=True, stop=True)
                    last.then_inc(s["logits"], 1)

            @block.scalar
            def _(a):
                nc.scalar.preload_act_table_set("natural_log_exp_and_others")
                a.wait_ge(s["folded"], 1)
                nc.scalar.activation(wvp[:, :], ps[:, 0, 0:D], ACT.Copy).then_inc(s["act_step"], 1)
                nc.scalar.activation(bvp[:, :], ps[0:T, 1, 0:D], ACT.Copy).then_inc(s["act_step"], 1)
                PER = 4
                with a.Fori(0, STEPS) as i:
                    st = Steps(a, s["act_step"], PER * i + 2)

                    def rsqrt(k):
                        a.wait_ge(s["var"], 2 * i + k)
                        st.link(nc.scalar.activation(ln[:, :], mv[:, :, 1], ACT.Ln))
                        nc.scalar.activation(rstd[:, :], ln[:, :], ACT.Exp, scale=-0.5).then_inc(s["rstd"], 1)
                    rsqrt(1)
                    a.wait_ge(s["x_T"], i + 1)
                    nc.scalar.activation(xT[:, :], ps[:, 0, 0:W], ACT.Copy).then_inc(s["x_Tc"], 1)
                    a.wait_ge(s["sc"], i + 1)
                    nc.scalar.activation(pw[:, :], ps[0:T, 6, 0:W], ACT.Relu, scale=D ** -0.5)
                    st.link(nc.scalar.activation(ab[:, :], ps[0:T, 6, 0:W], ACT.Abs, scale=D ** -0.5))
                    st.link(nc.scalar.activation(ab[:, :], ab[:, :], ACT.Exp, scale=-1.0))
                    nc.scalar.activation(ab[:, :], ab[:, :], ACT.Ln, bias=1.0).then_inc(s["sp_ln"], 1)
                    rsqrt(2)
                    a.wait_ge(s["xf_T"], i + 1)
                    a.wait_ge(s["stored"], 64 * i)
                    nc.scalar.activation(xfTs[:, :], ps[:, 0, 0:W], ACT.Copy).then_inc(s["xf_Tc"], 1)
                    a.wait_ge(s["l_sub"], i + 1)
                    nc.scalar.activation(le[:, :, :], le[:, :, :], ACT.Exp).then_inc(s["l_exp"], 1)
                    assert st.n == PER

            @block.vector
            def _(v):
                v.wait_ge(s["consts_in"], 176)
                v.wait_ge(s["act_step"], 2)
                PER = 19
                with v.Fori(0, STEPS) as i:
                    st = Steps(v, s["step"], PER * i)
                    v.wait_ge(s["x_in"], 16 * i + 16)
                    norm_stats(nc, v, st, gate[:, :], x, stats, mv, xn, s["var"])
                    v.wait_ge(s["rstd"], 2 * i + 1)
                    for g in range(GB):
                        last = nc.vector.tensor_scalar(xn[:, g, :], xn[:, g, :], rstd[:, g:g + 1], None, ALU.mult)
                    last.then_inc(s["normed"], 1)
                    v.wait_ge(s["kq"], i + 1)
                    for j, to in ((0, kT), (2, qT)):
                        nc.vector.scalar_tensor_tensor(bat(r1[:, :]), bat(ps[:, 1 + j, 0:W]), bkq[:, j:j + 1],
                                                       cos[:, :].unsqueeze(1).to_broadcast([D, GB, T]), ALU.add, ALU.mult)
                        st.link(nc.vector.scalar_tensor_tensor(bat(r2[:, :]), bat(ps[:, 2 + j, 0:W]), bkq[:, j + 1:j + 2],
                                                               sin[:, :].unsqueeze(1).to_broadcast([D, GB, T]), ALU.add, ALU.mult))
                        last = nc.vector.tensor_tensor(to[:, :], r1[:, :], r2[:, :], ALU.add)
                        if j == 0:
                            st.link(last)
                    last.then_inc(s["kq_rot"], 1)
                    v.wait_ge(s["v"], i + 1)
                    st.mark(nc.vector.tensor_tensor(vv[:, :, :], ps[0:T, 5, :].rearrange("p (g c) -> p g c", g=GB),
                                            bvp[:, :].unsqueeze(1).to_broadcast([T, GB, D]), ALU.add))
                    v.wait_ge(s["sp_ln"], i + 1)
                    st.link(nc.vector.tensor_tensor(pw[:, :], pw[:, :], ab[:, :], ALU.add))
                    nc.vector.tensor_tensor(bat(wei[:, :]), bat(pw[:, :]), tri[:, :].unsqueeze(1).to_broadcast([T, GB, T]),
                                            ALU.mult).then_inc(s["wei_ready"], 1)
                    v.wait_ge(s["stored"], 64 * i)
                    st.link(nc.vector.tensor_tensor(x[:, :, :], x[:, :, :], bp[:, :].unsqueeze(1).to_broadcast([T, GB, D]), ALU.add))
                    v.wait_ge(s["out"], i + 1)
                    last = nc.vector.tensor_tensor(h[:, :, :], ps[0:T, 7, :].rearrange("p (g c) -> p g c", g=GB), x[:, :, :], ALU.add)
                    last.then_inc(s["h_ready"], 1)
                    v.wait_ge(s["h_ready"], i + 1)
                    norm_stats(nc, v, st, gate[:, :], h, stats, mv, xn, s["var"])
                    v.wait_ge(s["rstd"], 2 * i + 2)
                    for g in range(GB):
                        last = nc.vector.tensor_scalar(xf[:, g, 0:D], xn[:, g, :], rstd[:, g:g + 1], None, ALU.mult)
                    last.then_inc(s["xf_ready"], 1)
                    v.wait_ge(s["logits"], i + 1)
                    lg = ps[0:T, 6, 0:GB * E].rearrange("p (g e) -> p g e", g=GB)
                    st.link(nc.vector.tensor_reduce(lm[:, :], lg, AX.X, ALU.max))
                    nc.vector.tensor_tensor(le[:, :, :], lg, lm[:, :].unsqueeze(2).to_broadcast([T, GB, E]),
                                            ALU.subtract).then_inc(s["l_sub"], 1)
                    v.wait_ge(s["l_exp"], i + 1)
                    st.link(nc.vector.tensor_reduce(lm[:, :], le[:, :, :], AX.X, ALU.add))
                    st.link(nc.vector.reciprocal(lm[:, :], lm[:, :]))
                    nc.vector.tensor_tensor(xf[:, :, D:D + E], le[:, :, :], lm[:, :].unsqueeze(2).to_broadcast([T, GB, E]),
                                            ALU.mult).then_inc(s["table_ready"], 1)
                    assert st.n == PER, st.n


def attend1(nc, d, src, dst):
    with ExitStack() as ctx:
        def sb(name, shape, dt=F32):
            return ctx.enter_context(nc.sbuf_tensor("a1_" + name, shape, dt))
        s = {n: ctx.enter_context(nc.semaphore("a1_" + n)) for n in
             ("consts_in step x_in var rstd normed x_T x_Tc qk qk_c u u_c sc e_in e_out A A_T A_Tc out h_ready stored act_step").split()}
        wq = sb("wq", [D, D]); wk = sb("wk", [D, D]); wo = sb("wo", [D, D]); bqk = sb("bqk", [D, 2])
        rows = sb("rows", [T, 3, D])
        band = sb("band", [T, T]); off = sb("off", [T, T])
        ident = sb("ident", [P, P])
        x = sb("x", [T, GB, D]); xn = sb("xn", [T, GB, D]); stats = sb("stats", [T, GB, 6]); mv = sb("mv", [T, GB, 2])
        ln = sb("ln", [T, GB]); rstd = sb("rstd", [T, GB]); gate = sb("gate", [T, 1])
        xT = sb("xT", [D, W]); qT = sb("qT", [D, W]); kT = sb("kT", [D, W]); u = sb("u", [T, GB, D])
        sc = sb("sc", [T, 2, GB, T]); ex = sb("ex", [T, 2, GB, T]); m = sb("m", [T, 2, GB]); A = sb("A", [T, GB, T])
        AT = sb("AT", [T, W]); res = sb("res", [T, GB, D]); h = sb("h", [T, GB, D])
        ps = ctx.enter_context(nc.psum_tensor("a1_ps", [P, 8, 512], F32))
        xr = src.rearrange("(b t) c -> t b c", t=T)
        hr = dst.rearrange("(b t) c -> t b c", t=T)
        with nc.Block() as block:
            @block.sync
            def _(sp):
                for to, name in ((wq, "wq1"), (wk, "wk1"), (wo, "wo1"), (bqk, "b_qk1"), (rows, "rows1"), (band, "band"),
                                 (off, "off_band"), (ident, "ident")):
                    sp.dma_start(to[:], d[name]).then_inc(s["consts_in"], 16)
                with sp.Fori(0, STEPS) as i:
                    sp.wait_ge(s["h_ready"], i)
                    sp.dma_start(x[:, :, :], xr[:, bass.ds(i * GB, GB), :]).then_inc(s["x_in"], 16)
                    sp.wait_ge(s["h_ready"], i + 1)
                    sp.dma_start(hr[:, bass.ds(i * GB, GB), :], h[:, :, :]).then_inc(s["stored"], 16)
                sp.wait_ge(s["stored"], 16 * STEPS)

            @block.tensor
            def _(pe):
                pe.wait_ge(s["consts_in"], 128)
                with pe.Fori(0, STEPS) as i:
                    pe.wait_ge(s["normed"], i + 1)
                    for g in range(GB):
                        last = nc.tensor.transpose(ps[:, 0, g * T:(g + 1) * T], xn[:, g, :], ident[0:T, 0:T])
                    last.then_inc(s["x_T"], 1)
                    pe.wait_ge(s["x_Tc"], i + 1)
                    nc.tensor.matmul(ps[:, 1, 0:W], wq[:, :], xT[:, :], start=True, stop=True)
                    nc.tensor.matmul(ps[:, 2, 0:W], wk[:, :], xT[:, :], start=True, stop=True).then_inc(s["qk"], 1)
                    for g in range(GB):
                        last = nc.tensor.matmul(ps[0:T, 3, g * D:(g + 1) * D], xT[:, g * T:(g + 1) * T], wo[:, :],
                                                start=True, stop=True)
                    last.then_inc(s["u"], 1)
                    pe.wait_ge(s["qk_c"], i + 1)
                    for g in range(GB):
                        c = slice(g * T, (g + 1) * T)
                        last = nc.tensor.matmul(ps[0:T, 4, c], qT[:, c], kT[:, c], start=True, stop=True)
                    last.then_inc(s["sc"], 1)
                    pe.wait_ge(s["A"], i + 1)
                    for g in range(GB):
                        last = nc.tensor.transpose(ps[0:T, 5, g * T:(g + 1) * T], A[:, g, :], ident[0:T, 0:T])
                    last.then_inc(s["A_T"], 1)
                    pe.wait_ge(s["A_Tc"], i + 1)
                    for g in range(GB):
                        last = nc.tensor.matmul(ps[0:T, 6, g * D:(g + 1) * D], AT[:, g * T:(g + 1) * T], u[:, g, :],
                                                start=True, stop=True)
                    last.then_inc(s["out"], 1)

            @block.scalar
            def _(a):
                nc.scalar.preload_act_table_set("natural_log_exp_and_others")
                a.wait_ge(s["consts_in"], 128)
                with a.Fori(0, STEPS) as i:
                    def rsqrt(k):
                        a.wait_ge(s["var"], 2 * i + k)
                        nc.scalar.activation(ln[:, :], mv[:, :, 1], ACT.Ln).then_inc(s["act_step"], 1)
                        a.wait_ge(s["act_step"], 2 * i + k)
                        nc.scalar.activation(rstd[:, :], ln[:, :], ACT.Exp, scale=-0.5).then_inc(s["rstd"], 1)
                    rsqrt(1)
                    a.wait_ge(s["x_T"], i + 1)
                    nc.scalar.activation(xT[:, :], ps[:, 0, 0:W], ACT.Copy).then_inc(s["x_Tc"], 1)
                    a.wait_ge(s["qk"], i + 1)
                    nc.scalar.activation(qT[:, :], ps[:, 1, 0:W], ACT.Identity, bias=bqk[:, 0:1])
                    nc.scalar.activation(kT[:, :], ps[:, 2, 0:W], ACT.Identity, bias=bqk[:, 1:2]).then_inc(s["qk_c"], 1)
                    a.wait_ge(s["u"], i + 1)
                    nc.scalar.activation(u[:, :, :].rearrange("p g c -> p (g c)"), ps[0:T, 3, :], ACT.Copy)
                    a.wait_ge(s["e_in"], i + 1)
                    nc.scalar.activation(ex[:, :, :, :], sc[:, :, :, :], ACT.Exp).then_inc(s["e_out"], 1)
                    a.wait_ge(s["A_T"], i + 1)
                    nc.scalar.activation(AT[:, :], ps[0:T, 5, 0:W], ACT.Copy).then_inc(s["A_Tc"], 1)
                    rsqrt(2)

            @block.vector
            def _(v):
                v.wait_ge(s["consts_in"], 128)
                PER = 23
                with v.Fori(0, STEPS) as i:
                    st = Steps(v, s["step"], PER * i)
                    gt = lambda ap: ap.unsqueeze(1).to_broadcast([T, GB, T])
                    gd = lambda ap: ap.unsqueeze(1).to_broadcast([T, GB, D])
                    v.wait_ge(s["x_in"], 16 * i + 16)
                    norm_stats(nc, v, st, gate[:, :], x, stats, mv, xn, s["var"])
                    v.wait_ge(s["rstd"], 2 * i + 1)
                    for g in range(GB):
                        last = nc.vector.tensor_scalar(xn[:, g, :], xn[:, g, :], rstd[:, g:g + 1], None, ALU.mult)
                    last.then_inc(s["normed"], 1)
                    v.wait_ge(s["sc"], i + 1)
                    st.link(nc.vector.tensor_scalar(sc[:, 0].rearrange("p g t -> p (g t)"), ps[0:T, 4, 0:W], D ** -0.5, None, ALU.mult))
                    st.link(nc.vector.tensor_tensor(sc[:, 1], sc[:, 0], gt(band[:, :]), ALU.mult))
                    st.link(nc.vector.tensor_tensor(sc[:, 1], sc[:, 1], gt(off[:, :]), ALU.add))
                    st.link(nc.vector.tensor_reduce(m[:, :, :], sc[:, :, :, :], AX.X, ALU.max))
                    for w_ in range(2):
                        last = nc.vector.tensor_tensor(sc[:, w_], sc[:, w_], m[:, w_, :].unsqueeze(2).to_broadcast([T, GB, T]), ALU.subtract)
                    last.then_inc(s["e_in"], 1)
                    v.wait_ge(s["e_out"], i + 1)
                    st.link(nc.vector.tensor_reduce(m[:, :, :], ex[:, :, :, :], AX.X, ALU.add))
                    st.link(nc.vector.reciprocal(m[:, :, :], m[:, :, :]))
                    nc.vector.tensor_scalar(m[:, 0, :], m[:, 0, :], 2.0 / 3.0, None, ALU.mult)
                    st.link(nc.vector.tensor_scalar(m[:, 1, :], m[:, 1, :], 1.0 / 3.0, None, ALU.mult))
                    for w_ in range(2):
                        last = nc.vector.tensor_tensor(ex[:, w_], ex[:, w_], m[:, w_, :].unsqueeze(2).to_broadcast([T, GB, T]), ALU.mult)
                    st.link(last)
                    nc.vector.tensor_tensor(A[:, :, :], ex[:, 0], ex[:, 1], ALU.add).then_inc(s["A"], 1)
                    st.link(nc.vector.tensor_tensor(xn[:, :, :], xn[:, :, :], gd(rows[:, 0, :]), ALU.add))
                    v.wait_ge(s["out"], i + 1)
                    st.link(nc.vector.tensor_tensor(res[:, :, :], ps[0:T, 6, :].rearrange("p (g c) -> p g c", g=GB), xn[:, :, :], ALU.add))
                    norm_stats(nc, v, st, gate[:, :], res, stats, mv, xn, s["var"])
                    v.wait_ge(s["rstd"], 2 * i + 2)
                    for g in range(GB):
                        last = nc.vector.tensor_scalar(xn[:, g, :], xn[:, g, :], rstd[:, g:g + 1], None, ALU.mult)
                    st.link(last)
                    st.link(nc.vector.tensor_tensor(xn[:, :, :], xn[:, :, :], gd(rows[:, 1, :]), ALU.mult))
                    st.link(nc.vector.tensor_tensor(xn[:, :, :], xn[:, :, :], gd(rows[:, 2, :]), ALU.add))
                    v.wait_ge(s["stored"], 16 * i)
                    nc.vector.tensor_tensor(h[:, :, :], xn[:, :, :], x[:, :, :], ALU.add).then_inc(s["h_ready"], 1)
                    assert st.n == PER, st.n


def attention_layout(i):
    c_ = np.ascontiguousarray
    W_ = i['L0_tok_W']
    pos = i['L0_tok_pos_embed']
    xp = i['x'].reshape(16, 8, 3, 8, 28, 8, 28).transpose(0, 2, 4, 6, 1, 3, 5).reshape(16, 2352, 512)
    sw = np.arange(128) ^ 1
    t = np.arange(T - 1, -1, -1)[None, :]
    ang = (t * (np.arange(128)[:, None] // 2)).astype(np.float64)
    sg = np.where(np.arange(128) % 2 == 0, -1.0, 1.0)[:, None]
    Wk, Wq, bk, bq = i['L0_attn_Wk'], i['L0_attn_Wq'], i['L0_attn_bk'], i['L0_attn_bq']
    tt = np.arange(T)
    band = (abs(tt[:, None] - tt[None, :]) <= 12).astype(np.float32)
    return dict(
        w_tok=c_(W_.T[:18 * 128].reshape(18, 128, 128).transpose(1, 0, 2)), w_tok_rest=c_(W_.T[18 * 128:]),
        b_tok=c_(i['L0_tok_b'][:, None]), pos_cols=c_(pos.T), cls_col=c_(i['L0_tok_class_token'].T),
        x_main=c_(xp[:, :18 * 128].reshape(16, 18, 128, 512).transpose(0, 2, 1, 3)), x_rest=c_(xp[:, 18 * 128:]),
        ident=np.eye(128, dtype=np.float32),
        w_kq=c_(np.stack([Wk, Wk[:, sw], Wq, Wq[:, sw]], 1)), b_kq=c_(np.stack([bk, bk[sw], bq, bq[sw]], 1)),
        wvT=c_(i['L0_attn_Wv'].T), wp=c_(i['L0_attn_Wp']), bv_cols=c_(np.broadcast_to(i['L0_attn_bv'][:, None], (128, T))),
        bp_rows=c_(np.broadcast_to(i['L0_attn_bp'], (T, 128))), gate_w=c_(i['L0_ffn_gate_w']),
        cos=np.cos(ang).astype(np.float32), sin=(sg * np.sin(ang)).astype(np.float32), tri=np.triu(np.ones((T, T), np.float32)),
        wq1=c_(i['L1_attn_Wq']), wk1=c_(i['L1_attn_Wk']), wo1=c_(i['L1_attn_Wo']), b_qk1=c_(np.stack([i['L1_attn_bq'], i['L1_attn_bk']], 1)),
        rows1=c_(np.broadcast_to(np.stack([i['L1_attn_bo'], i['L1_attn_gamma'], i['L1_attn_beta']]), (T, 3, 128))),
        band=band, off_band=((band - 1) * np.float32(1e9)).astype(np.float32))


E_ = 16
TILES = N // P
CAP = N // E_
CC, CP = 5, 104
HID = 512
PARTS = [(0, 5), (5, 5), (10, 6)]


def route(nc, d, probs, lists, cap=CAP):
    with ExitStack() as ctx:
        def sb(name, shape, dt=F32):
            return ctx.enter_context(nc.sbuf_tensor("rt_" + name, shape, dt))
        s = {n: ctx.enter_context(nc.semaphore("rt_" + n)) for n in
             "consts_in p_in step cnt total masks eq_sums sel sel_sums hots list_mm list_read stored".split()}
        A3 = lambda n, dt=F32: sb(n, [P, E_, TILES], dt)
        raw = sb("raw", [P, TILES, E_])
        pr = A3("pr"); gt = A3("gt"); eq = A3("eq"); tot = A3("tot"); rank = A3("rank"); off = A3("off"); hi = A3("hi")
        lo_b = A3("lo_b", BF16); hi_b = A3("hi_b", BF16)
        carry = sb("carry", [P, E_ * TILES])
        ones = sb("ones", [P, P]); below = sb("below", [P, P])
        iota_lo = sb("iota_lo", [P, CP], BF16); iota_f = sb("iota_f", [P, CP]); tile_no = sb("tile_no", [P, TILES]); pid = sb("pid", [P, 1])
        thr = sb("thr", [P, E_]); cand = sb("cand", [P, E_]); kept = sb("kept", [P, E_]); bit = sb("bit", [P, E_], I32)
        cnt = sb("cnt", [P, E_]); need = sb("need", [P, E_])
        hot_lo = sb("hot_lo", [P, 2, TILES, CP], BF16)
        hot_hi = sb("hot_hi", [P, 2, TILES, CC], BF16)
        ids = sb("ids", [P, 2, TILES, 2 * CC], BF16)
        lf = sb("lf", [CP, E_, CC]); lt = sb("lt", [CP, CC])
        lists_sb = sb("lists", [CP, E_, CC], U32)
        ps = ctx.enter_context(nc.psum_tensor("rt_ps", [P, 8, 512], F32))
        flat = lambda t: t[:, :, :].rearrange("p e t -> p (e t)")
        eb = lambda t: t[:, :].unsqueeze(2).to_broadcast([P, E_, TILES])
        bank = lambda k, n: ps[:, k, 0:n * TILES].rearrange("p (e t) -> p e t", t=TILES)
        with nc.Block() as block:
            @block.sync
            def _(sp):
                for to, name in ((ones, "ones"), (below, "below"), (iota_f, "iota_lo"), (tile_no, "tile_no"), (pid, "pid"),
                                 (carry, "carry"), (bit, "first_bit")):
                    sp.dma_start(to[:], d[name]).then_inc(s["consts_in"], 16)
                sp.dma_start(raw[:, :, :], probs.rearrange("(t p) e -> p t e", p=P)).then_inc(s["p_in"], 16)
                sp.wait_ge(s["list_read"], E_)
                sp.dma_start(lists, lists_sb[:, :, :]).then_inc(s["stored"], 16)
                sp.wait_ge(s["stored"], 16)

            @block.tensor
            def _(pe):
                pe.wait_ge(s["consts_in"], 112)
                with pe.Fori(0, 31) as i:
                    pe.wait_ge(s["cnt"], i + 1)
                    nc.tensor.matmul(ps[:, 6, 0:E_], ones[:, :], cnt[:, :], start=True, stop=True).then_inc(s["total"], 1)

                def sums(m):
                    for k, (e0, n) in enumerate(PARTS):
                        c = m[:, e0:e0 + n, :].rearrange("p e t -> p (e t)")
                        nc.tensor.matmul(ps[:, k, 0:n * TILES], below[:, :], c, start=True, stop=True)
                        last = nc.tensor.matmul(ps[:, 3 + k, 0:n * TILES], ones[:, :], c, start=True, stop=True)
                    return last
                sums(eq).then_inc(s["eq_sums"], 1)
                pe.wait_ge(s["sel"], 1)
                sums(gt).then_inc(s["sel_sums"], 1)
                with pe.Fori(0, E_ // 2) as j:
                    for k in range(2):
                        pe.wait_ge(s["hots"], 2 * j + k + 1)
                        pe.wait_ge(s["list_read"], 2 * j + k)
                        for t in range(TILES):
                            last = nc.tensor.matmul(ps[0:CP, 7, 0:2 * CC], hot_lo[:, k, t, :], ids[:, k, t, :],
                                                    start=(t == 0), stop=(t == TILES - 1))
                        last.then_inc(s["list_mm"], 1)

            @block.vector
            def _(v):
                v.wait_ge(s["consts_in"], 112)
                v.wait_ge(s["p_in"], 16)
                one = Steps(v, s["step"])
                one.mark(nc.vector.memset(thr[:, :], 0.0))
                nc.vector.tensor_copy(iota_lo[:, :], iota_f[:, :])
                one.link(nc.vector.tensor_copy(pr[:, :, :], raw[:, :, :].rearrange("p t e -> p e t")))
                PER = 5
                base = one.n
                with v.Fori(0, 30) as i:
                    st = Steps(v, s["step"], PER * i + base)
                    st.link(nc.vector.tensor_tensor(cand[:, :].bitcast(I32), thr[:, :].bitcast(I32), bit[:, :], ALU.bitwise_or))
                    st.mark(nc.vector.tensor_scalar(bit[:, :], bit[:, :], 1, None, ALU.logical_shift_right))
                    st.link(nc.vector.tensor_tensor(gt[:, :, :], pr[:, :, :], eb(cand), ALU.is_ge))
                    nc.vector.tensor_reduce(cnt[:, :], gt[:, :, :], AX.X, ALU.add).then_inc(s["cnt"], 1)
                    v.wait_ge(s["total"], i + 1)
                    st.link(nc.vector.scalar_tensor_tensor(kept[:, :], ps[:, 6, 0:E_], cap - 0.5, cand[:, :], ALU.is_gt, ALU.mult))
                    st.link(nc.vector.tensor_tensor(thr[:, :], thr[:, :], kept[:, :], ALU.max))
                    assert st.n == PER
                st = Steps(v, s["step"], PER * 30 + base)
                st.mark(nc.vector.tensor_tensor(eq[:, :, :], pr[:, :, :], eb(thr), ALU.is_equal))
                st.link(nc.vector.tensor_tensor(gt[:, :, :], pr[:, :, :], eb(thr), ALU.is_gt))
                nc.vector.tensor_reduce(cnt[:, :], gt[:, :, :], AX.X, ALU.add).then_inc(s["cnt"], 1)
                v.wait_ge(s["total"], 31)
                st.link(nc.vector.tensor_scalar(need[:, :], ps[:, 6, 0:E_], -1.0, float(cap), ALU.mult, ALU.add))

                def ranks():
                    for k, (e0, n) in enumerate(PARTS):
                        last = nc.vector.tensor_copy(tot[:, e0:e0 + n, :], bank(3 + k, n))
                    st.link(last)
                    st.link(nc.vector.tensor_tensor_scan(flat(off), carry[:, :], flat(tot), 0.0, ALU.mult, ALU.add))
                    st.link(nc.vector.tensor_tensor(off[:, :, :], off[:, :, :], tot[:, :, :], ALU.subtract))
                    for k, (e0, n) in enumerate(PARTS):
                        last = nc.vector.tensor_tensor(rank[:, e0:e0 + n, :], bank(k, n), off[:, e0:e0 + n, :], ALU.add)
                    st.link(last)
                v.wait_ge(s["eq_sums"], 1)
                ranks()
                st.link(nc.vector.tensor_tensor(rank[:, :, :], rank[:, :, :], eb(need), ALU.is_lt))
                st.link(nc.vector.tensor_tensor(eq[:, :, :], eq[:, :, :], rank[:, :, :], ALU.mult))
                nc.vector.tensor_tensor(gt[:, :, :], gt[:, :, :], eq[:, :, :], ALU.add).then_inc(s["sel"], 1)
                v.wait_ge(s["sel_sums"], 1)
                ranks()
                st.link(nc.vector.tensor_scalar(eq[:, :, :], gt[:, :, :], -2.0 * N, 2.0 * N, ALU.mult, ALU.add))
                st.link(nc.vector.tensor_tensor(rank[:, :, :], rank[:, :, :], eq[:, :, :], ALU.add))
                st.link(nc.vector.tensor_scalar(hi[:, :, :], rank[:, :, :], float(CP), None, ALU.is_ge))
                for k in range(2, CC):
                    st.link(nc.vector.scalar_tensor_tensor(hi[:, :, :], rank[:, :, :], float(CP * k), hi[:, :, :], ALU.is_ge, ALU.add))
                nc.vector.tensor_copy(hi_b[:, :, :], hi[:, :, :])
                st.link(nc.vector.scalar_tensor_tensor(lo_b[:, :, :], hi[:, :, :], -float(CP), rank[:, :, :], ALU.mult, ALU.add))
                base2, PER2 = st.base + st.n, 8
                with v.Fori(0, E_ // 2) as j:
                    st = Steps(v, s["step"], PER2 * j + base2)

                    def hots(k):
                        v.wait_ge(s["list_mm"], 2 * j + k) if k == 0 else None
                        e = 2 * j + k
                        lo_e = lo_b[:, bass.ds(e, 1), :].rearrange("p a t -> p (a t)").unsqueeze(2).to_broadcast([P, TILES, CP])
                        hi_e = hi_b[:, bass.ds(e, 1), :].rearrange("p a t -> p (a t)").unsqueeze(2).to_broadcast([P, TILES, CC])
                        st.mark(nc.vector.tensor_tensor(hot_lo[:, k], lo_e, iota_lo[:, :].unsqueeze(1).to_broadcast([P, TILES, CP]), ALU.is_equal))
                        st.link(nc.vector.tensor_tensor(hot_hi[:, k], hi_e, iota_lo[:, 0:CC].unsqueeze(1).to_broadcast([P, TILES, CC]), ALU.is_equal))
                        nc.vector.tensor_scalar(ids[:, k, :, 0:CC], hot_hi[:, k], pid[:, 0:1], None, ALU.mult)
                        nc.vector.tensor_tensor(ids[:, k, :, CC:2 * CC], hot_hi[:, k],
                                                tile_no[:, :].unsqueeze(2).to_broadcast([P, TILES, CC]), ALU.mult).then_inc(s["hots"], 1)

                    def read(k):
                        v.wait_ge(s["list_mm"], 2 * j + k + 1)
                        st.link(nc.vector.tensor_scalar(lt[:, :], ps[0:CP, 7, CC:2 * CC], float(P), None, ALU.mult))
                        st.mark(nc.vector.tensor_tensor(lists_sb[:, bass.ds(2 * j + k, 1), :].rearrange("p a c -> p (a c)"),
                                                ps[0:CP, 7, 0:CC], lt[:, :], ALU.add))
                        st.wait()
                        nc.vector.memset(lt[:, :], 0.0).then_inc(s["list_read"], 1)
                    hots(0)
                    hots(1)
                    read(0)
                    read(1)
                    assert st.n == PER2, st.n


def experts(nc, d, h1, table, xfT, lists, h2):
    HALF = CAP // 2
    PK_ = HID + HID + 4 + D
    with ExitStack() as ctx:
        def sb(name, shape, dt=F32):
            return ctx.enter_context(nc.sbuf_tensor("ex_" + name, shape, dt))
        s = {n: ctx.enter_context(nc.semaphore("ex_" + n)) for n in
             ("consts_in w_in0 w_in1 xT_in h1_in up gelu down y_ready stored idx tok_in0 tok_in1 pool_gate tok_T tok_Tc scattered mlp_done score step").split()}
        w_s = sb("w_s", [P, PK_]); w_e = sb("w_e", [P, 2, PK_])
        xT = sb("xT", [D, 2, CAP]); hT = sb("hT", [P, 4, CAP])
        h1_s = sb("h1_s", [CP, 2, CC, D]); y = sb("y", [CP, 2, CC, D])
        lists_sb = sb("lists", [CP, E_, CC], U32); idx = sb("idx", [CP, 2, CC], U32)
        tok = sb("tok", [CP, 2, CC, D + E_]); score = sb("score", [CP, CC])
        ident = sb("ident", [P, P])
        gate_in = sb("gate_in", [16, 1]); gate_out = sb("gate_out", [16, 1])
        ps = ctx.enter_context(nc.psum_tensor("ex_ps", [P, 8, 512], F32))
        parts = lambda w: (w[:, 0:HID], w[:, HID:2 * HID].rearrange("p (j c) -> p j c", j=4), w[:, 2 * HID:2 * HID + 4],
                           w[0:CP, 2 * HID + 4:])

        def mlp_pe(pe, n, w, x):
            w1, w2, _, _ = parts(w)
            for j in range(4):
                if j >= 2:
                    pe.wait_ge(s["gelu"], 4 * n + j - 1)
                for k in range(2):
                    last = nc.tensor.matmul(ps[:, 2 * (j % 2) + k, 0:HALF], w1[:, j * P:(j + 1) * P], x[:, k * HALF:(k + 1) * HALF],
                                            start=True, stop=True)
                last.then_inc(s["up"], 1)
            pe.wait_ge(s["gelu"], 4 * n + 4)
            pe.wait_ge(s["y_ready"], n)
            for c in range(CC):
                for j in range(4):
                    last = nc.tensor.matmul(ps[0:CP, 4 + c // 4, (c % 4) * D:(c % 4 + 1) * D], hT[:, j, c * CP:(c + 1) * CP],
                                            w2[:, j, :], start=(j == 0), stop=(j == 3))
            last.then_inc(s["down"], 1)

        def mlp_act(a, n, w):
            b1 = parts(w)[2]
            for j in range(4):
                a.wait_ge(s["up"], 4 * n + j + 1)
                if j == 0:
                    a.wait_ge(s["down"], n)
                nc.scalar.activation(hT[:, j, :].rearrange("p (k c) -> p k c", k=2), ps[:, 2 * (j % 2):2 * (j % 2) + 2, 0:HALF],
                                     ACT.Gelu_apprx_tanh, bias=b1[:, j:j + 1]).then_inc(s["gelu"], 1)
        chunk_sets = ((4, 0, 4), (5, 4, 1))
        h1r = h1.rearrange("(i c p) k -> p i c k", c=CC, p=CP)
        h2r = h2.rearrange("(i c p) k -> p i c k", c=CC, p=CP)
        with nc.Block() as block:
            @block.sync
            def _(sp):
                sp.dma_start(w_s[:, :], d["w_ffn"][E_]).then_inc(s["consts_in"], 16)
                sp.dma_start(ident[:, :], d["ident"]).then_inc(s["consts_in"], 16)
                sp.dma_start(lists_sb[:, :, :], lists).then_inc(s["consts_in"], 16)
                with sp.Fori(0, E_ // 2) as g:
                    for k in range(2):
                        i = 2 * g + k
                        sp.wait_ge(s["y_ready"], 2 * g)
                        sp.dma_start(xT[:, k, :], xfT[:, bass.ds(i * CAP, CAP)]).then_inc(s["xT_in"], 16)
                        sp.dma_start(h1_s[:, k], h1r[:, bass.ds(i, 1)].rearrange("p i c k -> p (i c) k")).then_inc(s["h1_in"], 16)
                    for k in range(2):
                        i = 2 * g + k
                        sp.wait_ge(s["y_ready"], i + 1)
                        sp.dma_start(h2r[:, bass.ds(i, 1)].rearrange("p i c k -> p (i c) k"), y[:, k]).then_inc(s["stored"], 16)
                with sp.Fori(0, E_ // 2) as g:
                    for k in range(2):
                        sp.wait_ge(s["y_ready"], E_ + 2 * g)
                        sp.dma_start(w_e[:, k], d["w_ffn"][bass.ds(2 * g + k, 1)].rearrange("e p c -> (e p) c")).then_inc(s[f"w_in{k}"], 16)

            @block.gpsimd
            def _(pool):
                nc.gpsimd.memset(gate_in[:, :], 0.0).then_inc(s["pool_gate"], 1)
                pool.wait_ge(s["pool_gate"], 1)

                def gate(n):
                    pool.wait_ge(s["pool_gate"], n + 1)
                    nc.gpsimd.tensor_tensor(gate_out[:, :], gate_in[:, :], gate_in[:, :], ALU.add).then_inc(s["pool_gate"], 1)

                def gather(e, k):
                    pool.wait_ge(s["idx"], e + 1)
                    gate(2 * e - k)
                    for c in range(CC):
                        pool.indirect_dma_start(out=tok[:, k, c, :], out_offset=None, in_=table[:, :],
                                                in_offset=bass.IndirectOffsetOnAxis(ap=idx[:, k, c:c + 1], axis=0)).then_inc(s[f"tok_in{k}"], 16)

                def scatter(e, k):
                    pool.wait_ge(s["y_ready"], E_ + e + 1)
                    pool.wait_ge(s["scattered"], 16 * CC * e)
                    gate(2 * e - k + 2)
                    for c in range(CC):
                        pool.indirect_dma_start(out=h2[:, :], out_offset=bass.IndirectOffsetOnAxis(ap=idx[:, k, c:c + 1], axis=0),
                                                in_=y[:, k, c, :], in_offset=None, compute_op=ALU.add).then_inc(s["scattered"], 16)
                pool.wait_ge(s["stored"], 16 * E_)
                with pool.Fori(0, E_ // 2) as g:
                    for k in range(2):
                        gather(2 * g + k, k)
                    for k in range(2):
                        scatter(2 * g + k, k)
                pool.wait_ge(s["scattered"], 16 * CC * E_)

            @block.tensor
            def _(pe):
                pe.wait_ge(s["consts_in"], 48)
                with pe.Fori(0, E_ // 2) as g:
                    for k in range(2):
                        pe.wait_ge(s["xT_in"], 32 * g + 32)
                        mlp_pe(pe, 2 * g + k, w_s, xT[:, k, :])
                with pe.Fori(0, E_ // 2) as g:
                    for k in range(2):
                        e = 2 * g + k
                        pe.wait_ge(s[f"tok_in{k}"], 16 * CC * (g + 1))
                        for c in range(CC):
                            last = nc.tensor.transpose(ps[:, 6 + c // 4, (c % 4) * CP:(c % 4 + 1) * CP], tok[:, k, c, 0:D], ident[0:CP, 0:CP])
                        last.then_inc(s["tok_T"], 1)
                        pe.wait_ge(s["tok_Tc"], e + 1)
                        pe.wait_ge(s[f"w_in{k}"], 16 * (g + 1))
                        mlp_pe(pe, E_ + e, w_e[:, k, :], xT[:, k, :])

            @block.scalar
            def _(a):
                a.wait_ge(s["consts_in"], 48)
                with a.Fori(0, E_) as i:
                    mlp_act(a, i, w_s)
                with a.Fori(0, E_ // 2) as g:
                    for k in range(2):
                        mlp_act(a, E_ + 2 * g + k, w_e[:, k, :])

            @block.vector
            def _(v):
                v.wait_ge(s["consts_in"], 48)
                with v.Fori(0, E_ // 2) as g:
                    for k in range(2):
                        i = 2 * g + k
                        b2 = parts(w_s)[3]
                        v.wait_ge(s["h1_in"], 32 * g + 32)
                        nc.vector.tensor_tensor(h1_s[:, k], h1_s[:, k], b2.unsqueeze(1).to_broadcast([CP, CC, D]), ALU.add).then_inc(s["step"], 1)
                        v.wait_ge(s["step"], i + 1)
                        v.wait_ge(s["down"], i + 1)
                        v.wait_ge(s["stored"], 32 * g)
                        for bank, c0, n in chunk_sets:
                            last = nc.vector.tensor_tensor(y[:, k, c0:c0 + n, :], ps[0:CP, bank, 0:n * D].rearrange("p (c k) -> p c k", c=n),
                                                           h1_s[:, k, c0:c0 + n, :], ALU.add)
                        last.then_inc(s["y_ready"], 1)
                with v.Fori(0, E_ // 2) as g:
                    for k in range(2):
                        e = 2 * g + k
                        v.wait_ge(s["scattered"], 32 * CC * g)
                        nc.vector.tensor_copy(idx[:, k, :], lists_sb[:, bass.ds(e, 1), :].rearrange("p a c -> p (a c)")).then_inc(s["idx"], 1)
                    for k in range(2):
                        e = 2 * g + k
                        b2 = parts(w_e[:, k, :])[3]
                        v.wait_ge(s["tok_T"], e + 1)
                        v.wait_ge(s["y_ready"], E_ + e)
                        nc.vector.tensor_copy(score[:, :], tok[:, k, :, bass.ds(D + e, 1)].rearrange("p c a -> p (c a)"))
                        nc.vector.tensor_copy(xT[:, k, 0:4 * CP], ps[:, 6, 0:4 * CP])
                        nc.vector.tensor_copy(xT[:, k, 4 * CP:CAP], ps[:, 7, 0:CP]).then_inc(s["tok_Tc"], 1)
                        v.wait_ge(s["down"], E_ + e + 1)
                        for bank, c0, n in chunk_sets:
                            last = nc.vector.tensor_tensor(y[:, k, c0:c0 + n, :], ps[0:CP, bank, 0:n * D].rearrange("p (c k) -> p c k", c=n),
                                                           b2.unsqueeze(1).to_broadcast([CP, n, D]), ALU.add)
                        last.then_inc(s["step"], 1)
                        v.wait_ge(s["step"], E_ + e + 1)
                        v.wait_ge(s["tok_Tc"], e + 1)
                        for c in range(CC):
                            last = nc.vector.tensor_scalar(y[:, k, c, :], y[:, k, c, :], score[:, c:c + 1], None, ALU.mult)
                        last.then_inc(s["y_ready"], 1)


def expert_layout(i):
    c_ = np.ascontiguousarray
    carry = np.ones((P, E_, TILES), np.float32); carry[:, :, 0] = 0
    def pack(w1, b1, w2, b2):
        return np.concatenate([w1, w2.reshape(4, P, D).transpose(1, 0, 2).reshape(P, HID), b1.reshape(4, P).T,
                               np.broadcast_to(b2, (P, D))], 1)
    w = [pack(i['L0_ffn_w1'][e], i['L0_ffn_b1'][e], i['L0_ffn_w2'][e], i['L0_ffn_b2'][e]) for e in range(E_)]
    w.append(pack(i['L0_ffn_sw1'], i['L0_ffn_sb1'], i['L0_ffn_sw2'], i['L0_ffn_sb2']))
    return dict(ones=np.ones((P, P), np.float32), below=np.triu(np.ones((P, P), np.float32), 1),
                iota_lo=c_(np.broadcast_to(np.arange(CP, dtype=np.float32), (P, CP))),
                tile_no=c_(np.broadcast_to(np.arange(TILES, dtype=np.float32), (P, TILES))),
                pid=np.arange(P, dtype=np.float32)[:, None], carry=carry.reshape(P, -1),
                first_bit=np.full((P, E_), 1 << 29, np.int32), w_ffn=c_(np.stack(w)))


def peer(nc, d, src, dst):
    H, QD, HALF, PK, K = 8, 64, 32, 64, 16
    RUNS = [(0, 1, 16), (1, 1, 8), (2, 1, 5), (3, 1, 4), (4, 1, 3), (5, 3, 2), (8, 8, 1)]
    C = sum(n * m for _, n, m in RUNS)
    CH, HC = 4, 2 * C
    LO, HI = 32, 4
    SPLIT = 3
    G, TG = 4, 32
    TAKEN = -3.0e38
    with ExitStack() as ctx:
        def sb(name, shape, dt=F32):
            return ctx.enter_context(nc.sbuf_tensor("pr_" + name, shape, dt))

        def sem(name):
            return ctx.enter_context(nc.semaphore("pr_" + name))
        wq = sb("wq", [P, 512])
        rows = sb("rows", [P, 3, 512])
        down = sb("down", [P, HI, P])
        up = sb("up", [P, HI, P])
        kpad = sb("kpad", [PK, 4, P])
        ksq = sb("ksq", [PK, 4, P])
        knorm = sb("knorm", [PK, 4])
        kblk = sb("kblk", [P, 4 * PK])
        ident = sb("ident", [P, P])
        x = sb("x", [P, D])
        stats = sb("stats", [P, 6])
        mv = sb("mv", [P, 2])
        rstd = sb("rstd", [P, 1])
        xn = sb("xn", [P, D])
        xT = sb("xT", [P, P])
        q = sb("q", [P, 512])
        qc = sb("qc", [P, 512])
        qs = sb("qs", [P, 512])
        hsum = sb("hsum", [P, H])
        hvar = sb("hvar", [P, H])
        hln = sb("hln", [P, H])
        hrstd = sb("hrstd", [P, H])
        nsum = sb("nsum", [P, 2 * H])
        nrm = sb("nrm", [P, 2 * H])
        qT = sb("qT", [P, 4, P])
        s = sb("s", [P, 16, PK])
        sw = sb("sw", [P, 16, PK])
        sv = sb("sv", [P, 16, K])
        si = sb("si", [P, 16, K], U32)
        sif = sb("sif", [P, 16, K])
        cand = sb("cand", [P, H, C])
        candi = sb("candi", [P, H, C])
        cw = sb("cw", [P, H, C])
        cw2 = sb("cw2", [P, H, C])
        cm = sb("cm", [P, H, K])
        ce = sb("ce", [P, H, C])
        wgt = sb("wgt", [P, H, C])
        wsum = sb("wsum", [P, H])
        wT = sb("wT", [HC, 512])
        w3 = sb("w3", [HC, SPLIT, 512], BF16)
        wr = sb("wr", [HC, 512])
        fi = sb("fi", [HC, 512], I32)
        lo_i = sb("lo_i", [HC, 512], I32)
        hi_i = sb("hi_i", [HC, 512], I32)
        lo = sb("lo", [HC, 512], BF16)
        hi = sb("hi", [HC, 512], BF16)
        oh_lo = sb("oh_lo", [HC, LO, 512], BF16)
        oh_hi = sb("oh_hi", [HC, HI, 512], BF16)
        w_hi = sb("w_hi", [HC, HI, SPLIT, 512], BF16)
        act = sb("act", [P, HI, P])
        wE = sb("wE", [P, TG, HI])
        gblk = sb("gblk", [P, HI, P])
        o = sb("o", [P, D])
        ps = ctx.enter_context(nc.psum_tensor("pr_ps", [P, 8, 512], F32))
        ps_x, ps_q, ps_qT = ps[:, 0, 0:P], ps[:, 1, :], ps[:, 2, :]
        ps_s = ps[:, 3:5, :]
        ps_w, ps_in = ps[:, 5, 0:TG * HI * SPLIT], ps[:, 6, :]
        ps_wT, ps_iT, ps_o = ps[0:HC, 2, :], ps[0:HC, 1, :], ps[:, 0, 0:D]
        ps_k = ps[:, 7, 0:4 * PK]

        consts_in = sem("consts_in")
        k_norm_ln = sem("k_norm_ln"); k_rnorm = sem("k_rnorm"); k_ready = sem("k_ready"); k_T = sem("k_T"); k_blk = sem("k_blk")
        dve_step = sem("dve_step"); k_step = sem("k_step")
        x_in = sem("x_in"); x_var = sem("x_var"); x_rstd = sem("x_rstd"); x_norm = sem("x_norm"); x_T = sem("x_T"); x_Tc = sem("x_Tc")
        q_mm = sem("q_mm"); q_var = sem("q_var"); q_rstd = sem("q_rstd"); q_nsum = sem("q_nsum"); q_rnorm = sem("q_rnorm")
        q_norm = sem("q_norm"); q_T = sem("q_T"); q_Tc = sem("q_Tc"); sims = sem("sims"); sims_c = sem("sims_c")
        cand_sub = sem("cand_sub"); cand_exp = sem("cand_exp"); w_ready = sem("w_ready"); w_T = sem("w_T")
        fi_c = sem("fi_c"); wT_c = sem("wT_c"); onehots = sem("onehots"); scat = sem("scat"); inner = sem("inner"); gelu = sem("gelu")
        g_ready = sem("g_ready"); out_mm = sem("out_mm"); o_ready = sem("o_ready"); stored = sem("stored")
        gate = sb("gate", [P, 1])
        act_step = sem("act_step"); scat_read = sem("scat_read")

        with nc.Block() as block:
            @block.sync
            def _(sp):
                for to, name in ((wq, "wq_peer"), (rows, "rows_peer"), (down, "down_cols"), (up, "up_rows"),
                                 (kpad, "keys_pad"), (ident, "ident")):
                    sp.dma_start(to[:], d[name]).then_inc(consts_in, 16)
                with sp.Fori(0, TILES) as i:
                    sp.wait_ge(o_ready, i)
                    sp.dma_start(x[:, :], src[bass.ds(i * P, P), :]).then_inc(x_in, 16)
                    sp.wait_ge(o_ready, i + 1)
                    sp.dma_start(dst[bass.ds(i * P, P), :], o[:, :]).then_inc(stored, 16)
                sp.wait_ge(stored, 16 * TILES)

            @block.tensor
            def _(pe):
                pe.wait_ge(consts_in, 96)
                pe.wait_ge(k_ready, 1)
                for j in range(4):
                    last = nc.tensor.transpose(ps_k[:, j * PK:(j + 1) * PK], kpad[:, j, :], ident[0:PK, 0:PK])
                last.then_inc(k_T, 1)
                pe.wait_ge(k_blk, 1)
                with pe.Fori(0, TILES) as i:
                    pe.wait_ge(x_norm, i + 1)
                    nc.tensor.transpose(ps_x, xn[:, :], ident[:, :]).then_inc(x_T, 1)
                    pe.wait_ge(x_Tc, i + 1)
                    nc.tensor.matmul(ps_q, xT[:, :], wq[:, :], start=True, stop=True).then_inc(q_mm, 1)
                    for j in range(HI):
                        last = nc.tensor.matmul(ps_in[:, j * P:(j + 1) * P], down[:, j, :], xT[:, :], start=True, stop=True)
                    last.then_inc(inner, 1)
                    pe.wait_ge(q_norm, i + 1)
                    for j in range(4):
                        last = nc.tensor.transpose(ps_qT[:, j * P:(j + 1) * P], q[:, j * P:(j + 1) * P], ident[:, :])
                    last.then_inc(q_T, 1)
                    pe.wait_ge(q_Tc, i + 1)
                    for j in range(4):
                        last = nc.tensor.matmul(ps_s[:, j // 2, (j % 2) * 256:(j % 2 + 1) * 256], qT[:, j, :], kblk[:, :],
                                                start=True, stop=True)
                    last.then_inc(sims, 1)
                    pe.wait_ge(w_ready, i + 1)
                    for j in range(CH):
                        nc.tensor.transpose(ps_iT[:, j * P:(j + 1) * P],
                                            candi[:, 2 * j:2 * j + 2, :].rearrange("p a b -> p (a b)"), ident[:, :])
                    for j in range(CH):
                        last = nc.tensor.transpose(ps_wT[:, j * P:(j + 1) * P],
                                                   wgt[:, 2 * j:2 * j + 2, :].rearrange("p a b -> p (a b)"), ident[:, :])
                    last.then_inc(w_T, 1)
                    pe.wait_ge(onehots, i + 1)
                    for t in range(P):
                        g, u = t // TG, t % TG
                        for j in range(CH):
                            c = j * P + t
                            last = nc.tensor.matmul(ps_w[g * 32:(g + 1) * 32, u * 12:(u + 1) * 12],
                                                    oh_lo[:, :, c], w_hi[:, :, :, c].rearrange("p a b -> p (a b)"),
                                                    start=(j == 0), stop=(j == CH - 1))
                    last.then_inc(scat, 1)
                    pe.wait_ge(g_ready, i + 1)
                    for j in range(HI):
                        last = nc.tensor.matmul(ps_o, gblk[:, j, :], up[:, j, :], start=(j == 0), stop=(j == HI - 1))
                    last.then_inc(out_mm, 1)

            @block.scalar
            def _(a):
                a.wait_ge(k_norm_ln, 1)
                nc.scalar.activation(knorm[:, :], knorm[:, :], ACT.Sqrt).then_inc(k_rnorm, 1)
                with a.Fori(0, TILES) as i:
                    def rsqrt(out, tmp, in_, k):
                        nc.scalar.activation(tmp, in_, ACT.Ln).then_inc(act_step, 1)
                        a.wait_ge(act_step, 5 * i + k)
                        return nc.scalar.activation(out, tmp, ACT.Exp, scale=-0.5)
                    a.wait_ge(x_var, i + 1)
                    rsqrt(rstd[:, :], mv[:, 0:1], mv[:, 1:2], 1).then_inc(x_rstd, 1)
                    a.wait_ge(x_T, i + 1)
                    nc.scalar.activation(xT[:, :], ps_x, ACT.Copy).then_inc(x_Tc, 1)
                    a.wait_ge(q_var, i + 1)
                    rsqrt(hrstd[:, :], hln[:, :], hvar[:, :], 2).then_inc(q_rstd, 1)
                    a.wait_ge(q_nsum, i + 1)
                    rsqrt(nrm[:, :], nsum[:, :], nsum[:, :], 3).then_inc(q_rnorm, 1)
                    a.wait_ge(q_T, i + 1)
                    nc.scalar.activation(qT[:, :, :].rearrange("p a b -> p (a b)"), ps_qT, ACT.Copy).then_inc(q_Tc, 1)
                    a.wait_ge(sims, i + 1)
                    for j in range(2):
                        last = nc.scalar.activation(s[:, 8 * j:8 * j + 8, :].rearrange("p a b -> p (a b)"), ps_s[:, j, :], ACT.Copy)
                    last.then_inc(sims_c, 1)
                    a.wait_ge(cand_sub, i + 1)
                    nc.scalar.activation(ce[:, :, :], cw[:, :, :], ACT.Exp).then_inc(cand_exp, 1)
                    a.wait_ge(w_T, i + 1)
                    nc.scalar.activation(fi[:, :], ps_iT, ACT.Copy).then_inc(fi_c, 1)
                    nc.scalar.activation(wT[:, :], ps_wT, ACT.Copy).then_inc(wT_c, 1)
                    a.wait_ge(wT_c, i + 1)
                    nc.scalar.activation(w3[:, 0, :], wT[:, :], ACT.Copy).then_inc(act_step, 1)
                    a.wait_ge(inner, i + 1)
                    nc.scalar.activation(act[:, :, :].rearrange("p a b -> p (a b)"), ps_in, ACT.Gelu).then_inc(act_step, 1)

            @block.vector
            def _(v):
                v.wait_ge(consts_in, 96)
                nc.vector.memset(gblk[:, :, :], 0.0).then_inc(k_step, 1)
                nc.vector.tensor_tensor(ksq[:, :, :], kpad[:, :, :], kpad[:, :, :], ALU.mult).then_inc(k_step, 1)
                v.wait_ge(k_step, 2)
                nc.vector.tensor_reduce(knorm[:, :], ksq[:, :, :], AX.X, ALU.add).then_inc(k_norm_ln, 1)
                v.wait_ge(k_rnorm, 1)
                nc.vector.tensor_scalar(knorm[:, :], knorm[:, :], 1e-12, None, ALU.max).then_inc(k_step, 1)
                v.wait_ge(k_step, 3)
                nc.vector.reciprocal(knorm[:, :], knorm[:, :]).then_inc(k_step, 1)
                v.wait_ge(k_step, 4)
                for j in range(4):
                    last = nc.vector.tensor_scalar(kpad[:, j, :], kpad[:, j, :], knorm[:, j:j + 1], None, ALU.mult)
                last.then_inc(k_ready, 1)
                v.wait_ge(k_T, 1)
                nc.vector.tensor_copy(kblk[:, :], ps_k).then_inc(k_blk, 1)
                PER = 43
                with v.Fori(0, TILES) as i:
                    n = [0]

                    def through():
                        n[0] += 1
                        nc.vector.memset(gate[:, :], 0.0).then_inc(dve_step, 1)

                    def link(ins):
                        n[0] += 1
                        ins.then_inc(dve_step, 1)
                        v.wait_ge(dve_step, PER * i + n[0])
                    hv = lambda t: t[:, :].rearrange("p (h c) -> p h c", h=H)
                    hb = lambda t: t[:, :].unsqueeze(2).to_broadcast([P, H, QD])
                    v.wait_ge(x_in, 16 * i + 16)
                    through()
                    link(nc.vector.bn_stats(stats[:, :], x[:, :]))
                    through()
                    link(nc.vector.bn_aggr(mv[:, :], stats[:, :]))
                    nc.vector.tensor_scalar(xn[:, :], x[:, :], mv[:, 0:1], None, ALU.subtract).then_inc(dve_step, 1)
                    nc.vector.tensor_scalar(mv[:, 1:2], mv[:, 1:2], 1e-5, None, ALU.add).then_inc(x_var, 1)
                    n[0] += 1
                    v.wait_ge(x_rstd, i + 1)
                    v.wait_ge(dve_step, PER * i + n[0])
                    nc.vector.tensor_scalar(xn[:, :], xn[:, :], rstd[:, 0:1], None, ALU.mult).then_inc(x_norm, 1)
                    v.wait_ge(q_mm, i + 1)
                    link(nc.vector.tensor_tensor(q[:, :], ps_q, rows[:, 0, :], ALU.add))
                    link(nc.vector.tensor_reduce(hsum[:, :], hv(q), AX.X, ALU.add))
                    link(nc.vector.tensor_scalar(hsum[:, :], hsum[:, :], 1.0 / QD, None, ALU.mult))
                    link(nc.vector.tensor_tensor(hv(qc), hv(q), hb(hsum), ALU.subtract))
                    link(nc.vector.tensor_tensor(qs[:, :], qc[:, :], qc[:, :], ALU.mult))
                    link(nc.vector.tensor_reduce(hvar[:, :], hv(qs), AX.X, ALU.add))
                    nc.vector.tensor_scalar(hvar[:, :], hvar[:, :], 1.0 / QD, 1e-5, ALU.mult, ALU.add).then_inc(q_var, 1)
                    v.wait_ge(q_rstd, i + 1)
                    link(nc.vector.tensor_tensor(hv(qc), hv(qc), hb(hrstd), ALU.mult))
                    link(nc.vector.tensor_tensor(qc[:, :], qc[:, :], rows[:, 1, :], ALU.mult))
                    link(nc.vector.tensor_tensor(qc[:, :], qc[:, :], rows[:, 2, :], ALU.add))
                    link(nc.vector.tensor_tensor(qs[:, :], qc[:, :], qc[:, :], ALU.mult))
                    link(nc.vector.tensor_reduce(nsum[:, :], qs[:, :].rearrange("p (h c) -> p h c", c=HALF), AX.X, ALU.add))
                    nc.vector.tensor_scalar(nsum[:, :], nsum[:, :], 1e-24, None, ALU.max).then_inc(q_nsum, 1)
                    v.wait_ge(q_rnorm, i + 1)
                    nc.vector.tensor_tensor(q[:, :].rearrange("p (h c) -> p h c", c=HALF),
                                            qc[:, :].rearrange("p (h c) -> p h c", c=HALF),
                                            nrm[:, :].unsqueeze(2).to_broadcast([P, 2 * H, HALF]), ALU.mult).then_inc(q_norm, 1)
                    v.wait_ge(sims_c, i + 1)
                    through()
                    for r in range(16):
                        last = nc.vector.max(sv[:, r, 0:8], s[:, r, :])
                    link(last)
                    through()
                    for r in range(16):
                        nc.vector.max_index(si[:, r, 0:8], sv[:, r, 0:8], s[:, r, :])
                    for r in range(16):
                        last = nc.vector.match_replace(sw[:, r, :], sv[:, r, 0:8], s[:, r, :], TAKEN)
                    link(last)
                    through()
                    for r in range(16):
                        last = nc.vector.max(sv[:, r, 8:16], sw[:, r, :])
                    link(last)
                    through()
                    for r in range(16):
                        last = nc.vector.max_index(si[:, r, 8:16], sv[:, r, 8:16], sw[:, r, :])
                    link(last)
                    link(nc.vector.tensor_copy(sif[:, :, :], si[:, :, :]))
                    for c_, v_ in ((cand, sv), (candi, sif)):
                        s0 = v_[:, :, :].rearrange("p (h u) k -> p h u k", u=2)
                        at = 0
                        for a0, na, m in RUNS:
                            o_ = c_[:, :, at:at + na * m]
                            if m == 1:
                                i0, i1 = s0[:, :, 0, a0:a0 + na], s0[:, :, 1, 0:1].to_broadcast([P, H, na])
                            elif na == 1:
                                i0, i1 = s0[:, :, 0, a0:a0 + 1].to_broadcast([P, H, m]), s0[:, :, 1, 0:m]
                            else:
                                o_ = o_.rearrange("p h (a b) -> p h a b", b=m)
                                i0 = s0[:, :, 0, a0:a0 + na].unsqueeze(3).to_broadcast([P, H, na, m])
                                i1 = s0[:, :, 1, 0:m].unsqueeze(2).to_broadcast([P, H, na, m])
                            last = nc.vector.tensor_tensor(o_, i0, i1, ALU.add)
                            at += na * m
                    link(last)
                    through()
                    for h in range(H):
                        last = nc.vector.max(cm[:, h, 0:8], cand[:, h, :])
                    link(last)
                    through()
                    for h in range(H):
                        last = nc.vector.match_replace(cw[:, h, :], cm[:, h, 0:8], cand[:, h, :], TAKEN)
                    link(last)
                    through()
                    for h in range(H):
                        last = nc.vector.max(cm[:, h, 8:16], cw[:, h, :])
                    link(last)
                    through()
                    for h in range(H):
                        last = nc.vector.match_replace(cw2[:, h, :], cm[:, h, 8:16], cw[:, h, :], TAKEN)
                    link(last)
                    nc.vector.tensor_tensor(cw[:, :, :], cand[:, :, :], cm[:, :, 0:1].to_broadcast([P, H, C]),
                                            ALU.subtract).then_inc(cand_sub, 1)
                    v.wait_ge(cand_exp, i + 1)
                    link(nc.vector.scalar_tensor_tensor(wgt[:, :, :], cw2[:, :, :], TAKEN, ce[:, :, :], ALU.is_equal, ALU.mult))
                    link(nc.vector.tensor_reduce(wsum[:, :], wgt[:, :, :], AX.X, ALU.add))
                    link(nc.vector.reciprocal(wsum[:, :], wsum[:, :]))
                    nc.vector.tensor_tensor(wgt[:, :, :], wgt[:, :, :], wsum[:, :].unsqueeze(2).to_broadcast([P, H, C]),
                                            ALU.mult).then_inc(w_ready, 1)
                    v.wait_ge(fi_c, i + 1)
                    nc.vector.tensor_scalar(lo_i[:, :], fi[:, :], LO - 1, None, ALU.bitwise_and)
                    link(nc.vector.tensor_scalar(hi_i[:, :], fi[:, :], 5, None, ALU.logical_shift_right))
                    nc.vector.tensor_copy(lo[:, :], lo_i[:, :])
                    link(nc.vector.tensor_copy(hi[:, :], hi_i[:, :]))
                    for e in range(HI):
                        nc.vector.tensor_scalar(oh_hi[:, e, :], hi[:, :], float(e), None, ALU.is_equal)
                    for e in range(LO):
                        nc.vector.tensor_scalar(oh_lo[:, e, :], lo[:, :], float(e), None, ALU.is_equal)
                    v.wait_ge(act_step, 5 * i + 4)
                    link(nc.vector.tensor_tensor(wr[:, :], wT[:, :], w3[:, 0, :], ALU.subtract))
                    link(nc.vector.tensor_copy(w3[:, 1, :], wr[:, :]))
                    link(nc.vector.tensor_tensor(w3[:, 2, :], wr[:, :], w3[:, 1, :], ALU.subtract))
                    for e in range(HI):
                        last = nc.vector.tensor_tensor(w_hi[:, e, :, :], w3[:, :, :],
                                                       oh_hi[:, e:e + 1, :].to_broadcast([HC, SPLIT, 512]), ALU.mult)
                    last.then_inc(onehots, 1)
                    v.wait_ge(scat, i + 1)
                    link(nc.vector.tensor_reduce(wE[:, :, :], ps_w.rearrange("p (t a b) -> p t a b", a=HI, b=SPLIT), AX.X, ALU.add))
                    v.wait_ge(act_step, 5 * i + 5)
                    for g in range(G):
                        r = slice(g * 32, (g + 1) * 32)
                        last = nc.vector.tensor_tensor(gblk[r, :, g * TG:(g + 1) * TG], act[r, :, g * TG:(g + 1) * TG],
                                                       wE[r, :, :].rearrange("p t a -> p a t"), ALU.mult)
                    last.then_inc(g_ready, 1)
                    v.wait_ge(out_mm, i + 1)
                    v.wait_ge(stored, 16 * i)
                    nc.vector.tensor_tensor(o[:, :], ps_o, x[:, :], ALU.add).then_inc(o_ready, 1)
                    assert n[0] == PER, n[0]


def peer_layout(i):
    kp = np.zeros((64, 4, 128), np.float32)
    for j in range(4):
        kp[:, j, 32 * j:32 * j + 32] = i['L1_ffn_keys1' if j % 2 else 'L1_ffn_keys0']
    dn = i['L1_ffn_expert_down'][:128].reshape(4, 1, 32, 128)
    dn = np.broadcast_to(dn, (4, 4, 32, 128)).transpose(3, 0, 1, 2).reshape(128, 4, 128)
    u = i['L1_ffn_expert_up'][:128].reshape(1, 4, 32, 128)
    u = np.broadcast_to(u, (4, 4, 32, 128)).transpose(0, 2, 1, 3).reshape(128, 4, 128)
    rows = np.stack([i['L1_ffn_bq'], np.tile(i['L1_ffn_ln_g'], 8), np.tile(i['L1_ffn_ln_b'], 8)])
    return dict(wq_peer=np.ascontiguousarray(i['L1_ffn_Wq'].T), rows_peer=np.ascontiguousarray(np.broadcast_to(rows, (128, 3, 512))),
                down_cols=np.ascontiguousarray(dn), up_rows=np.ascontiguousarray(u), keys_pad=kp,
                ident=np.eye(128, dtype=np.float32))


def build(nc, d, out):
    scratch = lambda name, shape, dt=F32: nc.dram_tensor(name, shape, dt, kind="Internal").ap()
    h0, h1, h2, h3 = (scratch(f"h{n}", [N, D]) for n in range(4))
    table, probs, xfT = scratch("table", [N, D + E_]), scratch("probs", [N, E_]), scratch("xfT", [D, N])
    lists = scratch("lists", [CP, E_, CC], U32)
    embed(nc, d, h0)
    attend0(nc, d, h0, h1, table, probs, xfT)
    route(nc, d, probs, lists)
    experts(nc, d, h1, table, xfT, lists, h2)
    attend1(nc, d, h2, h3)
    peer(nc, d, h3, out)


def kernel(**inputs):
    import concourse.bacc as bacc
    from concourse.bass_utils import run_bass_kernel_spmd

    i = {k: np.asarray(v) for k, v in inputs.items()}
    arrays = {**attention_layout(i), **expert_layout(i), **peer_layout(i)}
    nc = bacc.Bacc("TRN2", target_bir_lowering=False, num_devices=1)
    d = {k: nc.dram_tensor("in_" + k, a.shape, mybir.dt.from_np(a.dtype), kind="ExternalInput").ap() for k, a in arrays.items()}
    out = nc.dram_tensor("out", (N, D), F32, kind="ExternalOutput").ap()
    build(nc, d, out)
    r = run_bass_kernel_spmd(nc, [{"in_" + k: a for k, a in arrays.items()}], core_ids=[0])
    return r.results[0]["out"].reshape(B, T, D)
```

```python
import numpy as np
import concourse.bass as bass
from concourse import mybir
from contextlib import ExitStack, contextmanager

F32 = mybir.dt.float32
BF16 = mybir.dt.bfloat16
I32 = mybir.dt.int32
U16 = mybir.dt.uint16
F16 = mybir.dt.float16
U32 = mybir.dt.uint32
ALU = mybir.AluOpType
ACT = mybir.ActivationFunctionType
AX = mybir.AxisListType
D, B, T, P = 128, 128, 65, 128
N = B * T
GB = 4
STEPS = B // GB
W = GB * T
EPS = 1e-5


@contextmanager
def semaphores(nc, prefix, names):
    held = {n: nc.alloc_semaphore(prefix + n) for n in names.split()}
    yield held
    nc.clear_and_free_semaphores(list(held.values()))
    nc.all_engine_barrier()


class Steps:

    def __init__(self, eng, sem, base=0):
        self.eng, self.sem, self.base, self.n = eng, sem, base, 0

    def mark(self, ins):
        self.n += 1
        ins.then_inc(self.sem, 1)

    def wait(self):
        self.eng.wait_ge(self.sem, self.base + self.n)

    def link(self, ins):
        self.mark(ins)
        self.wait()


def embed(nc, d, dst):
    NB = 8
    BLOCKS = B // NB
    TOK = T - 1
    KC, REST = 18, 48
    with ExitStack() as ctx:
        def sb(name, shape, dt=F32):
            return ctx.enter_context(nc.sbuf_tensor("em_" + name, shape, dt))
        w = sb("w", [P, KC, D])
        w_rest = sb("w_rest", [REST, D])
        bias = sb("bias", [D, 1])
        pos = sb("pos", [D, T])
        cls = sb("cls", [D, 1])
        ident = sb("ident", [P, P])
        x = sb("x", [P, 2, KC, 512])
        x_rest = sb("x_rest", [REST, 2, 512])
        tokT = sb("tokT", [D, NB, T])
        tok = sb("tok", [T, NB, D])
        ps = ctx.enter_context(nc.psum_tensor("em_ps", [P, 8, 512], F32))
        s = ctx.enter_context(semaphores(nc, "em_", "consts_in x_in0 x_in1 acc_done tokT_ready tok_T tok_ready cls_ready stored"))
        rows = dst.rearrange("(b t) c -> t b c", t=T)
        with nc.Block() as block:
            @block.sync
            def _(sp):
                for to, name in ((w, "w_tok"), (w_rest, "w_tok_rest"), (bias, "b_tok"), (pos, "pos_cols"), (cls, "cls_col"),
                                 (ident, "ident")):
                    sp.dma_start(to[:], d[name]).then_inc(s["consts_in"], 16)
                with sp.Fori(0, BLOCKS // 2) as g:
                    for k in range(2):
                        sp.wait_ge(s["acc_done"], 2 * g)
                        sp.dma_start(x[:, k], d["x_main"][bass.ds(2 * g + k, 1)].rearrange("g p k t -> (g p) k t")).then_inc(s[f"x_in{k}"], 16)
                        sp.dma_start(x_rest[:, k], d["x_rest"][bass.ds(2 * g + k, 1)].rearrange("g p t -> (g p) t")).then_inc(s[f"x_in{k}"], 16)

            @block.gpsimd
            def _(pool):
                with pool.Fori(0, BLOCKS) as g:
                    pool.wait_ge(s["tok_ready"], g + 1)
                    pool.dma_start(rows[:, bass.ds(g * NB, NB), :], tok[:, :, :]).then_inc(s["stored"], 16)
                pool.wait_ge(s["stored"], 16 * BLOCKS)

            @block.tensor
            def _(pe):
                pe.wait_ge(s["consts_in"], 96)
                with pe.Fori(0, BLOCKS // 2) as g:
                    for k in range(2):
                        pe.wait_ge(s[f"x_in{k}"], 32 * g + 32)
                        pe.wait_ge(s["tokT_ready"], 2 * g + k)
                        for c in range(KC):
                            nc.tensor.matmul(ps[:, k, :], w[:, c, :], x[:, k, c, :], start=(c == 0), stop=False)
                        nc.tensor.matmul(ps[:, k, :], w_rest[:, :], x_rest[:, k, :], start=False, stop=True).then_inc(s["acc_done"], 1)
                        pe.wait_ge(s["tokT_ready"], 2 * g + k + 1)
                        pe.wait_ge(s["tok_ready"], 2 * g + k)
                        for b in range(NB):
                            last = nc.tensor.transpose(ps[0:T, 2 + b // 4, (b % 4) * D:(b % 4 + 1) * D], tokT[:, b, :], ident[:, :])
                        last.then_inc(s["tok_T"], 1)

            @block.scalar
            def _(a):
                with a.Fori(0, BLOCKS) as g:
                    a.wait_ge(s["tok_T"], g + 1)
                    a.wait_ge(s["stored"], 16 * g)
                    for k in range(2):
                        last = nc.scalar.activation(tok[:, 4 * k:4 * k + 4, :].rearrange("p w c -> p (w c)"),
                                                    ps[0:T, 2 + k, :], ACT.Copy)
                    last.then_inc(s["tok_ready"], 1)

            @block.vector
            def _(v):
                v.wait_ge(s["consts_in"], 96)
                nc.vector.tensor_scalar(tokT[:, :, 0:1], pos[:, 0:1].unsqueeze(1).to_broadcast([D, NB, 1]), cls[:, 0:1], None,
                                        ALU.mult).then_inc(s["cls_ready"], 1)
                with v.Fori(0, BLOCKS // 2) as g:
                    for k in range(2):
                        v.wait_ge(s["acc_done"], 2 * g + k + 1)
                        v.wait_ge(s["tok_T"], 2 * g + k)
                        nc.vector.scalar_tensor_tensor(tokT[:, :, 1:T], ps[:, k, :].rearrange("p (b t) -> p b t", t=TOK), bias[:, 0:1],
                                                       pos[:, 1:T].unsqueeze(1).to_broadcast([D, NB, TOK]),
                                                       ALU.add, ALU.mult).then_inc(s["tokT_ready"], 1)


def after(eng, sem, value):
    if not isinstance(value, int) or value > 0:
        eng.wait_ge(sem, value)


def pipelined(eng, body, count, ahead, behind):
    for i in range(-ahead, behind + 1):
        body(i)
    with eng.Fori(behind + 1, count - ahead) as i:
        body(i)
    for i in range(count - ahead, count + behind):
        body(i)


def newton_rsqrt(nc, pool, steps, rough_ready, n, y, t, v, c15, scale, add, done):
    pool.wait_ge(rough_ready, n + 1)
    st = Steps(pool, steps, 4 * n)
    st.mark(nc.gpsimd.tensor_tensor(t, y, y, ALU.mult))
    st.link(nc.gpsimd.tensor_scalar(v, v, -0.5 * scale, -0.5 * add, ALU.mult, ALU.add))
    st.link(nc.gpsimd.tensor_tensor(t, t, v, ALU.mult))
    st.link(nc.gpsimd.tensor_tensor(t, t, c15, ALU.add))
    nc.gpsimd.tensor_tensor(y, y, t, ALU.mult).then_inc(done, 1)


def row_stats(nc, v, steps, n, gate, x, stats, mv, done):
    st = Steps(v, steps, 3 * n)
    st.mark(nc.vector.memset(gate, 0.0))
    for j in range(x.shape[1]):
        last = nc.vector.bn_stats(stats[:, j, :], x[:, j, :])
    st.link(last)
    st.mark(nc.vector.memset(gate, 0.0))
    for j in range(x.shape[1]):
        last = nc.vector.bn_aggr(mv[:, j, :], stats[:, j, :])
    last.then_inc(done, 1)


def attend0(nc, d, src, dst, table, probs, xfT):
    E = 16
    with ExitStack() as ctx:
        def sb(name, shape, dt=F32):
            return ctx.enter_context(nc.sbuf_tensor("a0_" + name, shape, dt))
        wkq = sb("wkq", [D, 4, D])
        bkq = sb("bkq", [D, 4])
        wvT = sb("wvT", [D, D]); wp = sb("wp", [D, D]); bv = sb("bv", [D, T]); bp = sb("bp", [T, D])
        wvp = sb("wvp", [D, D]); bvp = sb("bvp", [T, D])
        gate_w = sb("gate_w", [D, E])
        cos = sb("cos", [D, T]); sin = sb("sin", [D, T]); tri = sb("tri", [T, T])
        ident = sb("ident", [P, P])
        x = sb("x", [T, GB, D]); xr = sb("xr", [T, GB, D]); xn = sb("xn", [T, GB, D])
        stats1 = sb("stats1", [T, GB, 6]); mv1 = sb("mv1", [T, GB, 2]); ln1 = sb("ln1", [T, GB]); rstd1 = sb("rstd1", [T, GB])
        stats2 = sb("stats2", [T, GB, 6]); mv2 = sb("mv2", [T, GB, 2]); ln2 = sb("ln2", [T, GB]); rstd2 = sb("rstd2", [T, GB])
        gate1 = sb("gate1", [T, 1]); gate2 = sb("gate2", [T, 1]); c15 = sb("c15", [T, GB]); eps = sb("eps", [T, 1])
        xT = sb("xT", [D, W])
        r1 = sb("r1", [D, 2, W]); r2 = sb("r2", [D, 2, W])
        kT = sb("kT", [D, W]); qT = sb("qT", [D, W]); vv = sb("vv", [T, GB, D])
        ab = sb("ab", [T, W]); raw = sb("raw", [T, W]); wei = sb("wei", [T, W])
        h = sb("h", [T, GB, D]); xf = sb("xf", [T, GB, D]); xfTs = sb("xfTs", [D, W])
        lm = sb("lm", [T, GB]); le = sb("le", [T, GB, E]); ls = sb("ls", [T, GB]); pb = sb("pb", [T, GB, E])
        ps = ctx.enter_context(nc.psum_tensor("a0_ps", [P, 8, 512], F32))
        ps_T, ps_l, ps_v, ps_sc, ps_out = ps[:, 0, 0:W], ps[0:T, 0, W:W + GB * E], ps[0:T, 5, :], ps[0:T, 6, 0:W], ps[0:T, 7, :]
        s = ctx.enter_context(semaphores(nc, "a0_", """consts_in folded unfolded scaled ready x_in xr_in var1 rough1 rstd1 normed x_T x_Tc kq v kq_rot vv_ready sc abs_step exp_step sp_ln
             wei_raw wei_ready out xb_ready h_ready var2 rough2 rstd2 xf_ready xf_T xf_Tc logits l_sub l_exp pb_ready
             h_stored xf_stored xfT_stored pb_stored stat1_step stat2_step ln1_step ln2_step newton1_step newton2_step
             rot_step max_step sum_step"""))
        rows_in = src.rearrange("(b t) c -> t b c", t=T)
        rows_h = dst.rearrange("(b t) c -> t b c", t=T)
        rows_t = table.rearrange("(b t) c -> t b c", t=T)
        rows_p = probs.rearrange("(b t) c -> t b c", t=T)
        bat = lambda ap: ap.rearrange("p (g t) -> p g t", g=GB)
        rows = lambda ap: ap.rearrange("p (g c) -> p g c", g=GB)
        per_image = lambda ap, parts, m: ap.unsqueeze(1).to_broadcast([parts, GB, m])
        has = lambda i, ahead: not isinstance(i, int) or 0 <= i + ahead < STEPS
        with nc.Block() as block:
            @block.sync
            def _(sp):
                for to, name in ((wkq, "w_kq"), (bkq, "b_kq"), (wvT, "wvT"), (wp, "wp"), (bv, "bv_cols"), (bp, "bp_rows"),
                                 (gate_w, "gate_w"), (cos, "cos"), (sin, "sin"), (tri, "tri"), (ident, "ident")):
                    sp.dma_start(to[:], d[name]).then_inc(s["consts_in"], 16)

                def load(n):
                    after(sp, s["normed"], n)
                    sp.dma_start(x[:, :, :], rows_in[:, bass.ds(n * GB, GB), :]).then_inc(s["x_in"], 16)

                def residual(n):
                    after(sp, s["h_ready"], n)
                    sp.dma_start(xr[:, :, :], rows_in[:, bass.ds(n * GB, GB), :]).then_inc(s["xr_in"], 16)

                def body(i):
                    if has(i, 3):
                        load(i + 3)
                    if has(i, 1):
                        residual(i + 1)
                    if has(i, 0):
                        sp.wait_ge(s["h_ready"], i + 1)
                        sp.dma_start(rows_h[:, bass.ds(i * GB, GB), :], h[:, :, :]).then_inc(s["h_stored"], 16)
                    if has(i, -1):
                        sp.wait_ge(s["pb_ready"], i)
                        sp.dma_start(rows_t[:, bass.ds((i - 1) * GB, GB), D:D + E], pb[:, :, :]).then_inc(s["pb_stored"], 16)
                        sp.dma_start(rows_p[:, bass.ds((i - 1) * GB, GB), :], pb[:, :, :]).then_inc(s["pb_stored"], 16)
                    if has(i, 0):
                        sp.wait_ge(s["xf_ready"], i + 1)
                        sp.dma_start(rows_t[:, bass.ds(i * GB, GB), 0:D], xf[:, :, :]).then_inc(s["xf_stored"], 16)
                        sp.wait_ge(s["xf_Tc"], i + 1)
                        sp.dma_start(xfT[:, bass.ds(i * W, W)], xfTs[:, :]).then_inc(s["xfT_stored"], 16)
                pipelined(sp, body, STEPS, 3, 1)
                for kind in ("h_stored", "xf_stored", "xfT_stored"):
                    sp.wait_ge(s[kind], 16 * STEPS)
                sp.wait_ge(s["pb_stored"], 32 * STEPS)

            @block.gpsimd
            def _(pool):
                nc.gpsimd.memset(c15[:, :], 1.5).then_inc(s["ready"], 1)
                pool.wait_ge(s["ready"], 1)
                pool.wait_ge(s["consts_in"], 176)

                def body(i):
                    if has(i, 1):
                        pool.wait_ge(s["wei_raw"], i + 2)
                        after(pool, s["out"], i + 1)
                        nc.gpsimd.tensor_tensor(bat(wei[:, :]), bat(raw[:, :]), per_image(tri[:, :], T, T), ALU.mult).then_inc(s["wei_ready"], 1)
                    if has(i, 0):
                        newton_rsqrt(nc, pool, s["newton2_step"], s["rough2"], i, rstd2[:, :], ln2[:, :], mv2[:, :, 1], c15[:, :], 1.0, EPS, s["rstd2"])
                    if has(i, 3):
                        newton_rsqrt(nc, pool, s["newton1_step"], s["rough1"], i + 3, rstd1[:, :], ln1[:, :], mv1[:, :, 1], c15[:, :], 1.0, EPS, s["rstd1"])
                    if has(i, 1):
                        pool.wait_ge(s["xr_in"], 16 * i + 32)
                        nc.gpsimd.tensor_tensor(xr[:, :, :], xr[:, :, :], per_image(bp[:, :], T, D), ALU.add).then_inc(s["xb_ready"], 1)
                pipelined(pool, body, STEPS, 3, 1)

            @block.tensor
            def _(pe):
                pe.wait_ge(s["consts_in"], 176)
                nc.tensor.matmul(ps[:, 0, 0:D], wvT[:, :], wp[:, :], start=True, stop=True)
                nc.tensor.matmul(ps[0:T, 1, 0:D], bv[:, :], wp[:, :], start=True, stop=True).then_inc(s["folded"], 1)
                pe.wait_ge(s["unfolded"], 2)
                pe.wait_ge(s["scaled"], 1)

                def body(i):
                    if has(i, 1):
                        pe.wait_ge(s["kq_rot"], i + 2)
                        after(pe, s["wei_raw"], i + 1)
                        for g in range(GB):
                            c = slice(g * T, (g + 1) * T)
                            last = nc.tensor.matmul(ps_sc[:, c], qT[:, c], kT[:, c], start=True, stop=True)
                        last.then_inc(s["sc"], 1)
                    if has(i, 2):
                        pe.wait_ge(s["normed"], i + 3)
                        after(pe, s["l_sub"], i)
                        for g in range(GB):
                            last = nc.tensor.transpose(ps_T[:, g * T:(g + 1) * T], xn[:, g, :], ident[0:T, 0:T])
                        last.then_inc(s["x_T"], 1)
                        pe.wait_ge(s["x_Tc"], i + 3)
                        for j in range(4):
                            last = nc.tensor.matmul(ps[:, 1 + j, 0:W], wkq[:, j, :], xT[:, :], start=True, stop=True)
                        last.then_inc(s["kq"], 1)
                        after(pe, s["vv_ready"], i + 2)
                        for g in range(GB):
                            last = nc.tensor.matmul(ps_v[:, g * D:(g + 1) * D], xT[:, g * T:(g + 1) * T], wvp[:, :],
                                                    start=True, stop=True)
                        last.then_inc(s["v"], 1)
                    if has(i, 1):
                        pe.wait_ge(s["vv_ready"], i + 2)
                        pe.wait_ge(s["wei_ready"], i + 2)
                        after(pe, s["h_ready"], i + 1)
                        for g in range(GB):
                            last = nc.tensor.matmul(ps_out[:, g * D:(g + 1) * D], wei[:, g * T:(g + 1) * T], vv[:, g, :],
                                                    start=True, stop=True)
                        last.then_inc(s["out"], 1)
                    if has(i, 0):
                        pe.wait_ge(s["xf_ready"], i + 1)
                        for g in range(GB):
                            last = nc.tensor.transpose(ps_T[:, g * T:(g + 1) * T], xf[:, g, :], ident[0:T, 0:T])
                        last.then_inc(s["xf_T"], 1)
                        pe.wait_ge(s["xf_Tc"], i + 1)
                        for g in range(GB):
                            last = nc.tensor.matmul(ps_l[:, g * E:(g + 1) * E], xfTs[:, g * T:(g + 1) * T], gate_w[:, :],
                                                    start=True, stop=True)
                        last.then_inc(s["logits"], 1)
                pipelined(pe, body, STEPS, 3, 1)

            @block.scalar
            def _(a):
                nc.scalar.preload_act_table_set("natural_log_exp_and_others")
                a.wait_ge(s["folded"], 1)
                nc.scalar.activation(wvp[:, :], ps[:, 0, 0:D], ACT.Copy).then_inc(s["unfolded"], 1)
                nc.scalar.activation(bvp[:, :], ps[0:T, 1, 0:D], ACT.Copy).then_inc(s["unfolded"], 1)
                a.wait_ge(s["scaled"], 1)

                def rsqrt(var, n, ln, mv, rstd, step, rough):
                    a.wait_ge(var, n + 1)
                    nc.scalar.activation(ln[:, :], mv[:, :, 1], ACT.Ln, bias=eps[:, 0:1]).then_inc(step, 1)
                    a.wait_ge(step, n + 1)
                    nc.scalar.activation(rstd[:, :], ln[:, :], ACT.Exp, scale=-0.5).then_inc(rough, 1)

                def body(i):
                    if has(i, 1):
                        a.wait_ge(s["sc"], i + 2)
                        nc.scalar.activation(ab[:, :], ps_sc, ACT.Abs).then_inc(s["abs_step"], 1)
                        a.wait_ge(s["abs_step"], i + 2)
                        nc.scalar.activation(ab[:, :], ab[:, :], ACT.Exp, scale=-1.0).then_inc(s["exp_step"], 1)
                        a.wait_ge(s["exp_step"], i + 2)
                        nc.scalar.activation(ab[:, :], ab[:, :], ACT.Ln, bias=1.0).then_inc(s["sp_ln"], 1)
                    if has(i, 2):
                        a.wait_ge(s["x_T"], i + 3)
                        after(a, s["v"], i + 2)
                        nc.scalar.activation(xT[:, :], ps_T, ACT.Copy).then_inc(s["x_Tc"], 1)
                    if has(i, -1):
                        a.wait_ge(s["l_sub"], i)
                        nc.scalar.activation(le[:, :, :], le[:, :, :], ACT.Exp).then_inc(s["l_exp"], 1)
                    if has(i, 0):
                        rsqrt(s["var2"], i, ln2, mv2, rstd2, s["ln2_step"], s["rough2"])
                    if has(i, 3):
                        rsqrt(s["var1"], i + 3, ln1, mv1, rstd1, s["ln1_step"], s["rough1"])
                    if has(i, 0):
                        a.wait_ge(s["xf_T"], i + 1)
                        after(a, s["logits"], i)
                        after(a, s["xfT_stored"], 16 * i)
                        nc.scalar.activation(xfTs[:, :], ps_T, ACT.Copy).then_inc(s["xf_Tc"], 1)
                pipelined(a, body, STEPS, 3, 1)

            @block.vector
            def _(v):
                v.wait_ge(s["consts_in"], 176)
                nc.vector.tensor_scalar(wkq[:, 0:2, :], wkq[:, 0:2, :], D ** -0.5, None, ALU.mult)
                nc.vector.tensor_scalar(bkq[:, 0:2], bkq[:, 0:2], D ** -0.5, None, ALU.mult)
                nc.vector.memset(eps[:, :], EPS).then_inc(s["scaled"], 1)
                v.wait_ge(s["scaled"], 1)
                v.wait_ge(s["unfolded"], 2)

                def rotate(n):
                    st = Steps(v, s["rot_step"], n)
                    v.wait_ge(s["kq"], n + 1)
                    for m, j in enumerate((0, 2)):
                        nc.vector.scalar_tensor_tensor(bat(r1[:, m, :]), bat(ps[:, 1 + j, 0:W]), bkq[:, j:j + 1],
                                                       per_image(cos[:, :], D, T), ALU.add, ALU.mult)
                        last = nc.vector.scalar_tensor_tensor(bat(r2[:, m, :]), bat(ps[:, 2 + j, 0:W]), bkq[:, j + 1:j + 2],
                                                              per_image(sin[:, :], D, T), ALU.add, ALU.mult)
                    st.link(last)
                    after(v, s["sc"], n)
                    nc.vector.tensor_tensor(kT[:, :], r1[:, 0, :], r2[:, 0, :], ALU.add)
                    nc.vector.tensor_tensor(qT[:, :], r1[:, 1, :], r2[:, 1, :], ALU.add).then_inc(s["kq_rot"], 1)

                def body(i):
                    if has(i, 1):
                        rotate(i + 1)
                        v.wait_ge(s["v"], i + 2)
                        after(v, s["out"], i + 1)
                        nc.vector.tensor_tensor(vv[:, :, :], rows(ps_v), per_image(bvp[:, :], T, D), ALU.add).then_inc(s["vv_ready"], 1)
                    if has(i, -1):
                        st = Steps(v, s["max_step"], i - 1)
                        v.wait_ge(s["logits"], i)
                        lg = ps_l.rearrange("p (g e) -> p g e", g=GB)
                        st.link(nc.vector.tensor_reduce(lm[:, :], lg, AX.X, ALU.max))
                        nc.vector.tensor_tensor(le[:, :, :], lg, lm[:, :].unsqueeze(2).to_broadcast([T, GB, E]),
                                                ALU.subtract).then_inc(s["l_sub"], 1)
                    if has(i, 2):
                        v.wait_ge(s["rstd1"], i + 3)
                        after(v, s["x_T"], i + 2)
                        for g in range(GB):
                            last = nc.vector.tensor_scalar(xn[:, g, :], x[:, g, :], mv1[:, g, 0:1], rstd1[:, g:g + 1], ALU.subtract, ALU.mult)
                        last.then_inc(s["normed"], 1)
                    if has(i, 0):
                        v.wait_ge(s["out"], i + 1)
                        v.wait_ge(s["xb_ready"], i + 1)
                        after(v, s["h_stored"], 16 * i)
                        nc.vector.tensor_tensor(h[:, :, :], rows(ps_out), xr[:, :, :], ALU.add).then_inc(s["h_ready"], 1)
                        v.wait_ge(s["h_ready"], i + 1)
                        row_stats(nc, v, s["stat2_step"], i, gate2[:, :], h, stats2, mv2, s["var2"])
                    if has(i, 1):
                        v.wait_ge(s["sp_ln"], i + 2)
                        after(v, s["wei_ready"], i + 1)
                        nc.vector.scalar_tensor_tensor(raw[:, :], ps_sc, 0.0, ab[:, :], ALU.max, ALU.add).then_inc(s["wei_raw"], 1)
                    if has(i, -1):
                        st = Steps(v, s["sum_step"], 2 * (i - 1))
                        v.wait_ge(s["l_exp"], i)
                        st.link(nc.vector.tensor_reduce(ls[:, :], le[:, :, :], AX.X, ALU.add))
                        st.link(nc.vector.reciprocal(ls[:, :], ls[:, :]))
                        after(v, s["pb_stored"], 32 * (i - 1))
                        nc.vector.tensor_tensor(pb[:, :, :], le[:, :, :], ls[:, :].unsqueeze(2).to_broadcast([T, GB, E]),
                                                ALU.mult).then_inc(s["pb_ready"], 1)
                    if has(i, 3):
                        v.wait_ge(s["x_in"], 16 * i + 64)
                        row_stats(nc, v, s["stat1_step"], i + 3, gate1[:, :], x, stats1, mv1, s["var1"])
                    if has(i, 0):
                        v.wait_ge(s["rstd2"], i + 1)
                        after(v, s["xf_T"], i)
                        after(v, s["xf_stored"], 16 * i)
                        for g in range(GB):
                            last = nc.vector.tensor_scalar(xf[:, g, :], h[:, g, :], mv2[:, g, 0:1], rstd2[:, g:g + 1], ALU.subtract, ALU.mult)
                        last.then_inc(s["xf_ready"], 1)
                pipelined(v, body, STEPS, 3, 1)


def attend1(nc, d, src, dst):
    with ExitStack() as ctx:
        def sb(name, shape, dt=F32):
            return ctx.enter_context(nc.sbuf_tensor("a1_" + name, shape, dt))
        wq = sb("wq", [D, D]); wk = sb("wk", [D, D]); wo = sb("wo", [D, D]); bqk = sb("bqk", [D, 2])
        rows1 = sb("rows1", [T, 3, D])
        bound = sb("bound", [T, T]); thirds = sb("thirds", [T, 2, GB])
        ident = sb("ident", [P, P])
        x = sb("x", [T, GB, D]); xr = sb("xr", [T, GB, D]); xn = sb("xn", [T, GB, D]); xb = sb("xb", [T, GB, D]); xb2 = sb("xb2", [T, GB, D])
        stats1 = sb("stats1", [T, GB, 6]); mv1 = sb("mv1", [T, GB, 2]); ln1 = sb("ln1", [T, GB]); rstd1 = sb("rstd1", [T, GB])
        stats2 = sb("stats2", [T, GB, 6]); mv2 = sb("mv2", [T, GB, 2]); ln2 = sb("ln2", [T, GB]); rstd2 = sb("rstd2", [T, GB])
        gate1 = sb("gate1", [T, 1]); gate2 = sb("gate2", [T, 1]); c15 = sb("c15", [T, GB]); eps = sb("eps", [T, 1])
        xT = sb("xT", [D, W]); qT = sb("qT", [D, W]); kT = sb("kT", [D, W]); u = sb("u", [T, GB, D])
        near = sb("near", [T, GB, T]); m = sb("m", [T, 2, GB]); ex = sb("ex", [T, 2, GB, T]); es = sb("es", [T, 2, GB])
        A = sb("A", [T, GB, T]); AT = sb("AT", [T, W]); res = sb("res", [T, GB, D]); y = sb("y", [T, GB, D]); h = sb("h", [T, GB, D])
        ps = ctx.enter_context(nc.psum_tensor("a1_ps", [P, 8, 512], F32))
        ps_xT, ps_q, ps_k, ps_u, ps_sc = ps[:, 0, 0:W], ps[:, 1, 0:W], ps[:, 2, 0:W], ps[0:T, 3, :], ps[0:T, 4, 0:W]
        ps_AT, ps_out = ps[0:T, 5, 0:W], ps[0:T, 6, :]
        s = ctx.enter_context(semaphores(nc, "a1_", """consts_in ready scaled x_in xr_in var1 rough1 rstd1 normed x_T x_Tc qk qk_c u u_c sc near_step max_step m_ready e_out
             recip_step third_step full_step A A_T A_Tc out xb_ready xb_moved res_ready var2 rough2 rstd2 y_ready beta_step gamma_step
             h_ready stored stat1_step stat2_step ln1_step ln2_step newton1_step newton2_step"""))
        rows_in = src.rearrange("(b t) c -> t b c", t=T)
        rows_h = dst.rearrange("(b t) c -> t b c", t=T)
        bat = lambda ap: ap.rearrange("p (g t) -> p g t", g=GB)
        rows = lambda ap: ap.rearrange("p (g c) -> p g c", g=GB)
        per_image = lambda ap, m: ap.unsqueeze(1).to_broadcast([T, GB, m])
        has = lambda i, ahead: not isinstance(i, int) or 0 <= i + ahead < STEPS
        with nc.Block() as block:
            @block.sync
            def _(sp):
                for to, name in ((wq, "wq1"), (wk, "wk1"), (wo, "wo1"), (bqk, "b_qk1"), (rows1, "rows1"), (bound, "bound"),
                                 (thirds, "thirds"), (ident, "ident")):
                    sp.dma_start(to[:], d[name]).then_inc(s["consts_in"], 16)

                def body(i):
                    if has(i, 3):
                        after(sp, s["normed"], i + 3)
                        sp.dma_start(x[:, :, :], rows_in[:, bass.ds((i + 3) * GB, GB), :]).then_inc(s["x_in"], 16)
                    if has(i, -1):
                        sp.wait_ge(s["h_ready"], i)
                        sp.dma_start(rows_h[:, bass.ds((i - 1) * GB, GB), :], h[:, :, :]).then_inc(s["stored"], 16)
                    if has(i, 0):
                        sp.dma_start(xr[:, :, :], rows_in[:, bass.ds(i * GB, GB), :]).then_inc(s["xr_in"], 16)
                pipelined(sp, body, STEPS, 3, 1)
                sp.wait_ge(s["stored"], 16 * STEPS)

            @block.gpsimd
            def _(pool):
                nc.gpsimd.memset(c15[:, :], 1.5).then_inc(s["ready"], 1)
                pool.wait_ge(s["ready"], 1)
                pool.wait_ge(s["consts_in"], 128)

                def body(i):
                    if has(i, -1):
                        pool.wait_ge(s["xr_in"], 16 * i)
                        nc.gpsimd.tensor_tensor(xr[:, :, :], xr[:, :, :], per_image(rows1[:, 2, :], D), ALU.add).then_inc(s["beta_step"], 1)
                        pool.wait_ge(s["y_ready"], i)
                        nc.gpsimd.tensor_tensor(y[:, :, :], y[:, :, :], per_image(rows1[:, 1, :], D), ALU.mult).then_inc(s["gamma_step"], 1)
                        pool.wait_ge(s["gamma_step"], i)
                        pool.wait_ge(s["beta_step"], i)
                        after(pool, s["stored"], 16 * (i - 1))
                        nc.gpsimd.tensor_tensor(h[:, :, :], y[:, :, :], xr[:, :, :], ALU.add).then_inc(s["h_ready"], 1)
                    if has(i, 2):
                        pool.wait_ge(s["normed"], i + 3)
                        after(pool, s["xb_moved"], i + 2)
                        nc.gpsimd.tensor_tensor(xb[:, :, :], xn[:, :, :], per_image(rows1[:, 0, :], D), ALU.add).then_inc(s["xb_ready"], 1)
                    if has(i, 0):
                        newton_rsqrt(nc, pool, s["newton2_step"], s["rough2"], i, rstd2[:, :], ln2[:, :], mv2[:, :, 1], c15[:, :], 1.0, EPS, s["rstd2"])
                    if has(i, 3):
                        newton_rsqrt(nc, pool, s["newton1_step"], s["rough1"], i + 3, rstd1[:, :], ln1[:, :], mv1[:, :, 1], c15[:, :], 1.0, EPS, s["rstd1"])
                pipelined(pool, body, STEPS, 3, 1)

            @block.tensor
            def _(pe):
                pe.wait_ge(s["consts_in"], 128)
                pe.wait_ge(s["scaled"], 1)

                def body(i):
                    if has(i, 2):
                        pe.wait_ge(s["normed"], i + 3)
                        for g in range(GB):
                            last = nc.tensor.transpose(ps_xT[:, g * T:(g + 1) * T], xn[:, g, :], ident[0:T, 0:T])
                        last.then_inc(s["x_T"], 1)
                        pe.wait_ge(s["x_Tc"], i + 3)
                        nc.tensor.matmul(ps_q, wq[:, :], xT[:, :], start=True, stop=True)
                        nc.tensor.matmul(ps_k, wk[:, :], xT[:, :], start=True, stop=True).then_inc(s["qk"], 1)
                        after(pe, s["u_c"], i + 2)
                        for g in range(GB):
                            last = nc.tensor.matmul(ps_u[:, g * D:(g + 1) * D], xT[:, g * T:(g + 1) * T], wo[:, :],
                                                    start=True, stop=True)
                        last.then_inc(s["u"], 1)
                    if has(i, 2):
                        pe.wait_ge(s["qk_c"], i + 3)
                        after(pe, s["e_out"], i + 2)
                        for g in range(GB):
                            c = slice(g * T, (g + 1) * T)
                            last = nc.tensor.matmul(ps_sc[:, c], qT[:, c], kT[:, c], start=True, stop=True)
                        last.then_inc(s["sc"], 1)
                    if has(i, 1):
                        pe.wait_ge(s["A"], i + 2)
                        for g in range(GB):
                            last = nc.tensor.transpose(ps_AT[:, g * T:(g + 1) * T], A[:, g, :], ident[0:T, 0:T])
                        last.then_inc(s["A_T"], 1)
                        pe.wait_ge(s["A_Tc"], i + 2)
                        pe.wait_ge(s["u_c"], i + 2)
                        after(pe, s["res_ready"], i + 1)
                        for g in range(GB):
                            last = nc.tensor.matmul(ps_out[:, g * D:(g + 1) * D], AT[:, g * T:(g + 1) * T], u[:, g, :],
                                                    start=True, stop=True)
                        last.then_inc(s["out"], 1)
                pipelined(pe, body, STEPS, 3, 1)

            @block.scalar
            def _(a):
                nc.scalar.preload_act_table_set("natural_log_exp_and_others")
                a.wait_ge(s["consts_in"], 128)
                a.wait_ge(s["scaled"], 1)

                def rsqrt(var, n, ln, mv, rstd, step, rough):
                    a.wait_ge(var, n + 1)
                    nc.scalar.activation(ln[:, :], mv[:, :, 1], ACT.Ln, bias=eps[:, 0:1]).then_inc(step, 1)
                    a.wait_ge(step, n + 1)
                    nc.scalar.activation(rstd[:, :], ln[:, :], ACT.Exp, scale=-0.5).then_inc(rough, 1)

                def body(i):
                    if has(i, 2):
                        a.wait_ge(s["x_T"], i + 3)
                        after(a, s["u"], i + 2)
                        nc.scalar.activation(xT[:, :], ps_xT, ACT.Copy).then_inc(s["x_Tc"], 1)
                    if has(i, 1):
                        a.wait_ge(s["m_ready"], i + 2)
                        after(a, s["A"], i + 1)
                        for g in range(GB):
                            nc.scalar.activation(ex[:, 0, g, :], ps_sc[:, g * T:(g + 1) * T], ACT.Exp, bias=m[:, 0, g:g + 1],
                                                 accum_out=es[:, 0, g:g + 1])
                            last = nc.scalar.activation(ex[:, 1, g, :], near[:, g, :], ACT.Exp, bias=m[:, 1, g:g + 1],
                                                        accum_out=es[:, 1, g:g + 1])
                        last.then_inc(s["e_out"], 1)
                    if has(i, 0):
                        rsqrt(s["var2"], i, ln2, mv2, rstd2, s["ln2_step"], s["rough2"])
                    if has(i, 2):
                        a.wait_ge(s["qk"], i + 3)
                        after(a, s["sc"], i + 2)
                        nc.scalar.activation(qT[:, :], ps_q, ACT.Identity, bias=bqk[:, 0:1])
                        nc.scalar.activation(kT[:, :], ps_k, ACT.Identity, bias=bqk[:, 1:2]).then_inc(s["qk_c"], 1)
                    if has(i, 3):
                        rsqrt(s["var1"], i + 3, ln1, mv1, rstd1, s["ln1_step"], s["rough1"])
                    if has(i, 1):
                        a.wait_ge(s["xb_ready"], i + 2)
                        after(a, s["res_ready"], i + 1)
                        nc.scalar.activation(xb2[:, :, :], xb[:, :, :], ACT.Copy).then_inc(s["xb_moved"], 1)
                        a.wait_ge(s["A_T"], i + 2)
                        after(a, s["out"], i + 1)
                        nc.scalar.activation(AT[:, :], ps_AT, ACT.Copy).then_inc(s["A_Tc"], 1)
                    if has(i, 2):
                        a.wait_ge(s["u"], i + 3)
                        after(a, s["out"], i + 2)
                        nc.scalar.activation(u[:, :, :].rearrange("p g c -> p (g c)"), ps_u, ACT.Copy).then_inc(s["u_c"], 1)
                pipelined(a, body, STEPS, 3, 1)

            @block.vector
            def _(v):
                v.wait_ge(s["consts_in"], 128)
                nc.vector.tensor_scalar(wq[:, :], wq[:, :], D ** -0.5, None, ALU.mult)
                nc.vector.tensor_scalar(bqk[:, 0:1], bqk[:, 0:1], D ** -0.5, None, ALU.mult)
                nc.vector.memset(eps[:, :], EPS).then_inc(s["scaled"], 1)
                v.wait_ge(s["scaled"], 1)

                def body(i):
                    if has(i, 2):
                        v.wait_ge(s["rstd1"], i + 3)
                        after(v, s["x_T"], i + 2)
                        after(v, s["xb_ready"], i + 2)
                        for g in range(GB):
                            last = nc.vector.tensor_scalar(xn[:, g, :], x[:, g, :], mv1[:, g, 0:1], rstd1[:, g:g + 1], ALU.subtract, ALU.mult)
                        last.then_inc(s["normed"], 1)
                    if has(i, 1):
                        v.wait_ge(s["sc"], i + 2)
                        after(v, s["e_out"], i + 1)
                        nc.vector.tensor_reduce(m[:, 0, :], bat(ps_sc), AX.X, ALU.max)
                        nc.vector.tensor_tensor(near[:, :, :], bat(ps_sc), per_image(bound[:, :], T), ALU.min).then_inc(s["near_step"], 1)
                        v.wait_ge(s["near_step"], i + 2)
                        nc.vector.tensor_reduce(m[:, 1, :], near[:, :, :], AX.X, ALU.max).then_inc(s["max_step"], 1)
                        v.wait_ge(s["max_step"], i + 2)
                        nc.vector.tensor_scalar(m[:, :, :], m[:, :, :], -1.0, None, ALU.mult).then_inc(s["m_ready"], 1)
                    if has(i, 0):
                        v.wait_ge(s["out"], i + 1)
                        v.wait_ge(s["xb_moved"], i + 1)
                        after(v, s["y_ready"], i)
                        nc.vector.tensor_tensor(res[:, :, :], rows(ps_out), xb2[:, :, :], ALU.add).then_inc(s["res_ready"], 1)
                        v.wait_ge(s["res_ready"], i + 1)
                        row_stats(nc, v, s["stat2_step"], i, gate2[:, :], res, stats2, mv2, s["var2"])
                    if has(i, 3):
                        v.wait_ge(s["x_in"], 16 * i + 64)
                        row_stats(nc, v, s["stat1_step"], i + 3, gate1[:, :], x, stats1, mv1, s["var1"])
                    if has(i, 1):
                        v.wait_ge(s["e_out"], i + 2)
                        after(v, s["A_T"], i + 1)
                        nc.vector.reciprocal(es[:, :, :], es[:, :, :]).then_inc(s["recip_step"], 1)
                        v.wait_ge(s["recip_step"], i + 2)
                        nc.vector.tensor_tensor(es[:, :, :], es[:, :, :], thirds[:, :, :], ALU.mult).then_inc(s["third_step"], 1)
                        v.wait_ge(s["third_step"], i + 2)
                        for g in range(GB):
                            last = nc.vector.tensor_scalar(ex[:, 0, g, :], ex[:, 0, g, :], es[:, 0, g:g + 1], None, ALU.mult)
                        last.then_inc(s["full_step"], 1)
                        v.wait_ge(s["full_step"], i + 2)
                        for g in range(GB):
                            last = nc.vector.scalar_tensor_tensor(A[:, g, :], ex[:, 1, g, :], es[:, 1, g:g + 1], ex[:, 0, g, :], ALU.mult, ALU.add)
                        last.then_inc(s["A"], 1)
                    if has(i, 0):
                        v.wait_ge(s["rstd2"], i + 1)
                        after(v, s["h_ready"], i)
                        for g in range(GB):
                            last = nc.vector.tensor_scalar(y[:, g, :], res[:, g, :], mv2[:, g, 0:1], rstd2[:, g:g + 1], ALU.subtract, ALU.mult)
                        last.then_inc(s["y_ready"], 1)

                pipelined(v, body, STEPS, 3, 1)


def attention_layout(i):
    c_ = np.ascontiguousarray
    W_ = i['L0_tok_W']
    pos = i['L0_tok_pos_embed']
    xp = i['x'].reshape(16, 8, 3, 8, 28, 8, 28).transpose(0, 2, 4, 6, 1, 3, 5).reshape(16, 2352, 512)
    sw = np.arange(128) ^ 1
    t = np.arange(T - 1, -1, -1)[None, :]
    ang = (t * (np.arange(128)[:, None] // 2)).astype(np.float64)
    sg = np.where(np.arange(128) % 2 == 0, -1.0, 1.0)[:, None]
    Wk, Wq, bk, bq = i['L0_attn_Wk'], i['L0_attn_Wq'], i['L0_attn_bk'], i['L0_attn_bq']
    tt = np.arange(T)
    return dict(
        w_tok=c_(W_.T[:18 * 128].reshape(18, 128, 128).transpose(1, 0, 2)), w_tok_rest=c_(W_.T[18 * 128:]),
        b_tok=c_(i['L0_tok_b'][:, None]), pos_cols=c_(pos.T), cls_col=c_(i['L0_tok_class_token'].T),
        x_main=c_(xp[:, :18 * 128].reshape(16, 18, 128, 512).transpose(0, 2, 1, 3)), x_rest=c_(xp[:, 18 * 128:]),
        ident=np.eye(128, dtype=np.float32),
        w_kq=c_(np.stack([Wk, Wk[:, sw], Wq, Wq[:, sw]], 1)), b_kq=c_(np.stack([bk, bk[sw], bq, bq[sw]], 1)),
        wvT=c_(i['L0_attn_Wv'].T), wp=c_(i['L0_attn_Wp']), bv_cols=c_(np.broadcast_to(i['L0_attn_bv'][:, None], (128, T))),
        bp_rows=c_(np.broadcast_to(i['L0_attn_bp'], (T, 128))), gate_w=c_(i['L0_ffn_gate_w']),
        cos=np.cos(ang).astype(np.float32), sin=(sg * np.sin(ang)).astype(np.float32), tri=np.triu(np.ones((T, T), np.float32)),
        wq1=c_(i['L1_attn_Wq']), wk1=c_(i['L1_attn_Wk']), wo1=c_(i['L1_attn_Wo']), b_qk1=c_(np.stack([i['L1_attn_bq'], i['L1_attn_bk']], 1)),
        rows1=c_(np.broadcast_to(np.stack([i['L1_attn_bo'], i['L1_attn_gamma'], i['L1_attn_beta']]), (T, 3, 128))),
        bound=np.where(abs(tt[:, None] - tt[None, :]) <= 12, np.float32(3.4e38), np.float32(-1e9)),
        thirds=c_(np.broadcast_to(np.array([2 / 3, 1 / 3], np.float32)[None, :, None], (T, 2, GB))))


E_ = 16
TILES = N // P
CAP = N // E_
CC, CP = 5, 104
HID = 512
PARTS = [(0, 5), (5, 5), (10, 6)]


def route(nc, d, probs, lists, cap=CAP):
    with ExitStack() as ctx:
        def sb(name, shape, dt=F32):
            return ctx.enter_context(nc.sbuf_tensor("rt_" + name, shape, dt))
        s = ctx.enter_context(semaphores(nc, "rt_", "consts_in p_in step cnt total masks eq_sums sel sel_sums hots list_mm list_read stored"))
        A3 = lambda n, dt=F32: sb(n, [P, E_, TILES], dt)
        raw = sb("raw", [P, TILES, E_])
        pr = A3("pr"); gt = A3("gt"); eq = A3("eq"); tot = A3("tot"); rank = A3("rank"); off = A3("off"); hi = A3("hi")
        lo_b = A3("lo_b", BF16); hi_b = A3("hi_b", BF16)
        carry = sb("carry", [P, E_ * TILES])
        ones = sb("ones", [P, P]); below = sb("below", [P, P])
        iota_lo = sb("iota_lo", [P, CP], BF16); iota_f = sb("iota_f", [P, CP]); tile_no = sb("tile_no", [P, TILES]); pid = sb("pid", [P, 1])
        thr = sb("thr", [P, E_]); cand = sb("cand", [P, E_]); kept = sb("kept", [P, E_]); bit = sb("bit", [P, E_], I32)
        cnt = sb("cnt", [P, E_]); need = sb("need", [P, E_])
        hot_lo = sb("hot_lo", [P, 2, TILES, CP], BF16)
        hot_hi = sb("hot_hi", [P, 2, TILES, CC], BF16)
        ids = sb("ids", [P, 2, TILES, 2 * CC], BF16)
        lf = sb("lf", [CP, E_, CC]); lt = sb("lt", [CP, CC])
        lists_sb = sb("lists", [CP, E_, CC], U32)
        ps = ctx.enter_context(nc.psum_tensor("rt_ps", [P, 8, 512], F32))
        flat = lambda t: t[:, :, :].rearrange("p e t -> p (e t)")
        eb = lambda t: t[:, :].unsqueeze(2).to_broadcast([P, E_, TILES])
        bank = lambda k, n: ps[:, k, 0:n * TILES].rearrange("p (e t) -> p e t", t=TILES)
        with nc.Block() as block:
            @block.sync
            def _(sp):
                for to, name in ((ones, "ones"), (below, "below"), (iota_f, "iota_lo"), (tile_no, "tile_no"), (pid, "pid"),
                                 (carry, "carry"), (bit, "first_bit")):
                    sp.dma_start(to[:], d[name]).then_inc(s["consts_in"], 16)
                sp.dma_start(raw[:, :, :], probs.rearrange("(t p) e -> p t e", p=P)).then_inc(s["p_in"], 16)
                sp.wait_ge(s["list_read"], E_)
                sp.dma_start(lists, lists_sb[:, :, :]).then_inc(s["stored"], 16)
                sp.wait_ge(s["stored"], 16)

            @block.tensor
            def _(pe):
                pe.wait_ge(s["consts_in"], 112)
                with pe.Fori(0, 31) as i:
                    pe.wait_ge(s["cnt"], i + 1)
                    nc.tensor.matmul(ps[:, 6, 0:E_], ones[:, :], cnt[:, :], start=True, stop=True).then_inc(s["total"], 1)

                def sums(m):
                    for k, (e0, n) in enumerate(PARTS):
                        c = m[:, e0:e0 + n, :].rearrange("p e t -> p (e t)")
                        nc.tensor.matmul(ps[:, k, 0:n * TILES], below[:, :], c, start=True, stop=True)
                        last = nc.tensor.matmul(ps[:, 3 + k, 0:n * TILES], ones[:, :], c, start=True, stop=True)
                    return last
                sums(eq).then_inc(s["eq_sums"], 1)
                pe.wait_ge(s["sel"], 1)
                sums(gt).then_inc(s["sel_sums"], 1)
                with pe.Fori(0, E_ // 2) as j:
                    for k in range(2):
                        pe.wait_ge(s["hots"], 2 * j + k + 1)
                        pe.wait_ge(s["list_read"], 2 * j + k)
                        for t in range(TILES):
                            last = nc.tensor.matmul(ps[0:CP, 7, 0:2 * CC], hot_lo[:, k, t, :], ids[:, k, t, :],
                                                    start=(t == 0), stop=(t == TILES - 1))
                        last.then_inc(s["list_mm"], 1)

            @block.vector
            def _(v):
                v.wait_ge(s["consts_in"], 112)
                v.wait_ge(s["p_in"], 16)
                one = Steps(v, s["step"])
                one.mark(nc.vector.memset(thr[:, :], 0.0))
                nc.vector.tensor_copy(iota_lo[:, :], iota_f[:, :])
                one.link(nc.vector.tensor_copy(pr[:, :, :], raw[:, :, :].rearrange("p t e -> p e t")))
                PER = 5
                base = one.n
                with v.Fori(0, 30) as i:
                    st = Steps(v, s["step"], PER * i + base)
                    st.link(nc.vector.tensor_tensor(cand[:, :].bitcast(I32), thr[:, :].bitcast(I32), bit[:, :], ALU.bitwise_or))
                    st.mark(nc.vector.tensor_scalar(bit[:, :], bit[:, :], 1, None, ALU.logical_shift_right))
                    st.link(nc.vector.tensor_tensor(gt[:, :, :], pr[:, :, :], eb(cand), ALU.is_ge))
                    nc.vector.tensor_reduce(cnt[:, :], gt[:, :, :], AX.X, ALU.add).then_inc(s["cnt"], 1)
                    v.wait_ge(s["total"], i + 1)
                    st.link(nc.vector.scalar_tensor_tensor(kept[:, :], ps[:, 6, 0:E_], cap - 0.5, cand[:, :], ALU.is_gt, ALU.mult))
                    st.link(nc.vector.tensor_tensor(thr[:, :], thr[:, :], kept[:, :], ALU.max))
                    assert st.n == PER
                st = Steps(v, s["step"], PER * 30 + base)
                st.mark(nc.vector.tensor_tensor(eq[:, :, :], pr[:, :, :], eb(thr), ALU.is_equal))
                st.link(nc.vector.tensor_tensor(gt[:, :, :], pr[:, :, :], eb(thr), ALU.is_gt))
                nc.vector.tensor_reduce(cnt[:, :], gt[:, :, :], AX.X, ALU.add).then_inc(s["cnt"], 1)
                v.wait_ge(s["total"], 31)
                st.link(nc.vector.tensor_scalar(need[:, :], ps[:, 6, 0:E_], -1.0, float(cap), ALU.mult, ALU.add))

                def ranks():
                    for k, (e0, n) in enumerate(PARTS):
                        last = nc.vector.tensor_copy(tot[:, e0:e0 + n, :], bank(3 + k, n))
                    st.link(last)
                    st.link(nc.vector.tensor_tensor_scan(flat(off), carry[:, :], flat(tot), 0.0, ALU.mult, ALU.add))
                    st.link(nc.vector.tensor_tensor(off[:, :, :], off[:, :, :], tot[:, :, :], ALU.subtract))
                    for k, (e0, n) in enumerate(PARTS):
                        last = nc.vector.tensor_tensor(rank[:, e0:e0 + n, :], bank(k, n), off[:, e0:e0 + n, :], ALU.add)
                    st.link(last)
                v.wait_ge(s["eq_sums"], 1)
                ranks()
                st.link(nc.vector.tensor_tensor(rank[:, :, :], rank[:, :, :], eb(need), ALU.is_lt))
                st.link(nc.vector.tensor_tensor(eq[:, :, :], eq[:, :, :], rank[:, :, :], ALU.mult))
                nc.vector.tensor_tensor(gt[:, :, :], gt[:, :, :], eq[:, :, :], ALU.add).then_inc(s["sel"], 1)
                v.wait_ge(s["sel_sums"], 1)
                ranks()
                st.link(nc.vector.tensor_scalar(eq[:, :, :], gt[:, :, :], -2.0 * N, 2.0 * N, ALU.mult, ALU.add))
                st.link(nc.vector.tensor_tensor(rank[:, :, :], rank[:, :, :], eq[:, :, :], ALU.add))
                st.link(nc.vector.tensor_scalar(hi[:, :, :], rank[:, :, :], float(CP), None, ALU.is_ge))
                for k in range(2, CC):
                    st.link(nc.vector.scalar_tensor_tensor(hi[:, :, :], rank[:, :, :], float(CP * k), hi[:, :, :], ALU.is_ge, ALU.add))
                nc.vector.tensor_copy(hi_b[:, :, :], hi[:, :, :])
                st.link(nc.vector.scalar_tensor_tensor(lo_b[:, :, :], hi[:, :, :], -float(CP), rank[:, :, :], ALU.mult, ALU.add))
                base2, PER2 = st.base + st.n, 8
                with v.Fori(0, E_ // 2) as j:
                    st = Steps(v, s["step"], PER2 * j + base2)

                    def hots(k):
                        v.wait_ge(s["list_mm"], 2 * j + k) if k == 0 else None
                        e = 2 * j + k
                        lo_e = lo_b[:, bass.ds(e, 1), :].rearrange("p a t -> p (a t)").unsqueeze(2).to_broadcast([P, TILES, CP])
                        hi_e = hi_b[:, bass.ds(e, 1), :].rearrange("p a t -> p (a t)").unsqueeze(2).to_broadcast([P, TILES, CC])
                        st.mark(nc.vector.tensor_tensor(hot_lo[:, k], lo_e, iota_lo[:, :].unsqueeze(1).to_broadcast([P, TILES, CP]), ALU.is_equal))
                        st.link(nc.vector.tensor_tensor(hot_hi[:, k], hi_e, iota_lo[:, 0:CC].unsqueeze(1).to_broadcast([P, TILES, CC]), ALU.is_equal))
                        nc.vector.tensor_scalar(ids[:, k, :, 0:CC], hot_hi[:, k], pid[:, 0:1], None, ALU.mult)
                        nc.vector.tensor_tensor(ids[:, k, :, CC:2 * CC], hot_hi[:, k],
                                                tile_no[:, :].unsqueeze(2).to_broadcast([P, TILES, CC]), ALU.mult).then_inc(s["hots"], 1)

                    def read(k):
                        v.wait_ge(s["list_mm"], 2 * j + k + 1)
                        st.link(nc.vector.tensor_scalar(lt[:, :], ps[0:CP, 7, CC:2 * CC], float(P), None, ALU.mult))
                        st.mark(nc.vector.tensor_tensor(lists_sb[:, bass.ds(2 * j + k, 1), :].rearrange("p a c -> p (a c)"),
                                                ps[0:CP, 7, 0:CC], lt[:, :], ALU.add))
                        st.wait()
                        nc.vector.memset(lt[:, :], 0.0).then_inc(s["list_read"], 1)
                    hots(0)
                    hots(1)
                    read(0)
                    read(1)
                    assert st.n == PER2, st.n


def experts(nc, d, h1, table, xfT, lists, h2):
    HALF = CAP // 2
    PK_ = HID + HID + 4 + D
    with ExitStack() as ctx:
        def sb(name, shape, dt=F32):
            return ctx.enter_context(nc.sbuf_tensor("ex_" + name, shape, dt))
        s = ctx.enter_context(semaphores(nc, "ex_", "consts_in w_in0 w_in1 xT_in h1_in up gelu down y_ready stored idx tok_in0 tok_in1 pool_gate tok_T tok_Tc scattered mlp_done score step"))
        w_s = sb("w_s", [P, PK_]); w_e = sb("w_e", [P, 2, PK_])
        xT = sb("xT", [D, 2, CAP]); hT = sb("hT", [P, 4, CAP])
        h1_s = sb("h1_s", [CP, 2, CC, D]); y = sb("y", [CP, 2, CC, D])
        lists_sb = sb("lists", [CP, E_, CC], U32); idx = sb("idx", [CP, 2, CC], U32)
        tok = sb("tok", [CP, 2, CC, D + E_]); score = sb("score", [CP, CC])
        ident = sb("ident", [P, P])
        gate_in = sb("gate_in", [16, 1]); gate_out = sb("gate_out", [16, 1])
        ps = ctx.enter_context(nc.psum_tensor("ex_ps", [P, 8, 512], F32))
        parts = lambda w: (w[:, 0:HID], w[:, HID:2 * HID].rearrange("p (j c) -> p j c", j=4), w[:, 2 * HID:2 * HID + 4],
                           w[0:CP, 2 * HID + 4:])

        def mlp_pe(pe, n, w, x):
            w1, w2, _, _ = parts(w)
            for j in range(4):
                if j >= 2:
                    pe.wait_ge(s["gelu"], 4 * n + j - 1)
                for k in range(2):
                    last = nc.tensor.matmul(ps[:, 2 * (j % 2) + k, 0:HALF], w1[:, j * P:(j + 1) * P], x[:, k * HALF:(k + 1) * HALF],
                                            start=True, stop=True)
                last.then_inc(s["up"], 1)
            pe.wait_ge(s["gelu"], 4 * n + 4)
            pe.wait_ge(s["y_ready"], n)
            for c in range(CC):
                for j in range(4):
                    last = nc.tensor.matmul(ps[0:CP, 4 + c // 4, (c % 4) * D:(c % 4 + 1) * D], hT[:, j, c * CP:(c + 1) * CP],
                                            w2[:, j, :], start=(j == 0), stop=(j == 3))
            last.then_inc(s["down"], 1)

        def mlp_act(a, n, w):
            b1 = parts(w)[2]
            for j in range(4):
                a.wait_ge(s["up"], 4 * n + j + 1)
                if j == 0:
                    a.wait_ge(s["down"], n)
                nc.scalar.activation(hT[:, j, :].rearrange("p (k c) -> p k c", k=2), ps[:, 2 * (j % 2):2 * (j % 2) + 2, 0:HALF],
                                     ACT.Gelu_apprx_tanh, bias=b1[:, j:j + 1]).then_inc(s["gelu"], 1)
        chunk_sets = ((4, 0, 4), (5, 4, 1))
        h1r = h1.rearrange("(i c p) k -> p i c k", c=CC, p=CP)
        h2r = h2.rearrange("(i c p) k -> p i c k", c=CC, p=CP)
        with nc.Block() as block:
            @block.sync
            def _(sp):
                sp.dma_start(w_s[:, :], d["w_ffn"][E_]).then_inc(s["consts_in"], 16)
                sp.dma_start(ident[:, :], d["ident"]).then_inc(s["consts_in"], 16)
                sp.dma_start(lists_sb[:, :, :], lists).then_inc(s["consts_in"], 16)
                with sp.Fori(0, E_ // 2) as g:
                    for k in range(2):
                        i = 2 * g + k
                        sp.wait_ge(s["y_ready"], 2 * g)
                        sp.dma_start(xT[:, k, :], xfT[:, bass.ds(i * CAP, CAP)]).then_inc(s["xT_in"], 16)
                        sp.dma_start(h1_s[:, k], h1r[:, bass.ds(i, 1)].rearrange("p i c k -> p (i c) k")).then_inc(s["h1_in"], 16)
                    for k in range(2):
                        i = 2 * g + k
                        sp.wait_ge(s["y_ready"], i + 1)
                        sp.dma_start(h2r[:, bass.ds(i, 1)].rearrange("p i c k -> p (i c) k"), y[:, k]).then_inc(s["stored"], 16)
                with sp.Fori(0, E_ // 2) as g:
                    for k in range(2):
                        sp.wait_ge(s["y_ready"], E_ + 2 * g)
                        sp.dma_start(w_e[:, k], d["w_ffn"][bass.ds(2 * g + k, 1)].rearrange("e p c -> (e p) c")).then_inc(s[f"w_in{k}"], 16)

            @block.gpsimd
            def _(pool):
                nc.gpsimd.memset(gate_in[:, :], 0.0).then_inc(s["pool_gate"], 1)
                pool.wait_ge(s["pool_gate"], 1)

                def gate(n):
                    pool.wait_ge(s["pool_gate"], n + 1)
                    nc.gpsimd.tensor_tensor(gate_out[:, :], gate_in[:, :], gate_in[:, :], ALU.add).then_inc(s["pool_gate"], 1)

                def gather(e, k):
                    pool.wait_ge(s["idx"], e + 1)
                    gate(2 * e - k)
                    for c in range(CC):
                        pool.indirect_dma_start(out=tok[:, k, c, :], out_offset=None, in_=table[:, :],
                                                in_offset=bass.IndirectOffsetOnAxis(ap=idx[:, k, c:c + 1], axis=0)).then_inc(s[f"tok_in{k}"], 16)

                def scatter(e, k):
                    pool.wait_ge(s["y_ready"], E_ + e + 1)
                    pool.wait_ge(s["scattered"], 16 * CC * e)
                    gate(2 * e - k + 2)
                    for c in range(CC):
                        pool.indirect_dma_start(out=h2[:, :], out_offset=bass.IndirectOffsetOnAxis(ap=idx[:, k, c:c + 1], axis=0),
                                                in_=y[:, k, c, :], in_offset=None, compute_op=ALU.add).then_inc(s["scattered"], 16)
                pool.wait_ge(s["stored"], 16 * E_)
                with pool.Fori(0, E_ // 2) as g:
                    for k in range(2):
                        gather(2 * g + k, k)
                    for k in range(2):
                        scatter(2 * g + k, k)
                pool.wait_ge(s["scattered"], 16 * CC * E_)

            @block.tensor
            def _(pe):
                pe.wait_ge(s["consts_in"], 48)
                with pe.Fori(0, E_ // 2) as g:
                    for k in range(2):
                        pe.wait_ge(s["xT_in"], 32 * g + 32)
                        mlp_pe(pe, 2 * g + k, w_s, xT[:, k, :])
                with pe.Fori(0, E_ // 2) as g:
                    for k in range(2):
                        e = 2 * g + k
                        pe.wait_ge(s[f"tok_in{k}"], 16 * CC * (g + 1))
                        for c in range(CC):
                            last = nc.tensor.transpose(ps[:, 6 + c // 4, (c % 4) * CP:(c % 4 + 1) * CP], tok[:, k, c, 0:D], ident[0:CP, 0:CP])
                        last.then_inc(s["tok_T"], 1)
                        pe.wait_ge(s["tok_Tc"], e + 1)
                        pe.wait_ge(s[f"w_in{k}"], 16 * (g + 1))
                        mlp_pe(pe, E_ + e, w_e[:, k, :], xT[:, k, :])

            @block.scalar
            def _(a):
                a.wait_ge(s["consts_in"], 48)
                with a.Fori(0, E_) as i:
                    mlp_act(a, i, w_s)
                with a.Fori(0, E_ // 2) as g:
                    for k in range(2):
                        mlp_act(a, E_ + 2 * g + k, w_e[:, k, :])

            @block.vector
            def _(v):
                v.wait_ge(s["consts_in"], 48)
                with v.Fori(0, E_ // 2) as g:
                    for k in range(2):
                        i = 2 * g + k
                        b2 = parts(w_s)[3]
                        v.wait_ge(s["h1_in"], 32 * g + 32)
                        nc.vector.tensor_tensor(h1_s[:, k], h1_s[:, k], b2.unsqueeze(1).to_broadcast([CP, CC, D]), ALU.add).then_inc(s["step"], 1)
                        v.wait_ge(s["step"], i + 1)
                        v.wait_ge(s["down"], i + 1)
                        v.wait_ge(s["stored"], 32 * g)
                        for bank, c0, n in chunk_sets:
                            last = nc.vector.tensor_tensor(y[:, k, c0:c0 + n, :], ps[0:CP, bank, 0:n * D].rearrange("p (c k) -> p c k", c=n),
                                                           h1_s[:, k, c0:c0 + n, :], ALU.add)
                        last.then_inc(s["y_ready"], 1)
                with v.Fori(0, E_ // 2) as g:
                    for k in range(2):
                        e = 2 * g + k
                        v.wait_ge(s["scattered"], 32 * CC * g)
                        nc.vector.tensor_copy(idx[:, k, :], lists_sb[:, bass.ds(e, 1), :].rearrange("p a c -> p (a c)")).then_inc(s["idx"], 1)
                    for k in range(2):
                        e = 2 * g + k
                        b2 = parts(w_e[:, k, :])[3]
                        v.wait_ge(s["tok_T"], e + 1)
                        v.wait_ge(s["y_ready"], E_ + e)
                        nc.vector.tensor_copy(score[:, :], tok[:, k, :, bass.ds(D + e, 1)].rearrange("p c a -> p (c a)"))
                        nc.vector.tensor_copy(xT[:, k, 0:4 * CP], ps[:, 6, 0:4 * CP])
                        nc.vector.tensor_copy(xT[:, k, 4 * CP:CAP], ps[:, 7, 0:CP]).then_inc(s["tok_Tc"], 1)
                        v.wait_ge(s["down"], E_ + e + 1)
                        for bank, c0, n in chunk_sets:
                            last = nc.vector.tensor_tensor(y[:, k, c0:c0 + n, :], ps[0:CP, bank, 0:n * D].rearrange("p (c k) -> p c k", c=n),
                                                           b2.unsqueeze(1).to_broadcast([CP, n, D]), ALU.add)
                        last.then_inc(s["step"], 1)
                        v.wait_ge(s["step"], E_ + e + 1)
                        v.wait_ge(s["tok_Tc"], e + 1)
                        for c in range(CC):
                            last = nc.vector.tensor_scalar(y[:, k, c, :], y[:, k, c, :], score[:, c:c + 1], None, ALU.mult)
                        last.then_inc(s["y_ready"], 1)


def expert_layout(i):
    c_ = np.ascontiguousarray
    carry = np.ones((P, E_, TILES), np.float32); carry[:, :, 0] = 0
    def pack(w1, b1, w2, b2):
        return np.concatenate([w1, w2.reshape(4, P, D).transpose(1, 0, 2).reshape(P, HID), b1.reshape(4, P).T,
                               np.broadcast_to(b2, (P, D))], 1)
    w = [pack(i['L0_ffn_w1'][e], i['L0_ffn_b1'][e], i['L0_ffn_w2'][e], i['L0_ffn_b2'][e]) for e in range(E_)]
    w.append(pack(i['L0_ffn_sw1'], i['L0_ffn_sb1'], i['L0_ffn_sw2'], i['L0_ffn_sb2']))
    return dict(ones=np.ones((P, P), np.float32), below=np.triu(np.ones((P, P), np.float32), 1),
                iota_lo=c_(np.broadcast_to(np.arange(CP, dtype=np.float32), (P, CP))),
                tile_no=c_(np.broadcast_to(np.arange(TILES, dtype=np.float32), (P, TILES))),
                pid=np.arange(P, dtype=np.float32)[:, None], carry=carry.reshape(P, -1),
                first_bit=np.full((P, E_), 1 << 29, np.int32), w_ffn=c_(np.stack(w)))


def peer(nc, d, src, dst):
    H, QD, HALF, PK, K = 8, 64, 32, 64, 16
    RUNS = [(0, 1, 16), (1, 1, 8), (2, 1, 5), (3, 1, 4), (4, 1, 3), (5, 3, 2), (8, 8, 1)]
    C = sum(n * m for _, n, m in RUNS)
    CH, HC = 4, 2 * C
    LO, HI = 32, 4
    SPLIT = 2
    UPSCALE = 4096.0
    G, TG = 4, 32
    TAKEN = -3.0e38
    R = 2 * H
    with ExitStack() as ctx:
        def sb(name, shape, dt=F32):
            return ctx.enter_context(nc.sbuf_tensor("pr_" + name, shape, dt))
        wq = sb("wq", [P, H * QD]); brow = sb("brow", [1, H * QD]); brest = sb("brest", [1, H * QD])
        bias3 = sb("bias3", [65, H * QD], BF16); ones3 = sb("ones3", [65, P], BF16)
        wmean = sb("wmean", [P, H]); bmean = sb("bmean", [1, H])
        gb = sb("gb", [P, 2])
        blk = sb("blk", [P, 4])
        down = sb("down", [P, HI, P]); up = sb("up", [P, HI, P])
        kpad = sb("kpad", [PK, 4, P]); ksq = sb("ksq", [PK, 4, P]); knorm = sb("knorm", [PK, 4]); kblk = sb("kblk", [P, 4 * PK])
        ident = sb("ident", [P, P])
        x = sb("x", [P, D]); xr = sb("xr", [P, D]); stats = sb("stats", [P, 6]); mv = sb("mv", [P, 2])
        xln = sb("xln", [P, 1]); rstd = sb("rstd", [P, 1]); xn = sb("xn", [P, D]); xT = sb("xT", [P, P])
        qs = sb("qs", [P, 512]); hvar = sb("hvar", [P, H]); hln = sb("hln", [P, H]); hrstd = sb("hrstd", [P, H])
        q = sb("q", [P, 512]); qT = sb("qT", [P, 4, P]); qsT = sb("qsT", [P, 4, P])
        nsum = sb("nsum", [P, R]); nln = sb("nln", [P, R]); nrm = sb("nrm", [P, R])
        s = sb("s", [P, R, PK]); sw = sb("sw", [P, R, PK])
        sv = sb("sv", [P, R, K]); si = sb("si", [P, R, K], U32); sif = sb("sif", [P, R, K])
        cand = sb("cand", [P, H, C]); candi = sb("candi", [P, H, C]); cw = sb("cw", [P, H, C]); cw2 = sb("cw2", [P, H, C])
        cm = sb("cm", [P, H, K]); ce = sb("ce", [P, H, C]); wraw = sb("wraw", [P, H, C]); wgt = sb("wgt", [P, H, C])
        wsum = sb("wsum", [P, H])
        w2 = sb("w2", [HC, SPLIT, 512], F16)
        fi = sb("fi", [HC, 512], U16); lo = sb("lo", [HC, 512], U16); hi = sb("hi", [HC, 512], U16)
        oh_lo = sb("oh_lo", [HC, LO, 512], F16); oh_hi = sb("oh_hi", [HC, HI, 512], F16)
        w_hi = sb("w_hi", [HC, HI, SPLIT, 512], F16)
        act = sb("act", [P, HI, P]); wE = sb("wE", [P, TG, HI]); gblk = sb("gblk", [P, HI, P]); o = sb("o", [P, D])
        gates = sb("gates", [P, 2]); eps = sb("eps", [P, 1]); one = sb("one", [P, 1]); c15 = sb("c15", [P, R]); gate_q = sb("gate_q", [P, 1])
        ps = ctx.enter_context(nc.psum_tensor("pr_ps", [P, 8, 512], F32))
        ps_x, ps_o, ps_q, ps_iT = ps[:, 0, 0:P], ps[:, 7, D:2 * D], ps[:, 1, :], ps[0:HC, 1, :]
        ps_qT, ps_wT, ps_s = ps[:, 2, :], ps[0:HC, 2, :], ps[:, 3:5, :]
        ps_w, ps_in, ps_n, ps_k = ps[:, 5, 0:TG * HI * SPLIT], ps[:, 6, :], ps[:, 7, 0:R], ps[:, 7, 0:4 * PK]
        S = ctx.enter_context(semaphores(nc, "pr_", """consts_in k_step k_norm k_root k_ready k_T k_blk x_in xr_in x_var x_rough x_rstd x_norm x_T x_Tc q_mm q_sq q_var q_rough q_rstd
             q_norm q_T q_Tc q_sqT norms sims n_max n_rough n_rstd sif_ready one_ready s_ready ranked found candi_ready cand_ready cand_exp w_raw w_ready
             w_T fi_c w_part wr_ready w_parts onehots scat inner gelu g_ready out_mm o_ready stored
             f_step t_step h_step o_step a_step0 a_step1 a_step2 p_step0 p_step1 p_step2"""))

        def skewed(eng, head, body, tail):
            head()
            body(0)
            with eng.Fori(1, TILES - 2) as i:
                body(i)
            body(TILES - 2)
            body(TILES - 1)
            tail()

        def has(i, ahead):
            return not isinstance(i, int) or 0 <= i + ahead < TILES

        def candidates(eng, out, v_):
            s0 = v_[:, :, :].rearrange("p (h u) k -> p h u k", u=2)
            at = 0
            for a0, na, m in RUNS:
                o_ = out[:, :, at:at + na * m]
                if m == 1:
                    i0, i1 = s0[:, :, 0, a0:a0 + na], s0[:, :, 1, 0:1].to_broadcast([P, H, na])
                elif na == 1:
                    i0, i1 = s0[:, :, 0, a0:a0 + 1].to_broadcast([P, H, m]), s0[:, :, 1, 0:m]
                else:
                    o_ = o_.rearrange("p h (a b) -> p h a b", b=m)
                    i0 = s0[:, :, 0, a0:a0 + na].unsqueeze(3).to_broadcast([P, H, na, m])
                    i1 = s0[:, :, 1, 0:m].unsqueeze(2).to_broadcast([P, H, na, m])
                last = eng.tensor_tensor(o_, i0, i1, ALU.add)
                at += na * m
            return last

        with nc.Block() as block:
            @block.sync
            def _(sp):
                for to, name in ((wq, "wq_peer"), (brow, "brow_peer"), (gb, "gb_peer"), (blk, "blk_ones"),
                                 (down, "down_cols"), (up, "up_rows"), (kpad, "keys_pad"), (ident, "ident")):
                    sp.dma_start(to[:], d[name]).then_inc(S["consts_in"], 16)

                def load(i):
                    sp.dma_start(x[:, :], src[bass.ds(i * P, P), :]).then_inc(S["x_in"], 16)

                def residual(i):
                    sp.dma_start(xr[:, :], src[bass.ds(i * P, P), :]).then_inc(S["xr_in"], 16)

                def store(i):
                    sp.wait_ge(S["o_ready"], i + 1)
                    sp.dma_start(dst[bass.ds(i * P, P), :], o[:, :]).then_inc(S["stored"], 16)

                def body(i):
                    if has(i, 3):
                        sp.wait_ge(S["x_norm"], i + 3)
                        load(i + 3)
                    if has(i, -1):
                        store(i - 1)
                        residual(i)
                load(0)
                residual(0)
                for n in range(1, 3):
                    sp.wait_ge(S["x_norm"], n)
                    load(n)
                body(0)
                with sp.Fori(1, TILES - 3) as i:
                    body(i)
                body(TILES - 3)
                body(TILES - 2)
                body(TILES - 1)
                store(TILES - 1)
                sp.wait_ge(S["stored"], 16 * TILES)

            @block.gpsimd
            def _(pool):
                def refine(i, n, rough, y, t, v, scale, add, done):
                    pool.wait_ge(rough, i + 1)
                    st = Steps(pool, S[f"p_step{n}"], 4 * i)
                    st.mark(nc.gpsimd.tensor_tensor(t, y, y, ALU.mult))
                    st.link(nc.gpsimd.tensor_scalar(v, v, -0.5 * scale, -0.5 * add, ALU.mult, ALU.add))
                    st.link(nc.gpsimd.tensor_tensor(t, t, v, ALU.mult))
                    st.link(nc.gpsimd.tensor_tensor(t, t, c15[:, 0:t.shape[1]], ALU.add))
                    nc.gpsimd.tensor_tensor(y, y, t, ALU.mult).then_inc(done, 1)

                def front_x(i):
                    refine(i, 0, S["x_rough"], rstd[:, :], xln[:, :], mv[:, 1:2], 1.0, EPS, S["x_rstd"])

                def front_a(i):
                    refine(i, 1, S["q_rough"], hrstd[:, :], hln[:, :], hvar[:, :], 1.0 / QD, EPS, S["q_rstd"])

                def front_b(i):
                    refine(i, 2, S["n_rough"], nrm[:, :], nln[:, :], nsum[:, :], 1.0, 0.0, S["n_rstd"])

                def body(i):
                    if has(i, 1):
                        front_a(i + 1)
                    pool.wait_ge(S["found"], i + 1)
                    after(pool, S["w_T"], 2 * i - 1)
                    nc.gpsimd.tensor_tensor(gate_q[:, :], one[:, :], one[:, :], ALU.add)
                    nc.gpsimd.tensor_copy(sif[:, :, :], si[:, :, :]).then_inc(S["sif_ready"], 1)
                    pool.wait_ge(S["sif_ready"], i + 1)
                    last = candidates(nc.gpsimd, candi, sif)
                    last.then_inc(S["candi_ready"], 1)
                    if has(i, 1):
                        front_b(i + 1)
                    pool.wait_ge(S["w_raw"], i + 1)
                    nc.gpsimd.tensor_tensor(wgt[:, :, :], wraw[:, :, :], wsum[:, :].unsqueeze(2).to_broadcast([P, H, C]),
                                            ALU.mult).then_inc(S["w_ready"], 1)
                    if has(i, 2):
                        front_x(i + 2)
                nc.gpsimd.memset(c15[:, :], 1.5)
                nc.gpsimd.memset(one[:, :], 1.0).then_inc(S["one_ready"], 1)
                pool.wait_ge(S["one_ready"], 1)

                def head():
                    front_x(0); front_a(0); front_b(0); front_x(1)
                skewed(pool, head, body, lambda: None)

            @block.tensor
            def _(pe):
                pe.wait_ge(S["consts_in"], 128)
                pe.wait_ge(S["k_ready"], 1)
                for j in range(4):
                    last = nc.tensor.transpose(ps_k[:, j * PK:(j + 1) * PK], kpad[:, j, :], ident[0:PK, 0:PK])
                last.then_inc(S["k_T"], 1)
                pe.wait_ge(S["k_blk"], 1)

                def turn_x(i):
                    pe.wait_ge(S["x_norm"], i + 1)
                    nc.tensor.transpose(ps_x, xn[:, :], ident[:, :]).then_inc(S["x_T"], 1)

                def queries(i):
                    pe.wait_ge(S["x_Tc"], i + 1)
                    after(pe, S["fi_c"], i - 1)
                    nc.tensor.matmul(ps_q, xT[:, :], wq[:, :], start=True, stop=False)
                    nc.tensor.matmul(ps_q, ones3[:, :], bias3[:, :], start=False, stop=True).then_inc(S["q_mm"], 1)

                def turn_q(i):
                    pe.wait_ge(S["q_norm"], i + 1)
                    for j in range(4):
                        last = nc.tensor.transpose(ps_qT[:, j * P:(j + 1) * P], q[:, j * P:(j + 1) * P], ident[:, :])
                    last.then_inc(S["q_T"], 1)

                def scores(i):
                    pe.wait_ge(S["q_Tc"], i + 1)
                    for j in range(4):
                        last = nc.tensor.matmul(ps_s[:, j // 2, (j % 2) * 256:(j % 2 + 1) * 256], qT[:, j, :], kblk[:, :],
                                                start=True, stop=True)
                    last.then_inc(S["sims"], 1)
                    pe.wait_ge(S["q_sqT"], i + 1)
                    for j in range(4):
                        last = nc.tensor.matmul(ps_n[:, 4 * j:4 * j + 4], qsT[:, j, :], blk[:, :], start=True, stop=True)
                    last.then_inc(S["norms"], 1)

                def inner(i):
                    pe.wait_ge(S["x_Tc"], i + 1)
                    after(pe, S["gelu"], i)
                    for j in range(HI):
                        last = nc.tensor.matmul(ps_in[:, j * P:(j + 1) * P], down[:, j, :], xT[:, :], start=True, stop=True)
                    last.then_inc(S["inner"], 1)

                def scatter(i, g):
                    if g == 0:
                        pe.wait_ge(S["onehots"], i + 1)
                    for u in range(TG):
                        for j in range(CH):
                            c = j * P + g * TG + u
                            last = nc.tensor.matmul(ps_w[g * 32:(g + 1) * 32, u * HI * SPLIT:(u + 1) * HI * SPLIT],
                                                    oh_lo[:, :, c], w_hi[:, :, :, c].rearrange("p a b -> p (a b)"),
                                                    start=(j == 0), stop=(j == CH - 1))
                    if g == G - 1:
                        last.then_inc(S["scat"], 1)

                def turn_w(i):
                    pe.wait_ge(S["candi_ready"], i + 1)
                    for j in range(CH):
                        last = nc.tensor.transpose(ps_iT[:, j * P:(j + 1) * P],
                                                   candi[:, 2 * j:2 * j + 2, :].rearrange("p a b -> p (a b)"), ident[:, :])
                    last.then_inc(S["w_T"], 1)
                    pe.wait_ge(S["w_ready"], i + 1)
                    for j in range(CH):
                        last = nc.tensor.transpose(ps_wT[:, j * P:(j + 1) * P],
                                                   wgt[:, 2 * j:2 * j + 2, :].rearrange("p a b -> p (a b)"), ident[:, :])
                    last.then_inc(S["w_T"], 1)

                def output(i):
                    pe.wait_ge(S["g_ready"], i + 1)
                    for j in range(HI):
                        last = nc.tensor.matmul(ps_o, gblk[:, j, :], up[:, j, :], start=(j == 0), stop=(j == HI - 1))
                    last.then_inc(S["out_mm"], 1)

                def head():
                    turn_x(0); queries(0); turn_q(0); scores(0); inner(0); turn_x(1); queries(1)

                def body(i):
                    if has(i, -1):
                        scatter(i - 1, 0)
                    if has(i, 1):
                        turn_q(i + 1)
                    if has(i, -1):
                        scatter(i - 1, 1)
                    if has(i, 1):
                        scores(i + 1)
                    if has(i, -1):
                        scatter(i - 1, 2)
                        scatter(i - 1, 3)
                    turn_w(i)
                    if has(i, -1):
                        output(i - 1)
                    if has(i, 1):
                        inner(i + 1)
                    if has(i, 2):
                        turn_x(i + 2)
                        queries(i + 2)

                def tail():
                    for g in range(G):
                        scatter(TILES - 1, g)
                    output(TILES - 1)
                skewed(pe, head, body, tail)

            @block.scalar
            def _(a):
                nc.scalar.preload_act_table_set("natural_log_exp_and_others")
                a.wait_ge(S["k_norm"], 1)
                nc.scalar.activation(knorm[:, :], knorm[:, :], ACT.Ln).then_inc(S["k_root"], 1)
                a.wait_ge(S["k_root"], 1)
                nc.scalar.activation(knorm[:, :], knorm[:, :], ACT.Exp, scale=-0.5).then_inc(S["k_root"], 1)

                def rsqrt(out, tmp, in_, which, i, bias=0.0, scale=1.0):
                    nc.scalar.activation(tmp, in_, ACT.Ln, bias=bias, scale=scale).then_inc(S[f"a_step{which}"], 1)
                    a.wait_ge(S[f"a_step{which}"], i + 1)
                    return nc.scalar.activation(out, tmp, ACT.Exp, scale=-0.5)

                def norm_x(i):
                    a.wait_ge(S["x_var"], i + 1)
                    rsqrt(rstd[:, :], xln[:, :], mv[:, 1:2], 0, i, eps[:, 0:1]).then_inc(S["x_rough"], 1)

                def front_x(i):
                    norm_x(i)
                    a.wait_ge(S["x_T"], i + 1)
                    after(a, S["inner"], i)
                    nc.scalar.activation(xT[:, :], ps_x, ACT.Copy).then_inc(S["x_Tc"], 1)
                    a.wait_ge(S["q_mm"], i + 1)
                    nc.scalar.activation(qs[:, :], ps_q, ACT.Square).then_inc(S["q_sq"], 1)

                def front_a(i):
                    a.wait_ge(S["q_var"], i + 1)
                    rsqrt(hrstd[:, :], hln[:, :], hvar[:, :], 1, i, eps[:, 0:1], 1.0 / QD).then_inc(S["q_rough"], 1)
                    a.wait_ge(S["q_T"], i + 1)
                    nc.scalar.activation(qT[:, :, :].rearrange("p a b -> p (a b)"), ps_qT, ACT.Identity,
                                         bias=gb[:, 1:2], scale=gb[:, 0:1]).then_inc(S["q_Tc"], 1)
                    a.wait_ge(S["q_Tc"], i + 1)
                    nc.scalar.activation(qsT[:, :, :], qT[:, :, :], ACT.Square).then_inc(S["q_sqT"], 1)

                def front_b(i):
                    a.wait_ge(S["n_max"], i + 1)
                    rsqrt(nrm[:, :], nln[:, :], nsum[:, :], 2, i).then_inc(S["n_rough"], 1)

                def head():
                    front_x(0); front_a(0); front_b(0); front_x(1)

                def body(i):
                    if has(i, 1):
                        front_a(i + 1)
                    a.wait_ge(S["cand_ready"], i + 1)
                    nc.scalar.activation(ce[:, :, :], cand[:, :, :], ACT.Exp).then_inc(S["cand_exp"], 1)
                    if has(i, 1):
                        front_b(i + 1)
                    a.wait_ge(S["w_T"], 2 * i + 1)
                    nc.scalar.activation(fi[:, :], ps_iT, ACT.Copy).then_inc(S["fi_c"], 1)
                    a.wait_ge(S["w_T"], 2 * i + 2)
                    nc.scalar.activation(w2[:, 0, :], ps_wT, ACT.Copy).then_inc(S["w_part"], 1)
                    after(a, S["g_ready"], i)
                    a.wait_ge(S["inner"], i + 1)
                    nc.scalar.activation(act[:, :, :].rearrange("p a b -> p (a b)"), ps_in, ACT.Gelu).then_inc(S["gelu"], 1)
                    nc.scalar.preload_act_table_set("natural_log_exp_and_others")
                    if has(i, 2):
                        front_x(i + 2)
                skewed(a, head, body, lambda: None)

            @block.vector
            def _(v):
                v.wait_ge(S["consts_in"], 128)
                k = Steps(v, S["k_step"])
                k.mark(nc.vector.memset(gblk[:, :, :], 0.0))
                k.mark(nc.vector.memset(eps[:, :], EPS))
                for w_, m_ in ((wq, wmean), (brow, bmean)):
                    hv = w_[:, :].rearrange("p (h c) -> p h c", h=H)
                    k.link(nc.vector.tensor_reduce(m_[:, :], hv, AX.X, ALU.add))
                    k.link(nc.vector.tensor_scalar(m_[:, :], m_[:, :], 1.0 / QD, None, ALU.mult))
                    k.mark(nc.vector.tensor_tensor(hv, hv, m_[:, :].unsqueeze(2).to_broadcast([w_.shape[0], H, QD]), ALU.subtract))
                k.mark(nc.vector.memset(ones3[:, :], 1.0))
                k.link(nc.vector.memset(bias3[:, :], 0.0))
                for r in range(3):
                    k.link(nc.vector.tensor_copy(bias3[32 * r:32 * r + 1, :], brow[:, :]))
                    k.link(nc.vector.tensor_copy(brest[:, :], bias3[32 * r:32 * r + 1, :]))
                    k.link(nc.vector.tensor_tensor(brow[:, :], brow[:, :], brest[:, :], ALU.subtract))
                k.mark(nc.vector.tensor_scalar(up[:, :, :], up[:, :, :], 1.0 / UPSCALE, None, ALU.mult))
                k.link(nc.vector.tensor_tensor(ksq[:, :, :], kpad[:, :, :], kpad[:, :, :], ALU.mult))
                k.link(nc.vector.tensor_reduce(knorm[:, :], ksq[:, :, :], AX.X, ALU.add))
                nc.vector.tensor_scalar(knorm[:, :], knorm[:, :], 1e-24, None, ALU.max).then_inc(S["k_norm"], 1)
                v.wait_ge(S["k_root"], 2)
                for j in range(4):
                    last = nc.vector.tensor_scalar(kpad[:, j, :], kpad[:, j, :], knorm[:, j:j + 1], None, ALU.mult)
                last.then_inc(S["k_ready"], 1)
                v.wait_ge(S["k_T"], 1)
                nc.vector.tensor_copy(kblk[:, :], ps_k).then_inc(S["k_blk"], 1)

                PF, PT, PH = 3, 17, 2

                def norm_x(i):
                    f = Steps(v, S["f_step"], PF * i)
                    v.wait_ge(S["x_in"], 16 * i + 16)
                    f.mark(nc.vector.memset(gates[:, 0:1], 0.0))
                    f.link(nc.vector.bn_stats(stats[:, :], x[:, :]))
                    f.mark(nc.vector.memset(gates[:, 0:1], 0.0))
                    nc.vector.bn_aggr(mv[:, :], stats[:, :]).then_inc(S["x_var"], 1)

                def apply_x(i):
                    v.wait_ge(S["x_rstd"], i + 1)
                    nc.vector.tensor_scalar(xn[:, :], x[:, :], mv[:, 0:1], rstd[:, 0:1], ALU.subtract, ALU.mult).then_inc(S["x_norm"], 1)

                def var_q(i):
                    v.wait_ge(S["q_sq"], i + 1)
                    nc.vector.tensor_reduce(hvar[:, :], qs[:, :].rearrange("p (h c) -> p h c", h=H), AX.X, ALU.add).then_inc(S["q_var"], 1)

                def apply_q(i):
                    v.wait_ge(S["q_rstd"], i + 1)
                    nc.vector.tensor_tensor(q[:, :].rearrange("p (h c) -> p h c", h=H), ps_q.rearrange("p (h c) -> p h c", h=H),
                                            hrstd[:, :].unsqueeze(2).to_broadcast([P, H, QD]), ALU.mult).then_inc(S["q_norm"], 1)

                def norms(i):
                    v.wait_ge(S["norms"], i + 1)
                    nc.vector.tensor_scalar(nsum[:, :], ps_n, 1e-24, None, ALU.max).then_inc(S["n_max"], 1)

                def apply_s(i):
                    v.wait_ge(S["sims"], i + 1)
                    v.wait_ge(S["n_rstd"], i + 1)
                    for b in range(2):
                        last = nc.vector.tensor_tensor(s[:, 8 * b:8 * b + 8, :], ps_s[:, b, :].rearrange("p (r c) -> p r c", c=PK),
                                                       nrm[:, 8 * b:8 * b + 8].unsqueeze(2).to_broadcast([P, 8, PK]), ALU.mult)
                    last.then_inc(S["s_ready"], 1)

                def head():
                    norm_x(0); apply_x(0); var_q(0); apply_q(0); norms(0); apply_s(0); norm_x(1); apply_x(1)

                def body(i):
                    t = Steps(v, S["t_step"], PT * i)
                    gate = lambda: t.mark(nc.vector.memset(gates[:, 1:2], 0.0))
                    if has(i, 1):
                        var_q(i + 1)
                    v.wait_ge(S["s_ready"], i + 1)
                    gate()
                    for r in range(R):
                        last = nc.vector.max(sv[:, r, 0:8], s[:, r, :])
                    t.link(last)
                    gate()
                    for r in range(R):
                        nc.vector.max_index(si[:, r, 0:8], sv[:, r, 0:8], s[:, r, :])
                    if has(i, 1):
                        apply_q(i + 1)
                    for r in range(R):
                        last = nc.vector.match_replace(sw[:, r, :], sv[:, r, 0:8], s[:, r, :], TAKEN)
                    t.link(last)
                    gate()
                    for r in range(R):
                        last = nc.vector.max(sv[:, r, 8:16], sw[:, r, :])
                    t.link(last)
                    gate()
                    for r in range(R):
                        last = nc.vector.max_index(si[:, r, 8:16], sv[:, r, 8:16], sw[:, r, :])
                    last.then_inc(S["found"], 1)
                    candidates(nc.vector, cand, sv).then_inc(S["cand_ready"], 1)
                    v.wait_ge(S["cand_ready"], i + 1)
                    gate()
                    for h in range(H):
                        last = nc.vector.max(cm[:, h, 0:8], cand[:, h, :])
                    t.link(last)
                    gate()
                    for h in range(H):
                        last = nc.vector.match_replace(cw[:, h, :], cm[:, h, 0:8], cand[:, h, :], TAKEN)
                    t.link(last)
                    gate()
                    for h in range(H):
                        last = nc.vector.max(cm[:, h, 8:16], cw[:, h, :])
                    t.link(last)
                    gate()
                    for h in range(H):
                        last = nc.vector.match_replace(cw2[:, h, :], cm[:, h, 8:16], cw[:, h, :], TAKEN)
                    last.then_inc(S["ranked"], 1)
                    if has(i, 1):
                        norms(i + 1)
                    v.wait_ge(S["ranked"], i + 1)
                    v.wait_ge(S["cand_exp"], i + 1)
                    after(v, S["w_ready"], i)
                    st = nc.vector.scalar_tensor_tensor(wraw[:, :, :], cw2[:, :, :], TAKEN, ce[:, :, :], ALU.is_equal, ALU.mult)
                    t.link(st)
                    t.link(nc.vector.tensor_reduce(wsum[:, :], wraw[:, :, :], AX.X, ALU.add))
                    t.link(nc.vector.tensor_scalar(wsum[:, :], wsum[:, :], 1.0 / UPSCALE, None, ALU.mult))
                    nc.vector.reciprocal(wsum[:, :], wsum[:, :]).then_inc(S["w_raw"], 1)
                    assert t.n == PT, t.n

                def h_stage(i):
                    h = Steps(v, S["h_step"], PH * i)
                    v.wait_ge(S["fi_c"], i + 1)
                    nc.vector.tensor_scalar(lo[:, :], fi[:, :], LO - 1, None, ALU.bitwise_and)
                    h.link(nc.vector.tensor_scalar(hi[:, :], fi[:, :], 5, None, ALU.logical_shift_right))
                    for e in range(HI):
                        nc.vector.tensor_scalar(oh_hi[:, e, :], hi[:, :], float(e), None, ALU.is_equal)
                    for e in range(LO):
                        last = nc.vector.tensor_scalar(oh_lo[:, e, :], lo[:, :], float(e), None, ALU.is_equal)
                    if has(i, 2):
                        apply_x(i + 2)
                    v.wait_ge(S["w_part"], i + 1)
                    h.link(nc.vector.tensor_tensor(w2[:, 1, :], ps_wT, w2[:, 0, :], ALU.subtract))
                    for e in range(HI):
                        last = nc.vector.tensor_tensor(w_hi[:, e, :, :], w2[:, :, :],
                                                       oh_hi[:, e:e + 1, :].to_broadcast([HC, SPLIT, 512]), ALU.mult)
                    last.then_inc(S["onehots"], 1)

                def o_first(i):
                    v.wait_ge(S["scat"], i + 1)
                    st = nc.vector.tensor_reduce(wE[:, :, :], ps_w.rearrange("p (t a b) -> p t a b", a=HI, b=SPLIT), AX.X, ALU.add)
                    st.then_inc(S["o_step"], 1)
                    v.wait_ge(S["o_step"], i + 1)
                    v.wait_ge(S["gelu"], i + 1)
                    for g in range(G):
                        r = slice(g * 32, (g + 1) * 32)
                        last = nc.vector.tensor_tensor(gblk[r, :, g * TG:(g + 1) * TG], act[r, :, g * TG:(g + 1) * TG],
                                                       wE[r, :, :].rearrange("p t a -> p a t"), ALU.mult)
                    last.then_inc(S["g_ready"], 1)

                def o_last(i):
                    v.wait_ge(S["out_mm"], i + 1)
                    v.wait_ge(S["xr_in"], 16 * i + 16)
                    after(v, S["stored"], 16 * i)
                    nc.vector.tensor_tensor(o[:, :], ps_o, xr[:, :], ALU.add).then_inc(S["o_ready"], 1)

                def whole(i):
                    body(i)
                    if has(i, 1):
                        apply_s(i + 1)
                    if has(i, -1):
                        o_first(i - 1)
                    if has(i, 2):
                        norm_x(i + 2)
                    h_stage(i)
                    if has(i, -1):
                        o_last(i - 1)

                def tail():
                    o_first(TILES - 1)
                    o_last(TILES - 1)
                skewed(v, head, whole, tail)


def peer_layout(i):
    c_ = np.ascontiguousarray
    kp = np.zeros((64, 4, 128), np.float32)
    for j in range(4):
        kp[:, j, 32 * j:32 * j + 32] = i['L1_ffn_keys1' if j % 2 else 'L1_ffn_keys0']
    dn = i['L1_ffn_expert_down'][:128].reshape(4, 1, 32, 128)
    dn = np.broadcast_to(dn, (4, 4, 32, 128)).transpose(3, 0, 1, 2).reshape(128, 4, 128)
    u = i['L1_ffn_expert_up'][:128].reshape(1, 4, 32, 128)
    u = np.broadcast_to(u, (4, 4, 32, 128)).transpose(0, 2, 1, 3).reshape(128, 4, 128)
    gb = np.tile(np.stack([i['L1_ffn_ln_g'], i['L1_ffn_ln_b']], 1), (2, 1))
    return dict(wq_peer=c_(i['L1_ffn_Wq'].T), brow_peer=c_(i['L1_ffn_bq'][None, :]), gb_peer=c_(gb),
                blk_ones=np.kron(np.eye(4), np.ones((32, 1))).astype(np.float32),
                down_cols=c_(dn), up_rows=c_(u), keys_pad=kp, ident=np.eye(128, dtype=np.float32))


def build(nc, d, out):
    scratch = lambda name, shape, dt=F32: nc.dram_tensor(name, shape, dt, kind="Internal").ap()
    h0, h1, h2, h3 = (scratch(f"h{n}", [N, D]) for n in range(4))
    table, probs, xfT = scratch("table", [N, D + E_]), scratch("probs", [N, E_]), scratch("xfT", [D, N])
    lists = scratch("lists", [CP, E_, CC], U32)
    embed(nc, d, h0)
    attend0(nc, d, h0, h1, table, probs, xfT)
    route(nc, d, probs, lists)
    experts(nc, d, h1, table, xfT, lists, h2)
    attend1(nc, d, h2, h3)
    peer(nc, d, h3, out)


def kernel(**inputs):
    import concourse.bacc as bacc
    from concourse.bass_utils import run_bass_kernel_spmd

    i = {k: np.asarray(v) for k, v in inputs.items()}
    arrays = {**attention_layout(i), **expert_layout(i), **peer_layout(i)}
    nc = bacc.Bacc("TRN2", target_bir_lowering=False, num_devices=1)
    d = {k: nc.dram_tensor("in_" + k, a.shape, mybir.dt.from_np(a.dtype), kind="ExternalInput").ap() for k, a in arrays.items()}
    out = nc.dram_tensor("out", (N, D), F32, kind="ExternalOutput").ap()
    build(nc, d, out)
    r = run_bass_kernel_spmd(nc, [{"in_" + k: a for k, a in arrays.items()}], core_ids=[0])
    return r.results[0]["out"].reshape(B, T, D)
```

```python
import numpy as np
import concourse.bass as bass
from concourse import mybir
from contextlib import ExitStack, contextmanager

F32 = mybir.dt.float32
BF16 = mybir.dt.bfloat16
I32 = mybir.dt.int32
U16 = mybir.dt.uint16
F16 = mybir.dt.float16
U32 = mybir.dt.uint32
ALU = mybir.AluOpType
ACT = mybir.ActivationFunctionType
AX = mybir.AxisListType
D, B, T, P = 128, 128, 65, 128
N = B * T
GB = 4
STEPS = B // GB
W = GB * T
EPS = 1e-5


@contextmanager
def semaphores(nc, prefix, names):
    held = {n: nc.alloc_semaphore(prefix + n) for n in names.split()}
    yield held
    nc.clear_and_free_semaphores(list(held.values()))
    nc.all_engine_barrier()


class Steps:

    def __init__(self, eng, sem, base=0):
        self.eng, self.sem, self.base, self.n = eng, sem, base, 0

    def mark(self, ins):
        self.n += 1
        ins.then_inc(self.sem, 1)

    def wait(self):
        self.eng.wait_ge(self.sem, self.base + self.n)

    def link(self, ins):
        self.mark(ins)
        self.wait()


def after(eng, sem, value):
    if not isinstance(value, int) or value > 0:
        eng.wait_ge(sem, value)


def pipelined(eng, body, count, ahead, behind):
    for i in range(-ahead, behind + 1):
        body(i)
    with eng.Fori(behind + 1, count - ahead) as i:
        body(i)
    for i in range(count - ahead, count + behind):
        body(i)


def paired(eng, body, count):
    body(0, 0)
    body(1, 1)
    with eng.Fori(1, count // 2) as g:
        for k in range(2):
            body(2 * g + k, k)


def embed(nc, d, dst):
    NB = 8
    BLOCKS = B // NB
    TOK = T - 1
    KC, REST = 18, 48
    PARTS_X = ((0, 2), (2, 8), (8, KC))
    with ExitStack() as ctx:
        def sb(name, shape, dt=F32):
            return ctx.enter_context(nc.sbuf_tensor("em_" + name, shape, dt))
        w = sb("w", [P, KC, D])
        w_rest = sb("w_rest", [REST, D])
        bias = sb("bias", [D, 1])
        pos = sb("pos", [D, T])
        cls = sb("cls", [D, 1])
        ident = sb("ident", [P, P])
        x = sb("x", [P, 2, KC, 512])
        x_rest = sb("x_rest", [REST, 2, 512])
        tokT = sb("tokT", [D, NB, T])
        tok = sb("tok", [T, NB, D])
        ps = ctx.enter_context(nc.psum_tensor("em_ps", [P, 8, 512], F32))
        s = ctx.enter_context(semaphores(nc, "em_", "consts_in w_in0 w_in1 w_in2 x_in00 x_in01 x_in02 x_in10 x_in11 x_in12 rest_in0 rest_in1 acc_done tokT_ready tok_T tok_ready cls_ready stored"))
        rows = dst.rearrange("(b t) c -> t b c", t=T)
        with nc.Block() as block:
            @block.sync
            def _(sp):
                def body(n, k):
                    after(sp, s["acc_done"], n - 1)
                    for part, (c0, c1) in enumerate(PARTS_X):
                        if isinstance(n, int) and n == 0:
                            sp.dma_start(w[:, c0:c1], d["w_tok"][:, c0:c1]).then_inc(s[f"w_in{part}"], 16)
                        sp.dma_start(x[:, k, c0:c1], d["x_main"][bass.ds(n, 1), :, c0:c1].rearrange("g p k t -> (g p) k t")).then_inc(s[f"x_in{k}{part}"], 16)
                    sp.dma_start(x_rest[:, k], d["x_rest"][bass.ds(n, 1)].rearrange("g p t -> (g p) t")).then_inc(s[f"rest_in{k}"], 16)
                    if isinstance(n, int) and n == 0:
                        for to, name in ((w_rest, "w_tok_rest"), (bias, "b_tok"), (pos, "pos_cols"), (cls, "cls_col"), (ident, "ident")):
                            sp.dma_start(to[:], d[name]).then_inc(s["consts_in"], 16)
                paired(sp, body, BLOCKS)

            @block.gpsimd
            def _(pool):
                with pool.Fori(0, BLOCKS) as n:
                    pool.wait_ge(s["tok_ready"], n + 1)
                    pool.dma_start(rows[:, bass.ds(n * NB, NB), :], tok[:, :, :]).then_inc(s["stored"], 16)
                pool.wait_ge(s["stored"], 16 * BLOCKS)

            @block.tensor
            def _(pe):
                def turn(n):
                    pe.wait_ge(s["tokT_ready"], n + 1)
                    after(pe, s["tok_ready"], n)
                    for b in range(NB):
                        last = nc.tensor.transpose(ps[0:T, 2 + b // 4, (b % 4) * D:(b % 4 + 1) * D], tokT[:, b, :], ident[:, :])
                    last.then_inc(s["tok_T"], 1)

                def body(n, k):
                    after(pe, s["tokT_ready"], n - 1)
                    loads = 16 * (n // 2) + 16 if isinstance(n, int) else 8 * (n - k) + 16
                    for part, (c0, c1) in enumerate(PARTS_X):
                        pe.wait_ge(s[f"x_in{k}{part}"], loads)
                        pe.wait_ge(s[f"w_in{part}"], 16)
                        for c in range(c0, c1):
                            nc.tensor.matmul(ps[:, k, :], w[:, c, :], x[:, k, c, :], start=(c == 0), stop=False)
                    pe.wait_ge(s[f"rest_in{k}"], loads)
                    pe.wait_ge(s["consts_in"], 80)
                    nc.tensor.matmul(ps[:, k, :], w_rest[:, :], x_rest[:, k, :], start=False, stop=True).then_inc(s["acc_done"], 1)
                    if not isinstance(n, int) or n > 0:
                        turn(n - 1)
                paired(pe, body, BLOCKS)
                turn(BLOCKS - 1)

            @block.scalar
            def _(a):
                def body(n, k):
                    a.wait_ge(s["tok_T"], n + 1)
                    after(a, s["stored"], 16 * n)
                    for b in range(2):
                        last = nc.scalar.activation(tok[:, 4 * b:4 * b + 4, :].rearrange("p w c -> p (w c)"),
                                                    ps[0:T, 2 + b, :], ACT.Copy)
                    last.then_inc(s["tok_ready"], 1)
                paired(a, body, BLOCKS)

            @block.vector
            def _(v):
                v.wait_ge(s["consts_in"], 80)
                nc.vector.tensor_scalar(tokT[:, :, 0:1], pos[:, 0:1].unsqueeze(1).to_broadcast([D, NB, 1]), cls[:, 0:1], None,
                                        ALU.mult).then_inc(s["cls_ready"], 1)

                def body(n, k):
                    v.wait_ge(s["acc_done"], n + 1)
                    after(v, s["tok_T"], n)
                    nc.vector.scalar_tensor_tensor(tokT[:, :, 1:T], ps[:, k, :].rearrange("p (b t) -> p b t", t=TOK), bias[:, 0:1],
                                                   pos[:, 1:T].unsqueeze(1).to_broadcast([D, NB, TOK]),
                                                   ALU.add, ALU.mult).then_inc(s["tokT_ready"], 1)
                paired(v, body, BLOCKS)


def newton_rsqrt(nc, pool, steps, rough_ready, n, y, t, v, c15, scale, add, done):
    pool.wait_ge(rough_ready, n + 1)
    st = Steps(pool, steps, 4 * n)
    st.mark(nc.gpsimd.tensor_tensor(t, y, y, ALU.mult))
    st.link(nc.gpsimd.tensor_scalar(v, v, -0.5 * scale, -0.5 * add, ALU.mult, ALU.add))
    st.link(nc.gpsimd.tensor_tensor(t, t, v, ALU.mult))
    st.link(nc.gpsimd.tensor_tensor(t, t, c15, ALU.add))
    nc.gpsimd.tensor_tensor(y, y, t, ALU.mult).then_inc(done, 1)


def row_stats(nc, v, steps, n, gate, x, stats, mv, done):
    st = Steps(v, steps, 3 * n)
    st.mark(nc.vector.memset(gate, 0.0))
    for j in range(x.shape[1]):
        last = nc.vector.bn_stats(stats[:, j, :], x[:, j, :])
    st.link(last)
    st.mark(nc.vector.memset(gate, 0.0))
    for j in range(x.shape[1]):
        last = nc.vector.bn_aggr(mv[:, j, :], stats[:, j, :])
    last.then_inc(done, 1)


def attend0(nc, d, src, dst, table, probs, xfT):
    E = 16
    with ExitStack() as ctx:
        def sb(name, shape, dt=F32):
            return ctx.enter_context(nc.sbuf_tensor("a0_" + name, shape, dt))
        wkq = sb("wkq", [D, 4, D])
        bkq = sb("bkq", [D, 4])
        wvT = sb("wvT", [D, D]); wp = sb("wp", [D, D]); bv = sb("bv", [D, T]); bp = sb("bp", [T, D])
        wvp = sb("wvp", [D, D]); bvp = sb("bvp", [T, D])
        gate_w = sb("gate_w", [D, E])
        cos = sb("cos", [D, T]); sin = sb("sin", [D, T]); tri = sb("tri", [T, T])
        ident = sb("ident", [P, P])
        x = sb("x", [T, GB, D]); xr = sb("xr", [T, GB, D]); xn = sb("xn", [T, GB, D])
        stats1 = sb("stats1", [T, GB, 6]); mv1 = sb("mv1", [T, GB, 2]); ln1 = sb("ln1", [T, GB]); rstd1 = sb("rstd1", [T, GB])
        stats2 = sb("stats2", [T, GB, 6]); mv2 = sb("mv2", [T, GB, 2]); ln2 = sb("ln2", [T, GB]); rstd2 = sb("rstd2", [T, GB])
        gate1 = sb("gate1", [T, 1]); gate2 = sb("gate2", [T, 1]); c15 = sb("c15", [T, GB]); eps = sb("eps", [T, 1])
        xT = sb("xT", [D, W])
        r1 = sb("r1", [D, 2, W]); r2 = sb("r2", [D, 2, W])
        kT = sb("kT", [D, W]); qT = sb("qT", [D, W]); vv = sb("vv", [T, GB, D])
        ab = sb("ab", [T, W]); raw = sb("raw", [T, W]); wei = sb("wei", [T, W])
        h = sb("h", [T, GB, D]); xf = sb("xf", [T, GB, D]); xfTs = sb("xfTs", [D, W])
        lm = sb("lm", [T, GB]); le = sb("le", [T, GB, E]); ls = sb("ls", [T, GB]); pb = sb("pb", [T, GB, E])
        ps = ctx.enter_context(nc.psum_tensor("a0_ps", [P, 8, 512], F32))
        ps_T, ps_l, ps_v, ps_sc, ps_out = ps[:, 0, 0:W], ps[0:T, 0, W:W + GB * E], ps[0:T, 5, :], ps[0:T, 6, 0:W], ps[0:T, 7, :]
        s = ctx.enter_context(semaphores(nc, "a0_", """consts_in folded unfolded scaled ready x_in xr_in var1 rough1 rstd1 normed x_T x_Tc kq v kq_rot vv_ready sc abs_step exp_step sp_ln
             wei_raw wei_ready out xb_ready h_ready var2 rough2 rstd2 xf_ready xf_T xf_Tc logits l_sub l_exp pb_ready
             h_stored xf_stored xfT_stored pb_stored stat1_step stat2_step ln1_step ln2_step newton1_step newton2_step
             rot_step max_step sum_step"""))
        rows_in = src.rearrange("(b t) c -> t b c", t=T)
        rows_h = dst.rearrange("(b t) c -> t b c", t=T)
        rows_t = table.rearrange("(b t) c -> t b c", t=T)
        rows_p = probs.rearrange("(b t) c -> t b c", t=T)
        bat = lambda ap: ap.rearrange("p (g t) -> p g t", g=GB)
        rows = lambda ap: ap.rearrange("p (g c) -> p g c", g=GB)
        per_image = lambda ap, parts, m: ap.unsqueeze(1).to_broadcast([parts, GB, m])
        has = lambda i, ahead: not isinstance(i, int) or 0 <= i + ahead < STEPS
        with nc.Block() as block:
            @block.sync
            def _(sp):
                for to, name in ((wkq, "w_kq"), (bkq, "b_kq"), (wvT, "wvT"), (wp, "wp"), (bv, "bv_cols"), (bp, "bp_rows"),
                                 (gate_w, "gate_w"), (cos, "cos"), (sin, "sin"), (tri, "tri"), (ident, "ident")):
                    sp.dma_start(to[:], d[name]).then_inc(s["consts_in"], 16)

                def load(n):
                    after(sp, s["normed"], n)
                    sp.dma_start(x[:, :, :], rows_in[:, bass.ds(n * GB, GB), :]).then_inc(s["x_in"], 16)

                def residual(n):
                    after(sp, s["h_ready"], n)
                    sp.dma_start(xr[:, :, :], rows_in[:, bass.ds(n * GB, GB), :]).then_inc(s["xr_in"], 16)

                def body(i):
                    if has(i, 3):
                        load(i + 3)
                    if has(i, 1):
                        residual(i + 1)
                    if has(i, 0):
                        sp.wait_ge(s["h_ready"], i + 1)
                        sp.dma_start(rows_h[:, bass.ds(i * GB, GB), :], h[:, :, :]).then_inc(s["h_stored"], 16)
                    if has(i, -1):
                        sp.wait_ge(s["pb_ready"], i)
                        sp.dma_start(rows_t[:, bass.ds((i - 1) * GB, GB), D:D + E], pb[:, :, :]).then_inc(s["pb_stored"], 16)
                        sp.dma_start(rows_p[:, bass.ds((i - 1) * GB, GB), :], pb[:, :, :]).then_inc(s["pb_stored"], 16)
                    if has(i, 0):
                        sp.wait_ge(s["xf_ready"], i + 1)
                        sp.dma_start(rows_t[:, bass.ds(i * GB, GB), 0:D], xf[:, :, :]).then_inc(s["xf_stored"], 16)
                        sp.wait_ge(s["xf_Tc"], i + 1)
                        sp.dma_start(xfT[:, bass.ds(i * W, W)], xfTs[:, :]).then_inc(s["xfT_stored"], 16)
                pipelined(sp, body, STEPS, 3, 1)
                for kind in ("h_stored", "xf_stored", "xfT_stored"):
                    sp.wait_ge(s[kind], 16 * STEPS)
                sp.wait_ge(s["pb_stored"], 32 * STEPS)

            @block.gpsimd
            def _(pool):
                nc.gpsimd.memset(c15[:, :], 1.5).then_inc(s["ready"], 1)
                pool.wait_ge(s["ready"], 1)
                pool.wait_ge(s["consts_in"], 176)

                def body(i):
                    if has(i, 1):
                        pool.wait_ge(s["wei_raw"], i + 2)
                        after(pool, s["out"], i + 1)
                        nc.gpsimd.tensor_tensor(bat(wei[:, :]), bat(raw[:, :]), per_image(tri[:, :], T, T), ALU.mult).then_inc(s["wei_ready"], 1)
                    if has(i, 0):
                        newton_rsqrt(nc, pool, s["newton2_step"], s["rough2"], i, rstd2[:, :], ln2[:, :], mv2[:, :, 1], c15[:, :], 1.0, EPS, s["rstd2"])
                    if has(i, 3):
                        newton_rsqrt(nc, pool, s["newton1_step"], s["rough1"], i + 3, rstd1[:, :], ln1[:, :], mv1[:, :, 1], c15[:, :], 1.0, EPS, s["rstd1"])
                    if has(i, 1):
                        pool.wait_ge(s["xr_in"], 16 * i + 32)
                        nc.gpsimd.tensor_tensor(xr[:, :, :], xr[:, :, :], per_image(bp[:, :], T, D), ALU.add).then_inc(s["xb_ready"], 1)
                pipelined(pool, body, STEPS, 3, 1)

            @block.tensor
            def _(pe):
                pe.wait_ge(s["consts_in"], 176)
                nc.tensor.matmul(ps[:, 0, 0:D], wvT[:, :], wp[:, :], start=True, stop=True)
                nc.tensor.matmul(ps[0:T, 1, 0:D], bv[:, :], wp[:, :], start=True, stop=True).then_inc(s["folded"], 1)
                pe.wait_ge(s["unfolded"], 2)
                pe.wait_ge(s["scaled"], 1)

                def body(i):
                    if has(i, 1):
                        pe.wait_ge(s["kq_rot"], i + 2)
                        after(pe, s["wei_raw"], i + 1)
                        for g in range(GB):
                            c = slice(g * T, (g + 1) * T)
                            last = nc.tensor.matmul(ps_sc[:, c], qT[:, c], kT[:, c], start=True, stop=True)
                        last.then_inc(s["sc"], 1)
                    if has(i, 2):
                        pe.wait_ge(s["normed"], i + 3)
                        after(pe, s["l_sub"], i)
                        for g in range(GB):
                            last = nc.tensor.transpose(ps_T[:, g * T:(g + 1) * T], xn[:, g, :], ident[0:T, 0:T])
                        last.then_inc(s["x_T"], 1)
                        pe.wait_ge(s["x_Tc"], i + 3)
                        for j in range(4):
                            last = nc.tensor.matmul(ps[:, 1 + j, 0:W], wkq[:, j, :], xT[:, :], start=True, stop=True)
                        last.then_inc(s["kq"], 1)
                        after(pe, s["vv_ready"], i + 2)
                        for g in range(GB):
                            last = nc.tensor.matmul(ps_v[:, g * D:(g + 1) * D], xT[:, g * T:(g + 1) * T], wvp[:, :],
                                                    start=True, stop=True)
                        last.then_inc(s["v"], 1)
                    if has(i, 1):
                        pe.wait_ge(s["vv_ready"], i + 2)
                        pe.wait_ge(s["wei_ready"], i + 2)
                        after(pe, s["h_ready"], i + 1)
                        for g in range(GB):
                            last = nc.tensor.matmul(ps_out[:, g * D:(g + 1) * D], wei[:, g * T:(g + 1) * T], vv[:, g, :],
                                                    start=True, stop=True)
                        last.then_inc(s["out"], 1)
                    if has(i, 0):
                        pe.wait_ge(s["xf_ready"], i + 1)
                        for g in range(GB):
                            last = nc.tensor.transpose(ps_T[:, g * T:(g + 1) * T], xf[:, g, :], ident[0:T, 0:T])
                        last.then_inc(s["xf_T"], 1)
                        pe.wait_ge(s["xf_Tc"], i + 1)
                        for g in range(GB):
                            last = nc.tensor.matmul(ps_l[:, g * E:(g + 1) * E], xfTs[:, g * T:(g + 1) * T], gate_w[:, :],
                                                    start=True, stop=True)
                        last.then_inc(s["logits"], 1)
                pipelined(pe, body, STEPS, 3, 1)

            @block.scalar
            def _(a):
                nc.scalar.preload_act_table_set("natural_log_exp_and_others")
                a.wait_ge(s["folded"], 1)
                nc.scalar.activation(wvp[:, :], ps[:, 0, 0:D], ACT.Copy).then_inc(s["unfolded"], 1)
                nc.scalar.activation(bvp[:, :], ps[0:T, 1, 0:D], ACT.Copy).then_inc(s["unfolded"], 1)
                a.wait_ge(s["scaled"], 1)

                def rsqrt(var, n, ln, mv, rstd, step, rough):
                    a.wait_ge(var, n + 1)
                    nc.scalar.activation(ln[:, :], mv[:, :, 1], ACT.Ln, bias=eps[:, 0:1]).then_inc(step, 1)
                    a.wait_ge(step, n + 1)
                    nc.scalar.activation(rstd[:, :], ln[:, :], ACT.Exp, scale=-0.5).then_inc(rough, 1)

                def body(i):
                    if has(i, 1):
                        a.wait_ge(s["sc"], i + 2)
                        nc.scalar.activation(ab[:, :], ps_sc, ACT.Abs).then_inc(s["abs_step"], 1)
                        a.wait_ge(s["abs_step"], i + 2)
                        nc.scalar.activation(ab[:, :], ab[:, :], ACT.Exp, scale=-1.0).then_inc(s["exp_step"], 1)
                        a.wait_ge(s["exp_step"], i + 2)
                        nc.scalar.activation(ab[:, :], ab[:, :], ACT.Ln, bias=1.0).then_inc(s["sp_ln"], 1)
                    if has(i, 2):
                        a.wait_ge(s["x_T"], i + 3)
                        after(a, s["v"], i + 2)
                        nc.scalar.activation(xT[:, :], ps_T, ACT.Copy).then_inc(s["x_Tc"], 1)
                    if has(i, -1):
                        a.wait_ge(s["l_sub"], i)
                        nc.scalar.activation(le[:, :, :], le[:, :, :], ACT.Exp).then_inc(s["l_exp"], 1)
                    if has(i, 0):
                        rsqrt(s["var2"], i, ln2, mv2, rstd2, s["ln2_step"], s["rough2"])
                    if has(i, 3):
                        rsqrt(s["var1"], i + 3, ln1, mv1, rstd1, s["ln1_step"], s["rough1"])
                    if has(i, 0):
                        a.wait_ge(s["xf_T"], i + 1)
                        after(a, s["logits"], i)
                        after(a, s["xfT_stored"], 16 * i)
                        nc.scalar.activation(xfTs[:, :], ps_T, ACT.Copy).then_inc(s["xf_Tc"], 1)
                pipelined(a, body, STEPS, 3, 1)

            @block.vector
            def _(v):
                v.wait_ge(s["consts_in"], 176)
                nc.vector.tensor_scalar(wkq[:, 0:2, :], wkq[:, 0:2, :], D ** -0.5, None, ALU.mult)
                nc.vector.tensor_scalar(bkq[:, 0:2], bkq[:, 0:2], D ** -0.5, None, ALU.mult)
                nc.vector.memset(eps[:, :], EPS).then_inc(s["scaled"], 1)
                v.wait_ge(s["scaled"], 1)
                v.wait_ge(s["unfolded"], 2)

                def rotate(n):
                    st = Steps(v, s["rot_step"], n)
                    v.wait_ge(s["kq"], n + 1)
                    for m, j in enumerate((0, 2)):
                        nc.vector.scalar_tensor_tensor(bat(r1[:, m, :]), bat(ps[:, 1 + j, 0:W]), bkq[:, j:j + 1],
                                                       per_image(cos[:, :], D, T), ALU.add, ALU.mult)
                        last = nc.vector.scalar_tensor_tensor(bat(r2[:, m, :]), bat(ps[:, 2 + j, 0:W]), bkq[:, j + 1:j + 2],
                                                              per_image(sin[:, :], D, T), ALU.add, ALU.mult)
                    st.link(last)
                    after(v, s["sc"], n)
                    nc.vector.tensor_tensor(kT[:, :], r1[:, 0, :], r2[:, 0, :], ALU.add)
                    nc.vector.tensor_tensor(qT[:, :], r1[:, 1, :], r2[:, 1, :], ALU.add).then_inc(s["kq_rot"], 1)

                def body(i):
                    if has(i, 1):
                        rotate(i + 1)
                        v.wait_ge(s["v"], i + 2)
                        after(v, s["out"], i + 1)
                        nc.vector.tensor_tensor(vv[:, :, :], rows(ps_v), per_image(bvp[:, :], T, D), ALU.add).then_inc(s["vv_ready"], 1)
                    if has(i, -1):
                        st = Steps(v, s["max_step"], i - 1)
                        v.wait_ge(s["logits"], i)
                        lg = ps_l.rearrange("p (g e) -> p g e", g=GB)
                        st.link(nc.vector.tensor_reduce(lm[:, :], lg, AX.X, ALU.max))
                        nc.vector.tensor_tensor(le[:, :, :], lg, lm[:, :].unsqueeze(2).to_broadcast([T, GB, E]),
                                                ALU.subtract).then_inc(s["l_sub"], 1)
                    if has(i, 2):
                        v.wait_ge(s["rstd1"], i + 3)
                        after(v, s["x_T"], i + 2)
                        for g in range(GB):
                            last = nc.vector.tensor_scalar(xn[:, g, :], x[:, g, :], mv1[:, g, 0:1], rstd1[:, g:g + 1], ALU.subtract, ALU.mult)
                        last.then_inc(s["normed"], 1)
                    if has(i, 0):
                        v.wait_ge(s["out"], i + 1)
                        v.wait_ge(s["xb_ready"], i + 1)
                        after(v, s["h_stored"], 16 * i)
                        nc.vector.tensor_tensor(h[:, :, :], rows(ps_out), xr[:, :, :], ALU.add).then_inc(s["h_ready"], 1)
                        v.wait_ge(s["h_ready"], i + 1)
                        row_stats(nc, v, s["stat2_step"], i, gate2[:, :], h, stats2, mv2, s["var2"])
                    if has(i, 1):
                        v.wait_ge(s["sp_ln"], i + 2)
                        after(v, s["wei_ready"], i + 1)
                        nc.vector.scalar_tensor_tensor(raw[:, :], ps_sc, 0.0, ab[:, :], ALU.max, ALU.add).then_inc(s["wei_raw"], 1)
                    if has(i, -1):
                        st = Steps(v, s["sum_step"], 2 * (i - 1))
                        v.wait_ge(s["l_exp"], i)
                        st.link(nc.vector.tensor_reduce(ls[:, :], le[:, :, :], AX.X, ALU.add))
                        st.link(nc.vector.reciprocal(ls[:, :], ls[:, :]))
                        after(v, s["pb_stored"], 32 * (i - 1))
                        nc.vector.tensor_tensor(pb[:, :, :], le[:, :, :], ls[:, :].unsqueeze(2).to_broadcast([T, GB, E]),
                                                ALU.mult).then_inc(s["pb_ready"], 1)
                    if has(i, 3):
                        v.wait_ge(s["x_in"], 16 * i + 64)
                        row_stats(nc, v, s["stat1_step"], i + 3, gate1[:, :], x, stats1, mv1, s["var1"])
                    if has(i, 0):
                        v.wait_ge(s["rstd2"], i + 1)
                        after(v, s["xf_T"], i)
                        after(v, s["xf_stored"], 16 * i)
                        for g in range(GB):
                            last = nc.vector.tensor_scalar(xf[:, g, :], h[:, g, :], mv2[:, g, 0:1], rstd2[:, g:g + 1], ALU.subtract, ALU.mult)
                        last.then_inc(s["xf_ready"], 1)
                pipelined(v, body, STEPS, 3, 1)


def attend1(nc, d, src, dst):
    with ExitStack() as ctx:
        def sb(name, shape, dt=F32):
            return ctx.enter_context(nc.sbuf_tensor("a1_" + name, shape, dt))
        wq = sb("wq", [D, D]); wk = sb("wk", [D, D]); wo = sb("wo", [D, D]); bqk = sb("bqk", [D, 2])
        rows1 = sb("rows1", [T, 3, D])
        bound = sb("bound", [T, T]); thirds = sb("thirds", [T, 2, GB])
        ident = sb("ident", [P, P])
        x = sb("x", [T, GB, D]); xr = sb("xr", [T, GB, D]); xn = sb("xn", [T, GB, D]); xb = sb("xb", [T, GB, D]); xb2 = sb("xb2", [T, GB, D])
        stats1 = sb("stats1", [T, GB, 6]); mv1 = sb("mv1", [T, GB, 2]); ln1 = sb("ln1", [T, GB]); rstd1 = sb("rstd1", [T, GB])
        stats2 = sb("stats2", [T, GB, 6]); mv2 = sb("mv2", [T, GB, 2]); ln2 = sb("ln2", [T, GB]); rstd2 = sb("rstd2", [T, GB])
        gate1 = sb("gate1", [T, 1]); gate2 = sb("gate2", [T, 1]); c15 = sb("c15", [T, GB]); eps = sb("eps", [T, 1])
        xT = sb("xT", [D, W]); qT = sb("qT", [D, W]); kT = sb("kT", [D, W]); u = sb("u", [T, GB, D])
        near = sb("near", [T, GB, T]); m = sb("m", [T, 2, GB]); ex = sb("ex", [T, 2, GB, T]); es = sb("es", [T, 2, GB])
        A = sb("A", [T, GB, T]); AT = sb("AT", [T, W]); res = sb("res", [T, GB, D]); y = sb("y", [T, GB, D]); h = sb("h", [T, GB, D])
        ps = ctx.enter_context(nc.psum_tensor("a1_ps", [P, 8, 512], F32))
        ps_xT, ps_q, ps_k, ps_u, ps_sc = ps[:, 0, 0:W], ps[:, 1, 0:W], ps[:, 2, 0:W], ps[0:T, 3, :], ps[0:T, 4, 0:W]
        ps_AT, ps_out = ps[0:T, 5, 0:W], ps[0:T, 6, :]
        s = ctx.enter_context(semaphores(nc, "a1_", """consts_in ready scaled x_in xr_in var1 rough1 rstd1 normed x_T x_Tc qk qk_c u u_c sc near_step max_step m_ready e_out
             recip_step third_step full_step A A_T A_Tc out xb_ready xb_moved res_ready var2 rough2 rstd2 y_ready beta_step gamma_step
             h_ready stored stat1_step stat2_step ln1_step ln2_step newton1_step newton2_step"""))
        rows_in = src.rearrange("(b t) c -> t b c", t=T)
        rows_h = dst.rearrange("(b t) c -> t b c", t=T)
        bat = lambda ap: ap.rearrange("p (g t) -> p g t", g=GB)
        rows = lambda ap: ap.rearrange("p (g c) -> p g c", g=GB)
        per_image = lambda ap, m: ap.unsqueeze(1).to_broadcast([T, GB, m])
        has = lambda i, ahead: not isinstance(i, int) or 0 <= i + ahead < STEPS
        with nc.Block() as block:
            @block.sync
            def _(sp):
                for to, name in ((wq, "wq1"), (wk, "wk1"), (wo, "wo1"), (bqk, "b_qk1"), (rows1, "rows1"), (bound, "bound"),
                                 (thirds, "thirds"), (ident, "ident")):
                    sp.dma_start(to[:], d[name]).then_inc(s["consts_in"], 16)

                def body(i):
                    if has(i, 3):
                        after(sp, s["normed"], i + 3)
                        sp.dma_start(x[:, :, :], rows_in[:, bass.ds((i + 3) * GB, GB), :]).then_inc(s["x_in"], 16)
                    if has(i, -1):
                        sp.wait_ge(s["h_ready"], i)
                        sp.dma_start(rows_h[:, bass.ds((i - 1) * GB, GB), :], h[:, :, :]).then_inc(s["stored"], 16)
                    if has(i, 0):
                        sp.dma_start(xr[:, :, :], rows_in[:, bass.ds(i * GB, GB), :]).then_inc(s["xr_in"], 16)
                pipelined(sp, body, STEPS, 3, 1)
                sp.wait_ge(s["stored"], 16 * STEPS)

            @block.gpsimd
            def _(pool):
                nc.gpsimd.memset(c15[:, :], 1.5).then_inc(s["ready"], 1)
                pool.wait_ge(s["ready"], 1)
                pool.wait_ge(s["consts_in"], 128)

                def body(i):
                    if has(i, -1):
                        pool.wait_ge(s["xr_in"], 16 * i)
                        nc.gpsimd.tensor_tensor(xr[:, :, :], xr[:, :, :], per_image(rows1[:, 2, :], D), ALU.add).then_inc(s["beta_step"], 1)
                        pool.wait_ge(s["y_ready"], i)
                        nc.gpsimd.tensor_tensor(y[:, :, :], y[:, :, :], per_image(rows1[:, 1, :], D), ALU.mult).then_inc(s["gamma_step"], 1)
                        pool.wait_ge(s["gamma_step"], i)
                        pool.wait_ge(s["beta_step"], i)
                        after(pool, s["stored"], 16 * (i - 1))
                        nc.gpsimd.tensor_tensor(h[:, :, :], y[:, :, :], xr[:, :, :], ALU.add).then_inc(s["h_ready"], 1)
                    if has(i, 2):
                        pool.wait_ge(s["normed"], i + 3)
                        after(pool, s["xb_moved"], i + 2)
                        nc.gpsimd.tensor_tensor(xb[:, :, :], xn[:, :, :], per_image(rows1[:, 0, :], D), ALU.add).then_inc(s["xb_ready"], 1)
                    if has(i, 0):
                        newton_rsqrt(nc, pool, s["newton2_step"], s["rough2"], i, rstd2[:, :], ln2[:, :], mv2[:, :, 1], c15[:, :], 1.0, EPS, s["rstd2"])
                    if has(i, 3):
                        newton_rsqrt(nc, pool, s["newton1_step"], s["rough1"], i + 3, rstd1[:, :], ln1[:, :], mv1[:, :, 1], c15[:, :], 1.0, EPS, s["rstd1"])
                pipelined(pool, body, STEPS, 3, 1)

            @block.tensor
            def _(pe):
                pe.wait_ge(s["consts_in"], 128)
                pe.wait_ge(s["scaled"], 1)

                def body(i):
                    if has(i, 2):
                        pe.wait_ge(s["normed"], i + 3)
                        for g in range(GB):
                            last = nc.tensor.transpose(ps_xT[:, g * T:(g + 1) * T], xn[:, g, :], ident[0:T, 0:T])
                        last.then_inc(s["x_T"], 1)
                        pe.wait_ge(s["x_Tc"], i + 3)
                        nc.tensor.matmul(ps_q, wq[:, :], xT[:, :], start=True, stop=True)
                        nc.tensor.matmul(ps_k, wk[:, :], xT[:, :], start=True, stop=True).then_inc(s["qk"], 1)
                        after(pe, s["u_c"], i + 2)
                        for g in range(GB):
                            last = nc.tensor.matmul(ps_u[:, g * D:(g + 1) * D], xT[:, g * T:(g + 1) * T], wo[:, :],
                                                    start=True, stop=True)
                        last.then_inc(s["u"], 1)
                    if has(i, 2):
                        pe.wait_ge(s["qk_c"], i + 3)
                        after(pe, s["e_out"], i + 2)
                        for g in range(GB):
                            c = slice(g * T, (g + 1) * T)
                            last = nc.tensor.matmul(ps_sc[:, c], qT[:, c], kT[:, c], start=True, stop=True)
                        last.then_inc(s["sc"], 1)
                    if has(i, 1):
                        pe.wait_ge(s["A"], i + 2)
                        for g in range(GB):
                            last = nc.tensor.transpose(ps_AT[:, g * T:(g + 1) * T], A[:, g, :], ident[0:T, 0:T])
                        last.then_inc(s["A_T"], 1)
                        pe.wait_ge(s["A_Tc"], i + 2)
                        pe.wait_ge(s["u_c"], i + 2)
                        after(pe, s["res_ready"], i + 1)
                        for g in range(GB):
                            last = nc.tensor.matmul(ps_out[:, g * D:(g + 1) * D], AT[:, g * T:(g + 1) * T], u[:, g, :],
                                                    start=True, stop=True)
                        last.then_inc(s["out"], 1)
                pipelined(pe, body, STEPS, 3, 1)

            @block.scalar
            def _(a):
                nc.scalar.preload_act_table_set("natural_log_exp_and_others")
                a.wait_ge(s["consts_in"], 128)
                a.wait_ge(s["scaled"], 1)

                def rsqrt(var, n, ln, mv, rstd, step, rough):
                    a.wait_ge(var, n + 1)
                    nc.scalar.activation(ln[:, :], mv[:, :, 1], ACT.Ln, bias=eps[:, 0:1]).then_inc(step, 1)
                    a.wait_ge(step, n + 1)
                    nc.scalar.activation(rstd[:, :], ln[:, :], ACT.Exp, scale=-0.5).then_inc(rough, 1)

                def body(i):
                    if has(i, 2):
                        a.wait_ge(s["x_T"], i + 3)
                        after(a, s["u"], i + 2)
                        nc.scalar.activation(xT[:, :], ps_xT, ACT.Copy).then_inc(s["x_Tc"], 1)
                    if has(i, 1):
                        a.wait_ge(s["m_ready"], i + 2)
                        after(a, s["A"], i + 1)
                        for g in range(GB):
                            nc.scalar.activation(ex[:, 0, g, :], ps_sc[:, g * T:(g + 1) * T], ACT.Exp, bias=m[:, 0, g:g + 1],
                                                 accum_out=es[:, 0, g:g + 1])
                            last = nc.scalar.activation(ex[:, 1, g, :], near[:, g, :], ACT.Exp, bias=m[:, 1, g:g + 1],
                                                        accum_out=es[:, 1, g:g + 1])
                        last.then_inc(s["e_out"], 1)
                    if has(i, 0):
                        rsqrt(s["var2"], i, ln2, mv2, rstd2, s["ln2_step"], s["rough2"])
                    if has(i, 2):
                        a.wait_ge(s["qk"], i + 3)
                        after(a, s["sc"], i + 2)
                        nc.scalar.activation(qT[:, :], ps_q, ACT.Identity, bias=bqk[:, 0:1])
                        nc.scalar.activation(kT[:, :], ps_k, ACT.Identity, bias=bqk[:, 1:2]).then_inc(s["qk_c"], 1)
                    if has(i, 3):
                        rsqrt(s["var1"], i + 3, ln1, mv1, rstd1, s["ln1_step"], s["rough1"])
                    if has(i, 1):
                        a.wait_ge(s["xb_ready"], i + 2)
                        after(a, s["res_ready"], i + 1)
                        nc.scalar.activation(xb2[:, :, :], xb[:, :, :], ACT.Copy).then_inc(s["xb_moved"], 1)
                        a.wait_ge(s["A_T"], i + 2)
                        after(a, s["out"], i + 1)
                        nc.scalar.activation(AT[:, :], ps_AT, ACT.Copy).then_inc(s["A_Tc"], 1)
                    if has(i, 2):
                        a.wait_ge(s["u"], i + 3)
                        after(a, s["out"], i + 2)
                        nc.scalar.activation(u[:, :, :].rearrange("p g c -> p (g c)"), ps_u, ACT.Copy).then_inc(s["u_c"], 1)
                pipelined(a, body, STEPS, 3, 1)

            @block.vector
            def _(v):
                v.wait_ge(s["consts_in"], 128)
                nc.vector.tensor_scalar(wq[:, :], wq[:, :], D ** -0.5, None, ALU.mult)
                nc.vector.tensor_scalar(bqk[:, 0:1], bqk[:, 0:1], D ** -0.5, None, ALU.mult)
                nc.vector.memset(eps[:, :], EPS).then_inc(s["scaled"], 1)
                v.wait_ge(s["scaled"], 1)

                def body(i):
                    if has(i, 2):
                        v.wait_ge(s["rstd1"], i + 3)
                        after(v, s["x_T"], i + 2)
                        after(v, s["xb_ready"], i + 2)
                        for g in range(GB):
                            last = nc.vector.tensor_scalar(xn[:, g, :], x[:, g, :], mv1[:, g, 0:1], rstd1[:, g:g + 1], ALU.subtract, ALU.mult)
                        last.then_inc(s["normed"], 1)
                    if has(i, 1):
                        v.wait_ge(s["sc"], i + 2)
                        after(v, s["e_out"], i + 1)
                        nc.vector.tensor_reduce(m[:, 0, :], bat(ps_sc), AX.X, ALU.max)
                        nc.vector.tensor_tensor(near[:, :, :], bat(ps_sc), per_image(bound[:, :], T), ALU.min).then_inc(s["near_step"], 1)
                        v.wait_ge(s["near_step"], i + 2)
                        nc.vector.tensor_reduce(m[:, 1, :], near[:, :, :], AX.X, ALU.max).then_inc(s["max_step"], 1)
                        v.wait_ge(s["max_step"], i + 2)
                        nc.vector.tensor_scalar(m[:, :, :], m[:, :, :], -1.0, None, ALU.mult).then_inc(s["m_ready"], 1)
                    if has(i, 0):
                        v.wait_ge(s["out"], i + 1)
                        v.wait_ge(s["xb_moved"], i + 1)
                        after(v, s["y_ready"], i)
                        nc.vector.tensor_tensor(res[:, :, :], rows(ps_out), xb2[:, :, :], ALU.add).then_inc(s["res_ready"], 1)
                        v.wait_ge(s["res_ready"], i + 1)
                        row_stats(nc, v, s["stat2_step"], i, gate2[:, :], res, stats2, mv2, s["var2"])
                    if has(i, 3):
                        v.wait_ge(s["x_in"], 16 * i + 64)
                        row_stats(nc, v, s["stat1_step"], i + 3, gate1[:, :], x, stats1, mv1, s["var1"])
                    if has(i, 1):
                        v.wait_ge(s["e_out"], i + 2)
                        after(v, s["A_T"], i + 1)
                        nc.vector.reciprocal(es[:, :, :], es[:, :, :]).then_inc(s["recip_step"], 1)
                        v.wait_ge(s["recip_step"], i + 2)
                        nc.vector.tensor_tensor(es[:, :, :], es[:, :, :], thirds[:, :, :], ALU.mult).then_inc(s["third_step"], 1)
                        v.wait_ge(s["third_step"], i + 2)
                        for g in range(GB):
                            last = nc.vector.tensor_scalar(ex[:, 0, g, :], ex[:, 0, g, :], es[:, 0, g:g + 1], None, ALU.mult)
                        last.then_inc(s["full_step"], 1)
                        v.wait_ge(s["full_step"], i + 2)
                        for g in range(GB):
                            last = nc.vector.scalar_tensor_tensor(A[:, g, :], ex[:, 1, g, :], es[:, 1, g:g + 1], ex[:, 0, g, :], ALU.mult, ALU.add)
                        last.then_inc(s["A"], 1)
                    if has(i, 0):
                        v.wait_ge(s["rstd2"], i + 1)
                        after(v, s["h_ready"], i)
                        for g in range(GB):
                            last = nc.vector.tensor_scalar(y[:, g, :], res[:, g, :], mv2[:, g, 0:1], rstd2[:, g:g + 1], ALU.subtract, ALU.mult)
                        last.then_inc(s["y_ready"], 1)

                pipelined(v, body, STEPS, 3, 1)


def attention_layout(i):
    c_ = np.ascontiguousarray
    W_ = i['L0_tok_W']
    pos = i['L0_tok_pos_embed']
    xp = i['x'].reshape(16, 8, 3, 8, 28, 8, 28).transpose(0, 2, 4, 6, 1, 3, 5).reshape(16, 2352, 512)
    sw = np.arange(128) ^ 1
    t = np.arange(T - 1, -1, -1)[None, :]
    ang = (t * (np.arange(128)[:, None] // 2)).astype(np.float64)
    sg = np.where(np.arange(128) % 2 == 0, -1.0, 1.0)[:, None]
    Wk, Wq, bk, bq = i['L0_attn_Wk'], i['L0_attn_Wq'], i['L0_attn_bk'], i['L0_attn_bq']
    tt = np.arange(T)
    return dict(
        w_tok=c_(W_.T[:18 * 128].reshape(18, 128, 128).transpose(1, 0, 2)), w_tok_rest=c_(W_.T[18 * 128:]),
        b_tok=c_(i['L0_tok_b'][:, None]), pos_cols=c_(pos.T), cls_col=c_(i['L0_tok_class_token'].T),
        x_main=c_(xp[:, :18 * 128].reshape(16, 18, 128, 512).transpose(0, 2, 1, 3)), x_rest=c_(xp[:, 18 * 128:]),
        ident=np.eye(128, dtype=np.float32),
        w_kq=c_(np.stack([Wk, Wk[:, sw], Wq, Wq[:, sw]], 1)), b_kq=c_(np.stack([bk, bk[sw], bq, bq[sw]], 1)),
        wvT=c_(i['L0_attn_Wv'].T), wp=c_(i['L0_attn_Wp']), bv_cols=c_(np.broadcast_to(i['L0_attn_bv'][:, None], (128, T))),
        bp_rows=c_(np.broadcast_to(i['L0_attn_bp'], (T, 128))), gate_w=c_(i['L0_ffn_gate_w']),
        cos=np.cos(ang).astype(np.float32), sin=(sg * np.sin(ang)).astype(np.float32), tri=np.triu(np.ones((T, T), np.float32)),
        wq1=c_(i['L1_attn_Wq']), wk1=c_(i['L1_attn_Wk']), wo1=c_(i['L1_attn_Wo']), b_qk1=c_(np.stack([i['L1_attn_bq'], i['L1_attn_bk']], 1)),
        rows1=c_(np.broadcast_to(np.stack([i['L1_attn_bo'], i['L1_attn_gamma'], i['L1_attn_beta']]), (T, 3, 128))),
        bound=np.where(abs(tt[:, None] - tt[None, :]) <= 12, np.float32(3.4e38), np.float32(-1e9)),
        thirds=c_(np.broadcast_to(np.array([2 / 3, 1 / 3], np.float32)[None, :, None], (T, 2, GB))))


E_ = 16
CAP = N // E_
CC, CP = 5, 104
SEG = P // E_
ST = N // SEG
GC = ST // CP
LO, HI = 32, CAP // 32 + 1
QE = 4
HID = 512


def mixture(nc, d, h1, table, probs, xfT, places, h2, cap=CAP):
    BITS, BIT_BLOCKS = 30, 10
    HALF = CAP // 2
    QUADS = E_ // QE
    QA = QUADS // 2
    RC = GC * QA * SEG
    QH = QUADS * HI
    CUTS = ((0, 4), (4, 8), (8, GC))
    RING = 4
    with ExitStack() as ctx:
        def sb(name, shape, dt=F32):
            return ctx.enter_context(nc.sbuf_tensor("mx_" + name, shape, dt))
        s = ctx.enter_context(semaphores(nc, "mx_", """consts_in p_in permuted p_T0 p_T1 p_T2 p_out0 p_out1 p_out2 bit_step bit_shift cnt total step cnt2 totals
                              cnt3 sel_total off_read rank_ready r_T0 r_T1 r_T2 r_out0 r_out1 r_out2 hots_ready masks_ready list_mm group_mm group_read
                              list_ready list_T tokT_ready written back_in back_T lists_ready
                              w_s_in x_in0 x_in1 h1_in0 h1_in1 h1_b2 up gelu down y_raw y_sum stored0 stored1
                              spare idx w_in0 w_in1 tok_in0 tok_in1 pool_gate tok_T tok_Tc scattered y_b2 y_ready"""))
        raw = sb("raw", [CP, SEG, GC, E_]); rawp = sb("rawp", [CP, GC, E_, SEG])
        pr = sb("pr", [P, ST]); reach = sb("reach", [P, ST], F16); gt = sb("gt", [P, ST]); eq = sb("eq", [P, ST])
        incl = sb("incl", [P, ST]); rank = sb("rank", [P, ST]); ones_row = sb("ones_row", [P, ST])
        of_expert = sb("of_expert", [P, P]); before = sb("before", [P, P]); ident = sb("ident", [P, P])
        quad = sb("quad", [P, QUADS]); quad_h = sb("quad_h", [P, QUADS], F16); member = sb("member", [P, QE])
        slot = sb("slot", [P, HI * LO], F16); slot_f = sb("slot_f", [P, HI * LO]); row_no = sb("row_no", [P, 1])
        thr = sb("thr", [P, 1]); cand = sb("cand", [P, 1]); kept = sb("kept", [P, 1]); bit = sb("bit", [P, 1], I32)
        cnt = sb("cnt", [P, 1]); cnt_gt = sb("cnt_gt", [P, 1]); cnt_eq = sb("cnt_eq", [P, 1]); cnt_sel = sb("cnt_sel", [P, 1])
        need = sb("need", [P, 1]); off = sb("off", [P, 1]); edge = sb("edge", [P, GC])
        r1 = sb("r1", [CP, QE, 2, RC], U16); lo = sb("lo", [CP, QE, 2, RC], U16); hi = sb("hi", [CP, QE, 2, RC], U16)
        hot_lo = sb("hot_lo", [CP, QE, LO, RC], BF16); hot_hi = sb("hot_hi", [CP, QE, HI, RC], BF16)
        past = sb("past", [P, HI * LO], F16); past_m = sb("past_m", [P, HI, QE, LO], F16)
        tok_no = sb("tok_no", [P, QUADS, HI]); grp = sb("grp", [P, QUADS, HI]); tokT = sb("tokT", [QH, P])
        back = sb("back", [E_, CAP]); lists_sb = sb("lists", [CP, E_ + 2, CC], U32)
        PACK = HID + HID + 4 + D
        w_s = sb("w_s", [P, PACK]); w_e = sb("w_e", [P, 2, PACK])
        xT = sb("xT", [D, 2, CAP]); hT = sb("hT", [P, 4, CAP])
        h1_s = sb("h1_s", [CP, 2, CC, D]); y = sb("y", [CP, 2, CC, D])
        idx = sb("idx", [CP, RING, CC], U32); tok = sb("tok", [CP, 2, CC, D + E_]); score = sb("score", [CP, 2, CC])
        gate_in = sb("gate_in", [16, 1]); gate_out = sb("gate_out", [16, 1])
        ps = ctx.enter_context(nc.psum_tensor("mx_ps", [P, 8, 512], F32))
        ps_total, ps_eq = ps[:, 6, 0:1], ps[:, 6, 1:2]
        parts = lambda w: (w[:, 0:HID], w[:, HID:2 * HID].rearrange("p (j c) -> p j c", j=4), w[:, 2 * HID:2 * HID + 4],
                           w[0:CP, 2 * HID + 4:])
        h1r = h1.rearrange("(i c p) k -> p i c k", c=CC, p=CP)
        h2r = h2.rearrange("(i c p) k -> p i c k", c=CC, p=CP)
        chunk_sets = ((4, 0, 4), (5, 4, 1))

        def rounds(eng, body, count, ring):
            for k in range(ring):
                body(k, k)
            with eng.Fori(1, count // ring) as g:
                for k in range(ring):
                    body(ring * g + k, k)

        def visits(n, k, ring, parity):
            return n // 2 + 1 if isinstance(n, int) else (n - k) // 2 + k // 2 + 1

        with nc.Block() as block:
            @block.sync
            def _(sp):
                sp.dma_start(raw[:, :, :, :], probs.rearrange("(s c p) e -> p s c e", p=CP, c=GC)).then_inc(s["p_in"], 16)
                for to, name in ((ident, "ident"), (of_expert, "of_expert"), (bit, "first_bit"), (before, "before"), (quad, "quad"),
                                 (member, "member"), (slot_f, "slot"), (row_no, "row_no")):
                    sp.dma_start(to[:], d[name]).then_inc(s["consts_in"], 16)
                sp.dma_start(w_s[:, :], d["w_ffn"][E_]).then_inc(s["w_s_in"], 16)

                def load(n, k):
                    after(sp, s["y_sum"], n - 1)
                    sp.dma_start(xT[:, k, :], xfT[:, bass.ds(n * CAP, CAP)]).then_inc(s[f"x_in{k}"], 16)
                    sp.dma_start(h1_s[:, k], h1r[:, bass.ds(n, 1)].rearrange("p i c k -> p (i c) k")).then_inc(s[f"h1_in{k}"], 16)
                rounds(sp, load, E_, 2)

                def weights(e, k):
                    after(sp, s["y_ready"], e - 1)
                    sp.dma_start(w_e[:, k], d["w_ffn"][bass.ds(e, 1)].rearrange("e p c -> (e p) c")).then_inc(s[f"w_in{k}"], 16)
                weights(0, 0)
                weights(1, 1)
                sp.wait_ge(s["tokT_ready"], 1)
                pl = places.rearrange("(q k) (h l) -> q h k l", k=QE, l=LO)
                for q in range(QUADS):
                    sp.dma_start(pl[q], tokT[q * HI:(q + 1) * HI, :].rearrange("h (k l) -> h k l", l=LO)).then_inc(s["written"], 16)
                sp.wait_ge(s["written"], 16 * QUADS)
                sp.dma_start(back[:, :], places[:, 1:1 + CAP]).then_inc(s["back_in"], 16)
                with sp.Fori(1, E_ // 2) as g:
                    for k in range(2):
                        weights(2 * g + k, k)

            @block.gpsimd
            def _(pool):
                nc.gpsimd.memset(gate_in[:, :], 0.0).then_inc(s["pool_gate"], 1)
                pool.wait_ge(s["w_s_in"], 16)
                b2 = parts(w_s)[3]

                def shared(n, k):
                    pool.wait_ge(s[f"h1_in{k}"], 16 * visits(n, k, 2, 2))
                    nc.gpsimd.tensor_tensor(h1_s[:, k], h1_s[:, k], b2.unsqueeze(1).to_broadcast([CP, CC, D]), ALU.add).then_inc(s["h1_b2"], 1)
                    pool.wait_ge(s["h1_b2"], n + 1)
                    pool.wait_ge(s["y_raw"], n + 1)
                    nc.gpsimd.tensor_tensor(y[:, k], y[:, k], h1_s[:, k], ALU.add).then_inc(s["y_sum"], 1)
                    pool.wait_ge(s["y_sum"], n + 1)
                    pool.dma_start(h2r[:, bass.ds(n, 1)].rearrange("p i c k -> p (i c) k"), y[:, k]).then_inc(s[f"stored{k}"], 16)
                rounds(pool, shared, E_, 2)

                def gate(n):
                    pool.wait_ge(s["pool_gate"], n + 1)
                    nc.gpsimd.tensor_tensor(gate_out[:, :], gate_in[:, :], gate_in[:, :], ALU.add).then_inc(s["pool_gate"], 1)

                def gather(e, k, gates):
                    pool.wait_ge(s["idx"], e + 1)
                    after(pool, s["tok_Tc"], e - 1)
                    gate(gates)
                    for c in range(CC):
                        pool.indirect_dma_start(out=tok[:, k % 2, c, :], out_offset=None, in_=table[:, :],
                                                in_offset=bass.IndirectOffsetOnAxis(ap=idx[:, k, c:c + 1], axis=0)).then_inc(s[f"tok_in{k % 2}"], 16)

                def scatter(e, k, gates):
                    pool.wait_ge(s["y_ready"], e + 1)
                    after(pool, s["scattered"], 16 * CC * e)
                    gate(gates)
                    for c in range(CC):
                        pool.indirect_dma_start(out=h2[:, :], out_offset=bass.IndirectOffsetOnAxis(ap=idx[:, k, c:c + 1], axis=0),
                                                in_=y[:, k % 2, c, :], in_offset=None, compute_op=ALU.add).then_inc(s["scattered"], 16)

                def routed(e, k):
                    gather(e + 1, (k + 1) % RING, 2 * e if not isinstance(e, int) or e > 0 else 1)
                    if isinstance(e, int) and e == 1:
                        for j in range(2):
                            pool.wait_ge(s[f"stored{j}"], 16 * (E_ // 2))
                    if not isinstance(e, int) or e > 0:
                        scatter(e - 1, (k - 1) % RING, 2 * e + 1)
                gather(0, 0, 0)
                rounds(pool, routed, E_, RING)
                scatter(E_ - 1, (E_ - 1) % RING, 2 * E_)
                pool.wait_ge(s["tok_in0"], 16 * CC * (E_ // 2 + 1))
                pool.wait_ge(s["scattered"], 16 * CC * E_)

            @block.tensor
            def _(pe):
                def up(n, w, x, j):
                    after(pe, s["gelu"], 4 * n + j - 1)
                    w1 = parts(w)[0]
                    for m in range(2):
                        last = nc.tensor.matmul(ps[:, 2 * (j % 2) + m, 0:HALF], w1[:, j * P:(j + 1) * P], x[:, m * HALF:(m + 1) * HALF],
                                                start=True, stop=True)
                    last.then_inc(s["up"], 1)

                def down(n, w):
                    w2 = parts(w)[1]
                    pe.wait_ge(s["gelu"], 4 * n + 4)
                    after(pe, s["y_raw"] if isinstance(n, int) and n <= E_ or not isinstance(n, int) and w is w_s else s["y_b2"],
                          n if isinstance(n, int) and n <= E_ or not isinstance(n, int) and w is w_s else n - E_)
                    for c in range(CC):
                        for j in range(4):
                            last = nc.tensor.matmul(ps[0:CP, 4 + c // 4, (c % 4) * D:(c % 4 + 1) * D], hT[:, j, c * CP:(c + 1) * CP],
                                                    w2[:, j, :], start=(j == 0), stop=(j == 3))
                    last.then_inc(s["down"], 1)

                def shared(n, k, between):
                    pe.wait_ge(s[f"x_in{k}"], 16 * visits(n, k, 2, 2))
                    for m in range(2):
                        up(n, w_s, xT[:, k, :], 2 * m)
                        up(n, w_s, xT[:, k, :], 2 * m + 1)
                        between[m]()
                    down(n, w_s)
                    between[2]()

                pe.wait_ge(s["consts_in"], 128)
                pe.wait_ge(s["permuted"], 1)
                for r, (c0, c1) in enumerate(CUTS):
                    if r == 2:
                        pe.wait_ge(s["p_out0"], 1)
                    for c in range(c0, c1):
                        last = nc.tensor.transpose(ps[:, 6 + r % 2, (c - c0) * CP:(c - c0 + 1) * CP], rawp[:, c].rearrange("p e s -> p (e s)"), ident[0:CP, 0:CP])
                    last.then_inc(s[f"p_T{r}"], 1)
                pe.wait_ge(s["p_out2"], 1)
                pe.wait_ge(s["w_s_in"], 16)

                def count(i):
                    def f():
                        pe.wait_ge(s["cnt"], i + 1)
                        nc.tensor.matmul(ps_total, of_expert[:, :], cnt[:, :], start=True, stop=True).then_inc(s["total"], 1)
                    return f

                def bits(n, k):
                    shared(n, k, [count(3 * n + m) for m in range(3)])
                assert BITS == 3 * BIT_BLOCKS
                bits(0, 0)
                bits(1, 1)
                with pe.Fori(1, BIT_BLOCKS // 2) as g:
                    for k in range(2):
                        bits(2 * g + k, k)

                def totals():
                    pe.wait_ge(s["cnt2"], 1)
                    nc.tensor.matmul(ps_total, of_expert[:, :], cnt_gt[:, :], start=True, stop=True)
                    nc.tensor.matmul(ps_eq, before[:, :], cnt_eq[:, :], start=True, stop=True).then_inc(s["totals"], 1)

                def sel_total():
                    pe.wait_ge(s["cnt3"], 1)
                    nc.tensor.matmul(ps_total, before[:, :], cnt_sel[:, :], start=True, stop=True).then_inc(s["sel_total"], 1)

                def turn_ranks(r):
                    def f():
                        pe.wait_ge(s["rank_ready"], 1)
                        if r == 2:
                            pe.wait_ge(s["r_out0"], 1)
                        c0, c1 = CUTS[r]
                        for c in range(c0, c1):
                            last = nc.tensor.transpose(ps[0:CP, 6 + r % 2, (c - c0) * P:(c - c0 + 1) * P], rank[:, c * CP:(c + 1) * CP], ident[:, :])
                        last.then_inc(s[f"r_T{r}"], 1)
                    return f

                def groups():
                    pe.wait_ge(s["masks_ready"], 1)
                    pe.wait_ge(s["r_out2"], 1)
                    for h in range(HI):
                        last = nc.tensor.matmul(ps[:, 6, 0:QH].rearrange("p (q h) -> p q h", h=HI)[:, :, h], past_m[:, h].rearrange("p k l -> p (k l)"),
                                                quad_h[:, :], start=True, stop=True)
                    last.then_inc(s["group_mm"], 1)

                def rows(half):
                    def f():
                        pe.wait_ge(s["hots_ready"], half + 1)
                        pe.wait_ge(s["r_out1"], 1)
                        v_lo = hot_lo[:, :, :, :].rearrange("p k l (c q s) -> p c q s (k l)", c=GC, q=QA)
                        v_hi = hot_hi[:, :, :, :].rearrange("p k h (c q s) -> p c q s (k h)", c=GC, q=QA)
                        for q in range(QA):
                            for c in range(GC):
                                for g in range(SEG):
                                    at = (half * QA + q) * QE * HI
                                    last = nc.tensor.matmul(ps[:, 7, at:at + QE * HI], v_lo[:, c, q, g], v_hi[:, c, q, g],
                                                            start=(c == 0 and g == 0), stop=(c == GC - 1 and g == SEG - 1))
                        last.then_inc(s["list_mm"], 1)
                    return f

                def turn_list():
                    pe.wait_ge(s["list_ready"], 1)
                    nc.tensor.transpose(ps[0:QH, 6, 0:P], tok_no[:, :, :].rearrange("p q h -> p (q h)"), ident[:, :]).then_inc(s["list_T"], 1)

                def turn_back():
                    pe.wait_ge(s["back_in"], 16)
                    for c in range(CC):
                        last = nc.tensor.transpose(ps[0:CP, 7, c * E_:(c + 1) * E_], back[:, c * CP:(c + 1) * CP], ident[0:E_, 0:E_])
                    last.then_inc(s["back_T"], 1)
                none = lambda: None
                steps = {(10, 1): totals, (10, 2): sel_total, (11, 1): turn_ranks(0), (11, 2): turn_ranks(1), (12, 0): turn_ranks(2),
                         (12, 2): groups, (13, 1): rows(0), (14, 1): rows(1), (14, 2): turn_list}
                for n in range(BIT_BLOCKS, E_):
                    shared(n, n % 2, [steps.get((n, m), none) for m in range(3)])
                turn_back()

                def routed(e, k):
                    pe.wait_ge(s[f"tok_in{k % 2}"], 16 * CC * visits(e, k, RING, 2))
                    pe.wait_ge(s["lists_ready"], 1)
                    after(pe, s["tok_Tc"], e)
                    for c in range(CC):
                        last = nc.tensor.transpose(ps[:, 6 + c // 4, (c % 4) * CP:(c % 4 + 1) * CP], tok[:, k % 2, c, 0:D], ident[0:CP, 0:CP])
                    last.then_inc(s["tok_T"], 1)
                    if not isinstance(e, int) or e > 0:
                        down(E_ + e - 1, w_e[:, (k - 1) % 2, :])
                    pe.wait_ge(s["tok_Tc"], e + 1)
                    pe.wait_ge(s[f"w_in{k % 2}"], 16 * visits(e, k, RING, 2))
                    for j in range(4):
                        up(E_ + e, w_e[:, k % 2, :], xT[:, k % 2, :], j)
                rounds(pe, routed, E_, RING)
                down(2 * E_ - 1, w_e[:, (E_ - 1) % 2, :])

            @block.scalar
            def _(a):
                a.wait_ge(s["w_s_in"], 16)

                def gelus(n, w):
                    b1 = parts(w)[2]
                    for j in range(4):
                        a.wait_ge(s["up"], 4 * n + j + 1)
                        if j == 0:
                            after(a, s["down"], n)
                        nc.scalar.activation(hT[:, j, :].rearrange("p (k c) -> p k c", k=2), ps[:, 2 * (j % 2):2 * (j % 2) + 2, 0:HALF],
                                             ACT.Gelu_apprx_tanh, bias=b1[:, j:j + 1]).then_inc(s["gelu"], 1)

                def shared(n, k):
                    gelus(n, w_s)
                    a.wait_ge(s["down"], n + 1)
                    after(a, s[f"stored{k}"], 16 * (visits(n, k, 2, 2) - 1))
                    for bank, c0, m in chunk_sets:
                        last = nc.scalar.activation(y[:, k, c0:c0 + m, :].rearrange("p c k -> p (c k)"), ps[0:CP, bank, 0:m * D], ACT.Copy)
                    last.then_inc(s["y_raw"], 1)
                rounds(a, shared, E_, 2)
                rounds(a, lambda e, k: gelus(E_ + e, w_e[:, k % 2, :]), E_, 2)

            @block.vector
            def _(v):
                st = Steps(v, s["step"])
                st.mark(nc.vector.memset(ones_row[:, :], 1.0))
                st.mark(nc.vector.memset(thr[:, :], 0.0))
                nc.vector.memset(lists_sb[:, E_:E_ + 2, :].bitcast(F32), 0.0).then_inc(s["spare"], 1)
                v.wait_ge(s["p_in"], 16)
                for e in range(E_):
                    last = nc.vector.tensor_copy(rawp[:, :, e, :], raw[:, :, :, e].rearrange("p s c -> p c s"))
                last.then_inc(s["permuted"], 1)
                v.wait_ge(s["consts_in"], 128)
                nc.vector.tensor_copy(slot[:, :], slot_f[:, :])
                st.link(nc.vector.tensor_copy(quad_h[:, :], quad[:, :]))
                for r, (c0, c1) in enumerate(CUTS):
                    v.wait_ge(s[f"p_T{r}"], 1)
                    nc.vector.tensor_copy(pr[:, c0 * CP:c1 * CP], ps[:, 6 + r % 2, 0:(c1 - c0) * CP]).then_inc(s[f"p_out{r}"], 1)
                v.wait_ge(s["p_out2"], 1)
                PER = 3
                with v.Fori(0, BITS) as i:
                    b_ = Steps(v, s["bit_step"], PER * i)
                    b_.link(nc.vector.tensor_tensor(cand[:, :].bitcast(I32), thr[:, :].bitcast(I32), bit[:, :], ALU.bitwise_or))
                    nc.vector.tensor_scalar(reach[:, :], pr[:, :], cand[:, 0:1], 0.0, ALU.is_ge, ALU.add, accum_out=cnt[:, 0:1]).then_inc(s["cnt"], 1)
                    nc.vector.tensor_scalar(bit[:, :], bit[:, :], 1, None, ALU.logical_shift_right).then_inc(s["bit_shift"], 1)
                    v.wait_ge(s["total"], i + 1)
                    b_.link(nc.vector.scalar_tensor_tensor(kept[:, :], ps_total, cap - 0.5, cand[:, :], ALU.is_gt, ALU.mult))
                    b_.link(nc.vector.tensor_tensor(thr[:, :], thr[:, :], kept[:, :], ALU.max))
                    assert b_.n == PER
                st.mark(nc.vector.tensor_scalar(gt[:, :], pr[:, :], thr[:, 0:1], 0.0, ALU.is_gt, ALU.add, accum_out=cnt_gt[:, 0:1]))
                st.link(nc.vector.tensor_scalar(eq[:, :], pr[:, :], thr[:, 0:1], None, ALU.is_equal))
                st.link(nc.vector.tensor_tensor_scan(incl[:, :], ones_row[:, :], eq[:, :], 0.0, ALU.mult, ALU.add))
                nc.vector.tensor_copy(cnt_eq[:, :], incl[:, ST - 1:ST]).then_inc(s["cnt2"], 1)
                v.wait_ge(s["totals"], 1)
                st.link(nc.vector.tensor_scalar(need[:, :], ps_total, -1.0, float(cap), ALU.mult, ALU.add))
                st.link(nc.vector.tensor_tensor(need[:, :], need[:, :], ps_eq, ALU.subtract))
                st.link(nc.vector.scalar_tensor_tensor(eq[:, :], incl[:, :], need[:, 0:1], eq[:, :], ALU.is_le, ALU.mult))
                st.link(nc.vector.tensor_tensor(gt[:, :], gt[:, :], eq[:, :], ALU.add))
                st.link(nc.vector.tensor_tensor_scan(incl[:, :], ones_row[:, :], gt[:, :], 0.0, ALU.mult, ALU.add))
                nc.vector.tensor_copy(cnt_sel[:, :], incl[:, ST - 1:ST]).then_inc(s["cnt3"], 1)
                v.wait_ge(s["sel_total"], 1)
                nc.vector.tensor_copy(off[:, :], ps_total).then_inc(s["off_read"], 1)
                v.wait_ge(s["off_read"], 1)
                nc.vector.scalar_tensor_tensor(rank[:, :], incl[:, :], off[:, 0:1], gt[:, :], ALU.add, ALU.mult).then_inc(s["rank_ready"], 1)
                st.link(nc.vector.tensor_scalar(edge[:, :], incl[:, CP - 1:ST:CP], off[:, 0:1], None, ALU.add))
                st.link(nc.vector.tensor_scalar(past[:, :], slot[:, :], edge[:, 0:1], None, ALU.is_gt))
                for c in range(1, GC):
                    st.link(nc.vector.scalar_tensor_tensor(past[:, :], slot[:, :], edge[:, c:c + 1], past[:, :], ALU.is_gt, ALU.add))
                for k in range(QE):
                    last = nc.vector.tensor_scalar(past_m[:, :, k, :], past[:, :].rearrange("p (h l) -> p h l", l=LO), member[:, k:k + 1], None, ALU.mult)
                last.then_inc(s["masks_ready"], 1)
                for r, (c0, c1) in enumerate(CUTS):
                    v.wait_ge(s[f"r_T{r}"], 1)
                    for k in range(QE):
                        for half in range(2):
                            last = nc.vector.tensor_copy(
                                r1[:, k, half, :].rearrange("p (c q s) -> p c q s", c=GC, q=QA)[:, c0:c1],
                                ps[0:CP, 6 + r % 2, 0:(c1 - c0) * P].rearrange("p (c h q k s) -> p h k c q s", h=2, q=QA, k=QE, s=SEG)[:, half, k])
                    last.then_inc(s[f"r_out{r}"], 1)
                v.wait_ge(s["r_out2"], 1)
                nc.vector.tensor_scalar(lo[:, :, :, :], r1[:, :, :, :], LO - 1, None, ALU.bitwise_and)
                st.link(nc.vector.tensor_scalar(hi[:, :, :, :], r1[:, :, :, :], 5, None, ALU.logical_shift_right))
                for half in range(2):
                    after(v, s["list_mm"], half)
                    for e in range(HI):
                        nc.vector.tensor_scalar(hot_hi[:, :, e, :], hi[:, :, half, :], float(e), row_no[0:CP, 0:1], ALU.is_equal, ALU.mult)
                    for e in range(LO):
                        last = nc.vector.tensor_scalar(hot_lo[:, :, e, :], lo[:, :, half, :], float(e), None, ALU.is_equal)
                    last.then_inc(s["hots_ready"], 1)
                v.wait_ge(s["group_mm"], 1)
                nc.vector.tensor_scalar(grp[:, :, :].rearrange("p q h -> p (q h)"), ps[:, 6, 0:QH], float(CP), None, ALU.mult).then_inc(s["group_read"], 1)
                v.wait_ge(s["group_read"], 1)
                v.wait_ge(s["list_mm"], 2)
                for q in range(QUADS):
                    for k in range(QE):
                        r = slice(k * LO, (k + 1) * LO)
                        c0 = (q * QE + k) * HI
                        last = nc.vector.tensor_tensor(tok_no[r, q, :], ps[r, 7, c0:c0 + HI], grp[r, q, :], ALU.add)
                last.then_inc(s["list_ready"], 1)
                v.wait_ge(s["list_T"], 1)
                nc.vector.tensor_copy(tokT[:, :], ps[0:QH, 6, 0:P]).then_inc(s["tokT_ready"], 1)
                v.wait_ge(s["back_T"], 1)
                nc.vector.tensor_copy(lists_sb[:, 0:E_, :], ps[0:CP, 7, 0:E_ * CC].rearrange("p (c e) -> p e c", e=E_)).then_inc(s["lists_ready"], 1)
                v.wait_ge(s["lists_ready"], 1)
                v.wait_ge(s["spare"], 1)

                def number(e, k):
                    after(v, s["scattered"], 16 * CC * (e - RING + 1))
                    nc.vector.tensor_copy(idx[:, k, :], lists_sb[:, bass.ds(e, 1), :].rearrange("p a c -> p (a c)")).then_inc(s["idx"], 1)

                def output(e, k):
                    b2 = parts(w_e[:, k % 2, :])[3]
                    v.wait_ge(s["down"], E_ + e + 1)
                    after(v, s["scattered"], 16 * CC * (e - 1))
                    for bank, c0, m in chunk_sets:
                        last = nc.vector.tensor_tensor(y[:, k % 2, c0:c0 + m, :], ps[0:CP, bank, 0:m * D].rearrange("p (c k) -> p c k", c=m),
                                                       b2.unsqueeze(1).to_broadcast([CP, m, D]), ALU.add)
                    last.then_inc(s["y_b2"], 1)
                    v.wait_ge(s["y_b2"], e + 1)
                    v.wait_ge(s["tok_Tc"], e + 1)
                    for c in range(CC):
                        last = nc.vector.tensor_scalar(y[:, k % 2, c, :], y[:, k % 2, c, :], score[:, k % 2, c:c + 1], None, ALU.mult)
                    last.then_inc(s["y_ready"], 1)

                def routed(e, k):
                    v.wait_ge(s["tok_T"], e + 1)
                    after(v, s["y_ready"], e - 1)
                    nc.vector.tensor_copy(score[:, k % 2, :], tok[:, k % 2, :, bass.ds(D + e, 1)].rearrange("p c a -> p (c a)"))
                    nc.vector.tensor_copy(xT[:, k % 2, 0:4 * CP], ps[:, 6, 0:4 * CP])
                    nc.vector.tensor_copy(xT[:, k % 2, 4 * CP:CAP], ps[:, 7, 0:CP]).then_inc(s["tok_Tc"], 1)
                    if not isinstance(e, int) or e > 0:
                        output(e - 1, (k - 1) % RING)
                    number(e + 2, (k + 2) % RING)
                for j in range(2):
                    v.wait_ge(s[f"stored{j}"], 16 * (E_ // 2))
                number(0, 0)
                number(1, 1)
                rounds(v, routed, E_, RING)
                output(E_ - 1, (E_ - 1) % RING)


def mixture_layout(i):
    def pack(w1, b1, w2, b2):
        return np.concatenate([w1, w2.reshape(4, P, D).transpose(1, 0, 2).reshape(P, HID), b1.reshape(4, P).T,
                               np.broadcast_to(b2, (P, D))], 1)
    w = [pack(i['L0_ffn_w1'][e], i['L0_ffn_b1'][e], i['L0_ffn_w2'][e], i['L0_ffn_b2'][e]) for e in range(E_)]
    w.append(pack(i['L0_ffn_sw1'], i['L0_ffn_sb1'], i['L0_ffn_sw2'], i['L0_ffn_sb2']))
    q = np.arange(P)
    e, sg = q // SEG, q % SEG
    f = lambda a: np.ascontiguousarray(a, dtype=np.float32)
    return dict(of_expert=f(e[:, None] == e[None, :]), before=f((e[:, None] == e[None, :]) & (sg[:, None] < sg[None, :])),
                quad=f((e // QE)[:, None] == np.arange(QE)[None, :]), member=f((e % QE)[:, None] == np.arange(QE)[None, :]),
                slot=f(np.broadcast_to(np.arange(HI * LO), (P, HI * LO))), row_no=f(q[:, None]),
                first_bit=np.full((P, 1), 1 << 29, np.int32), w_ffn=np.ascontiguousarray(np.stack(w)))


TILES = N // P


def peer(nc, d, src, dst):
    H, QD, HALF, PK, K = 8, 64, 32, 64, 16
    RUNS = [(0, 1, 16), (1, 1, 8), (2, 1, 5), (3, 1, 4), (4, 1, 3), (5, 3, 2), (8, 8, 1)]
    C = sum(n * m for _, n, m in RUNS)
    CH, HC = 4, 2 * C
    LO, HI = 32, 4
    BY_ACT = (24, 32)
    X_AT = 6
    SPLIT = 2
    UPSCALE = 4096.0
    G, TG = 4, 32
    TAKEN = -3.0e38
    R = 2 * H
    with ExitStack() as ctx:
        def sb(name, shape, dt=F32):
            return ctx.enter_context(nc.sbuf_tensor("pr_" + name, shape, dt))
        wq = sb("wq", [P, H * QD]); brow = sb("brow", [1, H * QD]); brest = sb("brest", [1, H * QD])
        bias3 = sb("bias3", [65, H * QD], BF16); ones3 = sb("ones3", [65, P], BF16)
        wmean = sb("wmean", [P, H]); bmean = sb("bmean", [1, H])
        gb = sb("gb", [P, 2])
        blk = sb("blk", [P, 4])
        down = sb("down", [P, HI, P]); up = sb("up", [P, HI, P])
        kpad = sb("kpad", [PK, 4, P]); ksq = sb("ksq", [PK, 4, P]); knorm = sb("knorm", [PK, 4]); kblk = sb("kblk", [P, 4 * PK])
        ident = sb("ident", [P, P])
        x = sb("x", [P, D]); xr = sb("xr", [P, D]); stats = sb("stats", [P, 6]); mv = sb("mv", [P, 2])
        xln = sb("xln", [P, 1]); rstd = sb("rstd", [P, 1]); xn = sb("xn", [P, D]); xT = sb("xT", [P, P])
        qs = sb("qs", [P, 512]); hvar = sb("hvar", [P, H]); hln = sb("hln", [P, H]); hrstd = sb("hrstd", [P, H])
        q = sb("q", [P, 512]); qT = sb("qT", [P, 4, P]); qsT = sb("qsT", [P, 4, P])
        nsum = sb("nsum", [P, R]); nln = sb("nln", [P, R]); nrm = sb("nrm", [P, R])
        s = sb("s", [P, R, PK]); sw = sb("sw", [P, R, PK])
        sv = sb("sv", [P, R, K]); si = sb("si", [P, R, K], U32); sif = sb("sif", [P, R, K])
        cand = sb("cand", [P, H, C]); candi = sb("candi", [P, H, C]); cw = sb("cw", [P, H, C]); cw2 = sb("cw2", [P, H, C])
        cm = sb("cm", [P, H, K]); ce = sb("ce", [P, H, C]); wraw = sb("wraw", [P, H, C]); wgt = sb("wgt", [P, H, C])
        wsum = sb("wsum", [P, H])
        w2 = sb("w2", [HC, SPLIT, 512], F16)
        fi = sb("fi", [HC, 512], U16); lo = sb("lo", [HC, 512], U16); hi = sb("hi", [HC, 512], U16)
        oh_lo = sb("oh_lo", [HC, LO, 512], F16); oh_hi = sb("oh_hi", [HC, HI, 512], F16)
        apart = sb("apart", [HC, BY_ACT[1] - BY_ACT[0], 512], F16); minus = sb("minus", [HC, LO])
        w_hi = sb("w_hi", [HC, HI, SPLIT, 512], F16)
        act_in = sb("act_in", [P, HI, P]); act = sb("act", [P, HI, P]); wE = sb("wE", [P, TG, HI]); gblk = sb("gblk", [P, HI, P]); o = sb("o", [P, D])
        gates = sb("gates", [P, 2]); eps = sb("eps", [P, 1]); one = sb("one", [P, 1]); c15 = sb("c15", [P, R]); gate_q = sb("gate_q", [P, 1]); gate_a = sb("gate_a", [P, 1])
        ps = ctx.enter_context(nc.psum_tensor("pr_ps", [P, 8, 512], F32))
        ps_x, ps_o, ps_q, ps_iT = ps[:, 0, 0:P], ps[:, 7, D:2 * D], ps[:, 1, :], ps[0:HC, 1, :]
        ps_qT, ps_wT, ps_s = ps[:, 2, :], ps[0:HC, 2, :], ps[:, 3:5, :]
        ps_w, ps_in, ps_n, ps_k = ps[:, 5, 0:TG * HI * SPLIT], ps[:, 6, :], ps[:, 7, 0:R], ps[:, 7, 0:4 * PK]
        S = ctx.enter_context(semaphores(nc, "pr_", """consts_in k_step k_norm k_root k_ready k_T k_blk x_in xr_in x_var x_rough x_rstd x_norm x_T x_Tc q_mm q_sq q_rough q_rstd
             q_norm q_T q_Tc q_sqT norms sims n_max n_rough n_rstd sif_ready one_ready lo_ready apart_step hots_act act_ready s_ready ranked found candi_ready cand_ready cand_exp w_raw w_ready
             w_T fi_c w_part onehots scat inner gelu g_ready out_mm o_ready stored
             f_step t_step h_step o_step a_step0 a_step1 a_step2 p_step0 p_step1 p_step2"""))

        def skewed(eng, head, body, tail):
            head()
            body(0)
            body(1)
            with eng.Fori(2, TILES - 2) as i:
                body(i)
            body(TILES - 2)
            body(TILES - 1)
            tail()

        def has(i, ahead):
            return not isinstance(i, int) or 0 <= i + ahead < TILES

        def candidates(eng, out, v_):
            s0 = v_[:, :, :].rearrange("p (h u) k -> p h u k", u=2)
            at = 0
            for a0, na, m in RUNS:
                o_ = out[:, :, at:at + na * m]
                if m == 1:
                    i0, i1 = s0[:, :, 0, a0:a0 + na], s0[:, :, 1, 0:1].to_broadcast([P, H, na])
                elif na == 1:
                    i0, i1 = s0[:, :, 0, a0:a0 + 1].to_broadcast([P, H, m]), s0[:, :, 1, 0:m]
                else:
                    o_ = o_.rearrange("p h (a b) -> p h a b", b=m)
                    i0 = s0[:, :, 0, a0:a0 + na].unsqueeze(3).to_broadcast([P, H, na, m])
                    i1 = s0[:, :, 1, 0:m].unsqueeze(2).to_broadcast([P, H, na, m])
                last = eng.tensor_tensor(o_, i0, i1, ALU.add)
                at += na * m
            return last

        with nc.Block() as block:
            @block.sync
            def _(sp):
                for to, name in ((wq, "wq_peer"), (brow, "brow_peer"), (gb, "gb_peer"), (blk, "blk_ones"),
                                 (down, "down_cols"), (up, "up_rows"), (kpad, "keys_pad"), (ident, "ident")):
                    sp.dma_start(to[:], d[name]).then_inc(S["consts_in"], 16)

                def load(i):
                    sp.dma_start(x[:, :], src[bass.ds(i * P, P), :]).then_inc(S["x_in"], 16)

                def residual(i):
                    sp.dma_start(xr[:, :], src[bass.ds(i * P, P), :]).then_inc(S["xr_in"], 16)

                def store(i):
                    sp.wait_ge(S["o_ready"], i + 1)
                    sp.dma_start(dst[bass.ds(i * P, P), :], o[:, :]).then_inc(S["stored"], 16)

                def body(i):
                    if has(i, 3):
                        sp.wait_ge(S["x_norm"], i + 3)
                        load(i + 3)
                    if has(i, -1):
                        store(i - 1)
                        residual(i)
                load(0)
                residual(0)
                for n in range(1, 3):
                    sp.wait_ge(S["x_norm"], n)
                    load(n)
                body(0)
                with sp.Fori(1, TILES - 3) as i:
                    body(i)
                body(TILES - 3)
                body(TILES - 2)
                body(TILES - 1)
                store(TILES - 1)
                sp.wait_ge(S["stored"], 16 * TILES)

            @block.gpsimd
            def _(pool):
                def refine(i, n, rough, y, t, v, scale, add, done):
                    pool.wait_ge(rough, i + 1)
                    st = Steps(pool, S[f"p_step{n}"], 4 * i)
                    st.mark(nc.gpsimd.tensor_tensor(t, y, y, ALU.mult))
                    st.link(nc.gpsimd.tensor_scalar(v, v, -0.5 * scale, -0.5 * add, ALU.mult, ALU.add))
                    st.link(nc.gpsimd.tensor_tensor(t, t, v, ALU.mult))
                    st.link(nc.gpsimd.tensor_tensor(t, t, c15[:, 0:t.shape[1]], ALU.add))
                    nc.gpsimd.tensor_tensor(y, y, t, ALU.mult).then_inc(done, 1)

                def front_x(i):
                    refine(i, 0, S["x_rough"], rstd[:, :], xln[:, :], mv[:, 1:2], 1.0, EPS, S["x_rstd"])

                def front_a(i):
                    refine(i, 1, S["q_rough"], hrstd[:, :], hln[:, :], hvar[:, :], 1.0 / QD, EPS, S["q_rstd"])

                def front_b(i):
                    refine(i, 2, S["n_rough"], nrm[:, :], nln[:, :], nsum[:, :], 1.0, 0.0, S["n_rstd"])

                def move_gelus(i):
                    after(pool, S["g_ready"], i)
                    pool.wait_ge(S["gelu"], i + 1)
                    after(pool, S["act_ready"], i)
                    nc.gpsimd.tensor_tensor(gate_a[:, :], one[:, :], one[:, :], ALU.add)
                    nc.gpsimd.tensor_copy(act[:, :, :], act_in[:, :, :]).then_inc(S["act_ready"], 1)

                def body(i):
                    if has(i, 1):
                        front_a(i + 1)
                    if has(i, -1):
                        move_gelus(i - 1)
                    pool.wait_ge(S["found"], i + 1)
                    after(pool, S["w_T"], 2 * i - 1)
                    nc.gpsimd.tensor_tensor(gate_q[:, :], one[:, :], one[:, :], ALU.add)
                    nc.gpsimd.tensor_copy(sif[:, :, :], si[:, :, :]).then_inc(S["sif_ready"], 1)
                    pool.wait_ge(S["sif_ready"], i + 1)
                    last = candidates(nc.gpsimd, candi, sif)
                    last.then_inc(S["candi_ready"], 1)
                    if has(i, 1):
                        front_b(i + 1)
                    pool.wait_ge(S["w_raw"], i + 1)
                    nc.gpsimd.tensor_tensor(wgt[:, :, :], wraw[:, :, :], wsum[:, :].unsqueeze(2).to_broadcast([P, H, C]),
                                            ALU.mult).then_inc(S["w_ready"], 1)
                    if has(i, 2):
                        front_x(i + 2)
                nc.gpsimd.memset(c15[:, :], 1.5)
                nc.gpsimd.memset(one[:, :], 1.0).then_inc(S["one_ready"], 1)
                pool.wait_ge(S["one_ready"], 1)

                def head():
                    front_x(0); front_a(0); front_b(0); front_x(1)
                skewed(pool, head, body, lambda: move_gelus(TILES - 1))

            @block.tensor
            def _(pe):
                pe.wait_ge(S["consts_in"], 128)
                pe.wait_ge(S["k_ready"], 1)
                for j in range(4):
                    last = nc.tensor.transpose(ps_k[:, j * PK:(j + 1) * PK], kpad[:, j, :], ident[0:PK, 0:PK])
                last.then_inc(S["k_T"], 1)
                pe.wait_ge(S["k_blk"], 1)

                def turn_x(i):
                    pe.wait_ge(S["x_norm"], i + 1)
                    nc.tensor.transpose(ps_x, xn[:, :], ident[:, :]).then_inc(S["x_T"], 1)

                def queries(i):
                    pe.wait_ge(S["x_Tc"], i + 1)
                    after(pe, S["fi_c"], i - 1)
                    nc.tensor.matmul(ps_q, xT[:, :], wq[:, :], start=True, stop=False)
                    nc.tensor.matmul(ps_q, ones3[:, :], bias3[:, :], start=False, stop=True).then_inc(S["q_mm"], 1)

                def turn_q(i):
                    pe.wait_ge(S["q_norm"], i + 1)
                    for j in range(4):
                        last = nc.tensor.transpose(ps_qT[:, j * P:(j + 1) * P], q[:, j * P:(j + 1) * P], ident[:, :])
                    last.then_inc(S["q_T"], 1)

                def scores(i):
                    pe.wait_ge(S["q_Tc"], i + 1)
                    after(pe, S["s_ready"], i)
                    for j in range(4):
                        last = nc.tensor.matmul(ps_s[:, j // 2, (j % 2) * 256:(j % 2 + 1) * 256], qT[:, j, :], kblk[:, :],
                                                start=True, stop=True)
                    last.then_inc(S["sims"], 1)
                    pe.wait_ge(S["q_sqT"], i + 1)
                    after(pe, S["o_ready"], i - 2)
                    for j in range(4):
                        last = nc.tensor.matmul(ps_n[:, 4 * j:4 * j + 4], qsT[:, j, :], blk[:, :], start=True, stop=True)
                    last.then_inc(S["norms"], 1)

                def inner(i):
                    pe.wait_ge(S["x_Tc"], i + 1)
                    after(pe, S["gelu"], i)
                    for j in range(HI):
                        last = nc.tensor.matmul(ps_in[:, j * P:(j + 1) * P], down[:, j, :], xT[:, :], start=True, stop=True)
                    last.then_inc(S["inner"], 1)

                def scatter(i, g):
                    if g == 0:
                        pe.wait_ge(S["onehots"], i + 1)
                        pe.wait_ge(S["hots_act"], i + 1)
                    for u in range(TG):
                        for j in range(CH):
                            c = j * P + g * TG + u
                            last = nc.tensor.matmul(ps_w[g * 32:(g + 1) * 32, u * HI * SPLIT:(u + 1) * HI * SPLIT],
                                                    oh_lo[:, :, c], w_hi[:, :, :, c].rearrange("p a b -> p (a b)"),
                                                    start=(j == 0), stop=(j == CH - 1))
                    if g == G - 1:
                        last.then_inc(S["scat"], 1)

                def turn_w(i):
                    pe.wait_ge(S["candi_ready"], i + 1)
                    for j in range(CH):
                        last = nc.tensor.transpose(ps_iT[:, j * P:(j + 1) * P],
                                                   candi[:, 2 * j:2 * j + 2, :].rearrange("p a b -> p (a b)"), ident[:, :])
                    last.then_inc(S["w_T"], 1)
                    pe.wait_ge(S["w_ready"], i + 1)
                    for j in range(CH):
                        last = nc.tensor.transpose(ps_wT[:, j * P:(j + 1) * P],
                                                   wgt[:, 2 * j:2 * j + 2, :].rearrange("p a b -> p (a b)"), ident[:, :])
                    last.then_inc(S["w_T"], 1)

                def output(i):
                    pe.wait_ge(S["g_ready"], i + 1)
                    for j in range(HI):
                        last = nc.tensor.matmul(ps_o, gblk[:, j, :], up[:, j, :], start=(j == 0), stop=(j == HI - 1))
                    last.then_inc(S["out_mm"], 1)

                def head():
                    turn_x(0); queries(0); turn_q(0); scores(0); inner(0); turn_x(1); queries(1)

                def body(i):
                    if has(i, -1):
                        scatter(i - 1, 0)
                        scatter(i - 1, 1)
                    if has(i, 1):
                        turn_q(i + 1)
                    if has(i, -1):
                        scatter(i - 1, 2)
                    if has(i, 1):
                        scores(i + 1)
                    if has(i, -1):
                        scatter(i - 1, 3)
                    turn_w(i)
                    if has(i, -1):
                        output(i - 1)
                    if has(i, 1):
                        inner(i + 1)
                    if has(i, 2):
                        turn_x(i + 2)
                        queries(i + 2)

                def tail():
                    for g in range(G):
                        scatter(TILES - 1, g)
                    output(TILES - 1)
                skewed(pe, head, body, tail)

            @block.scalar
            def _(a):
                nc.scalar.preload_act_table_set("natural_log_exp_and_others")
                a.wait_ge(S["k_norm"], 1)
                nc.scalar.activation(knorm[:, :], knorm[:, :], ACT.Ln).then_inc(S["k_root"], 1)
                a.wait_ge(S["k_root"], 1)
                nc.scalar.activation(knorm[:, :], knorm[:, :], ACT.Exp, scale=-0.5).then_inc(S["k_root"], 1)

                def rsqrt(out, tmp, in_, which, i, bias=0.0, scale=1.0):
                    nc.scalar.activation(tmp, in_, ACT.Ln, bias=bias, scale=scale).then_inc(S[f"a_step{which}"], 1)
                    a.wait_ge(S[f"a_step{which}"], i + 1)
                    return nc.scalar.activation(out, tmp, ACT.Exp, scale=-0.5)

                def norm_x(i):
                    a.wait_ge(S["x_var"], i + 1)
                    rsqrt(rstd[:, :], xln[:, :], mv[:, 1:2], 0, i, eps[:, 0:1]).then_inc(S["x_rough"], 1)

                def front_x(i):
                    a.wait_ge(S["x_T"], i + 1)
                    after(a, S["inner"], i)
                    nc.scalar.activation(xT[:, :], ps_x, ACT.Copy).then_inc(S["x_Tc"], 1)

                def front_q(i):
                    a.wait_ge(S["q_mm"], i + 1)
                    for h in range(H):
                        last = nc.scalar.activation(qs[:, h * QD:(h + 1) * QD], ps_q[:, h * QD:(h + 1) * QD], ACT.Square,
                                                    accum_out=hvar[:, h:h + 1])
                    last.then_inc(S["q_sq"], 1)

                def front_a(i):
                    a.wait_ge(S["q_sq"], i + 1)
                    rsqrt(hrstd[:, :], hln[:, :], hvar[:, :], 1, i, eps[:, 0:1], 1.0 / QD).then_inc(S["q_rough"], 1)
                    a.wait_ge(S["q_rstd"], i + 1)
                    for h in range(H):
                        last = nc.scalar.activation(q[:, h * QD:(h + 1) * QD], ps_q[:, h * QD:(h + 1) * QD], ACT.Copy, scale=hrstd[:, h:h + 1])
                    last.then_inc(S["q_norm"], 1)

                def front_t(i):
                    a.wait_ge(S["q_T"], i + 1)
                    nc.scalar.activation(qT[:, :, :].rearrange("p a b -> p (a b)"), ps_qT, ACT.Identity,
                                         bias=gb[:, 1:2], scale=gb[:, 0:1]).then_inc(S["q_Tc"], 1)
                    a.wait_ge(S["q_Tc"], i + 1)
                    nc.scalar.activation(qsT[:, :, :], qT[:, :, :], ACT.Square).then_inc(S["q_sqT"], 1)

                def front_b(i):
                    a.wait_ge(S["n_max"], i + 1)
                    rsqrt(nrm[:, :], nln[:, :], nsum[:, :], 2, i).then_inc(S["n_rough"], 1)

                def apart_from(i):
                    e0, e1 = BY_ACT
                    a.wait_ge(S["lo_ready"], i + 1)
                    after(a, S["scat"], i)
                    for e in range(e0, e1):
                        last = nc.scalar.activation(apart[:, e - e0, :], lo[:, :], ACT.Abs, bias=minus[:, e:e + 1])
                    last.then_inc(S["apart_step"], 1)

                def one_hots(i):
                    e0, e1 = BY_ACT
                    a.wait_ge(S["apart_step"], i + 1)
                    nc.scalar.activation(oh_lo[:, e0:e1, :], apart[:, :, :], ACT.Relu, bias=1.0, scale=-1.0).then_inc(S["hots_act"], 1)
                    a.wait_ge(S["hots_act"], i + 1)

                def head():
                    norm_x(0); front_x(0); front_q(0); front_a(0); front_t(0); front_b(0); norm_x(1); front_x(1); front_q(1)

                def body(i):
                    if has(i, 1):
                        front_a(i + 1)
                    if has(i, 1):
                        front_t(i + 1)
                    a.wait_ge(S["cand_ready"], i + 1)
                    nc.scalar.activation(ce[:, :, :], cand[:, :, :], ACT.Exp).then_inc(S["cand_exp"], 1)
                    after(a, S["act_ready"], i)
                    a.wait_ge(S["inner"], i + 1)
                    nc.scalar.activation(act_in[:, :, :].rearrange("p a b -> p (a b)"), ps_in, ACT.Gelu).then_inc(S["gelu"], 1)
                    nc.scalar.preload_act_table_set("natural_log_exp_and_others")
                    if has(i, 1):
                        front_b(i + 1)
                    a.wait_ge(S["w_T"], 2 * i + 1)
                    nc.scalar.activation(fi[:, :], ps_iT, ACT.Copy).then_inc(S["fi_c"], 1)
                    a.wait_ge(S["w_T"], 2 * i + 2)
                    nc.scalar.activation(w2[:, 0, :], ps_wT, ACT.Copy, scale=UPSCALE).then_inc(S["w_part"], 1)
                    if has(i, 2):
                        norm_x(i + 2)
                    apart_from(i)
                    if has(i, 2):
                        front_x(i + 2)
                    one_hots(i)
                    if has(i, 2):
                        front_q(i + 2)
                skewed(a, head, body, lambda: None)

            @block.vector
            def _(v):
                v.wait_ge(S["consts_in"], 128)
                k = Steps(v, S["k_step"])
                k.mark(nc.vector.memset(gblk[:, :, :], 0.0))
                k.mark(nc.vector.memset(eps[:, :], EPS))
                for e in range(LO):
                    last = nc.vector.memset(minus[:, e:e + 1], -float(e))
                k.mark(last)
                for w_, m_ in ((wq, wmean), (brow, bmean)):
                    hv = w_[:, :].rearrange("p (h c) -> p h c", h=H)
                    k.link(nc.vector.tensor_reduce(m_[:, :], hv, AX.X, ALU.add))
                    k.link(nc.vector.tensor_scalar(m_[:, :], m_[:, :], 1.0 / QD, None, ALU.mult))
                    k.mark(nc.vector.tensor_tensor(hv, hv, m_[:, :].unsqueeze(2).to_broadcast([w_.shape[0], H, QD]), ALU.subtract))
                k.mark(nc.vector.memset(ones3[:, :], 1.0))
                k.link(nc.vector.memset(bias3[:, :], 0.0))
                for r in range(3):
                    k.link(nc.vector.tensor_copy(bias3[32 * r:32 * r + 1, :], brow[:, :]))
                    k.link(nc.vector.tensor_copy(brest[:, :], bias3[32 * r:32 * r + 1, :]))
                    k.link(nc.vector.tensor_tensor(brow[:, :], brow[:, :], brest[:, :], ALU.subtract))
                k.mark(nc.vector.tensor_scalar(up[:, :, :], up[:, :, :], 1.0 / UPSCALE, None, ALU.mult))
                k.link(nc.vector.tensor_tensor(ksq[:, :, :], kpad[:, :, :], kpad[:, :, :], ALU.mult))
                k.link(nc.vector.tensor_reduce(knorm[:, :], ksq[:, :, :], AX.X, ALU.add))
                nc.vector.tensor_scalar(knorm[:, :], knorm[:, :], 1e-24, None, ALU.max).then_inc(S["k_norm"], 1)
                v.wait_ge(S["k_root"], 2)
                for j in range(4):
                    last = nc.vector.tensor_scalar(kpad[:, j, :], kpad[:, j, :], knorm[:, j:j + 1], None, ALU.mult)
                last.then_inc(S["k_ready"], 1)
                v.wait_ge(S["k_T"], 1)
                nc.vector.tensor_copy(kblk[:, :], ps_k).then_inc(S["k_blk"], 1)

                PF, PT, PH = 3, 16, 2

                def norm_x(i):
                    f = Steps(v, S["f_step"], PF * i)
                    v.wait_ge(S["x_in"], 16 * i + 16)
                    f.mark(nc.vector.memset(gates[:, 0:1], 0.0))
                    f.link(nc.vector.bn_stats(stats[:, :], x[:, :]))
                    f.mark(nc.vector.memset(gates[:, 0:1], 0.0))
                    nc.vector.bn_aggr(mv[:, :], stats[:, :]).then_inc(S["x_var"], 1)

                def apply_x(i):
                    v.wait_ge(S["x_rstd"], i + 1)
                    nc.vector.tensor_scalar(xn[:, :], x[:, :], mv[:, 0:1], rstd[:, 0:1], ALU.subtract, ALU.mult).then_inc(S["x_norm"], 1)

                def norms(i):
                    v.wait_ge(S["norms"], i + 1)
                    nc.vector.tensor_scalar(nsum[:, :], ps_n, 1e-24, None, ALU.max).then_inc(S["n_max"], 1)

                def apply_s(i):
                    v.wait_ge(S["sims"], i + 1)
                    v.wait_ge(S["n_rstd"], i + 1)
                    for b in range(2):
                        last = nc.vector.tensor_tensor(s[:, 8 * b:8 * b + 8, :], ps_s[:, b, :].rearrange("p (r c) -> p r c", c=PK),
                                                       nrm[:, 8 * b:8 * b + 8].unsqueeze(2).to_broadcast([P, 8, PK]), ALU.mult)
                    last.then_inc(S["s_ready"], 1)

                def head():
                    norm_x(0); apply_x(0); norms(0); apply_s(0); norm_x(1); apply_x(1)

                def body(i):
                    t = Steps(v, S["t_step"], PT * i)
                    gate = lambda: t.mark(nc.vector.memset(gates[:, 1:2], 0.0))
                    v.wait_ge(S["s_ready"], i + 1)
                    gate()
                    for r in range(R):
                        last = nc.vector.max(sv[:, r, 0:8], s[:, r, :])
                    t.link(last)
                    gate()
                    for r in range(R):
                        nc.vector.max_index(si[:, r, 0:8], sv[:, r, 0:8], s[:, r, :])
                    for r in range(R):
                        last = nc.vector.match_replace(sw[:, r, :], sv[:, r, 0:8], s[:, r, :], TAKEN)
                    t.link(last)
                    gate()
                    for r in range(R):
                        last = nc.vector.max(sv[:, r, 8:16], sw[:, r, :])
                    t.link(last)
                    gate()
                    for r in range(R):
                        last = nc.vector.max_index(si[:, r, 8:16], sv[:, r, 8:16], sw[:, r, :])
                    last.then_inc(S["found"], 1)
                    candidates(nc.vector, cand, sv).then_inc(S["cand_ready"], 1)
                    v.wait_ge(S["cand_ready"], i + 1)
                    gate()
                    for h in range(H):
                        last = nc.vector.max(cm[:, h, 0:8], cand[:, h, :])
                    t.link(last)
                    gate()
                    for h in range(H):
                        last = nc.vector.match_replace(cw[:, h, :], cm[:, h, 0:8], cand[:, h, :], TAKEN)
                    t.link(last)
                    gate()
                    for h in range(H):
                        last = nc.vector.max(cm[:, h, 8:16], cw[:, h, :])
                    t.link(last)
                    gate()
                    for h in range(H):
                        last = nc.vector.match_replace(cw2[:, h, :], cm[:, h, 8:16], cw[:, h, :], TAKEN)
                    last.then_inc(S["ranked"], 1)
                    if has(i, 1):
                        norms(i + 1)
                    v.wait_ge(S["ranked"], i + 1)
                    v.wait_ge(S["cand_exp"], i + 1)
                    after(v, S["w_ready"], i)
                    st = nc.vector.scalar_tensor_tensor(wraw[:, :, :], cw2[:, :, :], TAKEN, ce[:, :, :], ALU.is_equal, ALU.mult)
                    t.link(st)
                    t.link(nc.vector.tensor_reduce(wsum[:, :], wraw[:, :, :], AX.X, ALU.add))
                    nc.vector.reciprocal(wsum[:, :], wsum[:, :]).then_inc(S["w_raw"], 1)
                    assert t.n == PT, t.n

                def h_stage(i):
                    h = Steps(v, S["h_step"], PH * i)
                    v.wait_ge(S["fi_c"], i + 1)
                    after(v, S["hots_act"], i)
                    nc.vector.tensor_scalar(lo[:, :], fi[:, :], LO - 1, None, ALU.bitwise_and).then_inc(S["lo_ready"], 1)
                    h.link(nc.vector.tensor_scalar(hi[:, :], fi[:, :], 5, None, ALU.logical_shift_right))
                    for e in range(HI):
                        nc.vector.tensor_scalar(oh_hi[:, e, :], hi[:, :], float(e), None, ALU.is_equal)
                    for e in range(BY_ACT[0]):
                        if e == X_AT and has(i, 2):
                            apply_x(i + 2)
                        last = nc.vector.tensor_scalar(oh_lo[:, e, :], lo[:, :], float(e), None, ALU.is_equal)
                    v.wait_ge(S["w_part"], i + 1)
                    h.link(nc.vector.scalar_tensor_tensor(w2[:, 1, :], ps_wT, UPSCALE, w2[:, 0, :], ALU.mult, ALU.subtract))
                    for e in range(HI):
                        last = nc.vector.tensor_tensor(w_hi[:, e, :, :], w2[:, :, :],
                                                       oh_hi[:, e:e + 1, :].to_broadcast([HC, SPLIT, 512]), ALU.mult)
                    last.then_inc(S["onehots"], 1)

                def o_first(i):
                    v.wait_ge(S["scat"], i + 1)
                    st = nc.vector.tensor_reduce(wE[:, :, :], ps_w.rearrange("p (t a b) -> p t a b", a=HI, b=SPLIT), AX.X, ALU.add)
                    st.then_inc(S["o_step"], 1)
                    v.wait_ge(S["o_step"], i + 1)
                    v.wait_ge(S["act_ready"], i + 1)
                    for g in range(G):
                        r = slice(g * 32, (g + 1) * 32)
                        last = nc.vector.tensor_tensor(gblk[r, :, g * TG:(g + 1) * TG], act[r, :, g * TG:(g + 1) * TG],
                                                       wE[r, :, :].rearrange("p t a -> p a t"), ALU.mult)
                    last.then_inc(S["g_ready"], 1)

                def o_last(i):
                    v.wait_ge(S["out_mm"], i + 1)
                    v.wait_ge(S["xr_in"], 16 * i + 16)
                    after(v, S["stored"], 16 * i)
                    nc.vector.tensor_tensor(o[:, :], ps_o, xr[:, :], ALU.add).then_inc(S["o_ready"], 1)

                def whole(i):
                    body(i)
                    if has(i, 2):
                        norm_x(i + 2)
                    if has(i, 1):
                        apply_s(i + 1)
                    if has(i, -1):
                        o_first(i - 1)
                    h_stage(i)
                    if has(i, -1):
                        o_last(i - 1)

                def tail():
                    o_first(TILES - 1)
                    o_last(TILES - 1)
                skewed(v, head, whole, tail)


def peer_layout(i):
    c_ = np.ascontiguousarray
    kp = np.zeros((64, 4, 128), np.float32)
    for j in range(4):
        kp[:, j, 32 * j:32 * j + 32] = i['L1_ffn_keys1' if j % 2 else 'L1_ffn_keys0']
    dn = i['L1_ffn_expert_down'][:128].reshape(4, 1, 32, 128)
    dn = np.broadcast_to(dn, (4, 4, 32, 128)).transpose(3, 0, 1, 2).reshape(128, 4, 128)
    u = i['L1_ffn_expert_up'][:128].reshape(1, 4, 32, 128)
    u = np.broadcast_to(u, (4, 4, 32, 128)).transpose(0, 2, 1, 3).reshape(128, 4, 128)
    gb = np.tile(np.stack([i['L1_ffn_ln_g'], i['L1_ffn_ln_b']], 1), (2, 1))
    return dict(wq_peer=c_(i['L1_ffn_Wq'].T), brow_peer=c_(i['L1_ffn_bq'][None, :]), gb_peer=c_(gb),
                blk_ones=np.kron(np.eye(4), np.ones((32, 1))).astype(np.float32),
                down_cols=c_(dn), up_rows=c_(u), keys_pad=kp, ident=np.eye(128, dtype=np.float32))


def build(nc, d, out):
    scratch = lambda name, shape, dt=F32: nc.dram_tensor(name, shape, dt, kind="Internal").ap()
    h0, h1, h2, h3 = (scratch(f"h{n}", [N, D]) for n in range(4))
    table, probs, xfT = scratch("table", [N, D + E_]), scratch("probs", [N, E_]), scratch("xfT", [D, N])
    places = scratch("places", [E_, HI * LO])
    embed(nc, d, h0)
    attend0(nc, d, h0, h1, table, probs, xfT)
    mixture(nc, d, h1, table, probs, xfT, places, h2)
    attend1(nc, d, h2, h3)
    peer(nc, d, h3, out)


def kernel(**inputs):
    import concourse.bacc as bacc
    from concourse.bass_utils import run_bass_kernel_spmd

    i = {k: np.asarray(v) for k, v in inputs.items()}
    arrays = {**attention_layout(i), **mixture_layout(i), **peer_layout(i)}
    nc = bacc.Bacc("TRN2", target_bir_lowering=False, num_devices=1)
    d = {k: nc.dram_tensor("in_" + k, a.shape, mybir.dt.from_np(a.dtype), kind="ExternalInput").ap() for k, a in arrays.items()}
    out = nc.dram_tensor("out", (N, D), F32, kind="ExternalOutput").ap()
    build(nc, d, out)
    r = run_bass_kernel_spmd(nc, [{"in_" + k: a for k, a in arrays.items()}], core_ids=[0])
    return r.results[0]["out"].reshape(B, T, D)
```
